# Optimizing a Trainium2 kernel written in Bass

```python
import numpy as np
import jax
import jax.numpy as jnp

def _softmax(x, axis=-1):
    return jax.nn.softmax(x, axis=axis)

def _gelu(x):
    return jax.nn.gelu(x, approximate=True)

def _silu(x):
    return jax.nn.silu(x)

def _sigmoid(x):
    return jax.nn.sigmoid(x)

def _layernorm(x, axis=-1, eps=1e-05):
    m = jnp.mean(x, axis=axis, keepdims=True)
    v = jnp.var(x, axis=axis, keepdims=True)
    return (x - m) / jnp.sqrt(v + eps)

def _scatter_add(tgt, idx, src, axis=0):
    return tgt.at[idx].add(src)

def _segment_sum(src, seg, n):
    return jax.ops.segment_sum(src, seg, n)
kernel_name = 'mk_perceiver_d1_seqx_r2_f00846'

def setup_inputs(seed: int=0):
    np.random.seed(seed)
    _w = jnp.asarray

    def _rec_inputs():
        import jax
        import jax.numpy as jnp
        _rk = jax.random.key(seed)
        x = -0.0003929 + 0.9999 * jax.random.normal(jax.random.fold_in(_rk, 1), (2, 512, 512), jnp.float32)
        _lenS = 512 - jax.random.randint(jax.random.fold_in(_rk, 7), (2,), 0, max(1, 512 // 4) + 1, jnp.int32)
        _lenS2 = 8192 - jax.random.randint(jax.random.fold_in(_rk, 8), (2,), 0, max(1, 8192 // 4) + 1, jnp.int32)
        _ctx_1024P = jax.random.normal(jax.random.fold_in(_rk, 11), (2, 16, 512), jnp.float32)
        _ctx_1024c = jax.random.dirichlet(jax.random.fold_in(_rk, 511), 0.3 * jnp.ones((16,), jnp.float32), (2, 8192))
        _ctx_1024t = jnp.einsum('bsk,bkd->bsd', _ctx_1024c, _ctx_1024P)
        _ctx_1024t = _ctx_1024t * jax.lax.rsqrt(jnp.mean(jnp.square(_ctx_1024t)) + 1e-12) * 0.953939
        ctx_1024 = 2.81802e-05 + 1.00001 * (_ctx_1024t + 0.3 * jax.random.normal(jax.random.fold_in(_rk, 611), (2, 8192, 512), jnp.float32))
        _validS = jnp.arange(512)[None, :] < _lenS[:, None]
        _validS2 = jnp.arange(8192)[None, :] < _lenS2[:, None]
        _causal = jnp.tril(jnp.ones((512, 512), dtype=bool))
        mask_SxS2_bk0 = jnp.logical_not(jnp.broadcast_to(_validS2[0:1, :], (512, 8192)))
        return (x, ctx_1024, mask_SxS2_bk0)
    x, ctx_1024, mask_SxS2_bk0 = _rec_inputs()

    def _L0_xattn_setup():
        import jax, jax.numpy as jnp
        import numpy as np
        B, S, D = (8, 1024, 512)
        key = jax.random.key(seed)
        ks = jax.random.split(key, 9)
        scale = 1.0 / np.sqrt(D)
        inp = {'query': jax.random.normal(ks[0], (B, S, D), dtype=jnp.float32), 'key': jax.random.normal(ks[1], (B, S, D), dtype=jnp.float32), 'value': jax.random.normal(ks[2], (B, S, D), dtype=jnp.float32), 'mask': jnp.tril(jnp.ones((S, S), dtype=bool)), 'Wq': jax.random.normal(ks[3], (D, D), dtype=jnp.float32) * scale, 'bq': jax.random.normal(ks[4], (D,), dtype=jnp.float32) * 0.02, 'Wk': jax.random.normal(ks[5], (D, D), dtype=jnp.float32) * scale, 'bk': jax.random.normal(ks[6], (D,), dtype=jnp.float32) * 0.02, 'Wv': jax.random.normal(ks[7], (D, D), dtype=jnp.float32) * scale, 'bv': jax.random.normal(ks[8], (D,), dtype=jnp.float32) * 0.02}
        return inp
    _L0_xattn_all = _L0_xattn_setup()
    _L0_xattn_in = {k: v for k, v in _L0_xattn_all.items() if k in ('Wq', 'bq', 'Wk', 'bk', 'Wv', 'bv')}
    del _L0_xattn_all

    def _L0_attn_setup():
        import math
        import jax, jax.numpy as jnp
        import numpy as np
        D_MODEL = 512
        N_HEADS = 16
        D_K = D_MODEL // N_HEADS
        D_C = 128
        B, S = (2, 1024)
        key = jax.random.key(seed)
        ks = jax.random.split(key, 7)
        sd = lambda fan_in: 1.0 / math.sqrt(fan_in)
        return {'x': jax.random.normal(ks[0], (B, S, D_MODEL), dtype=jnp.float32), 'W_dq': jax.random.uniform(ks[1], (D_MODEL, D_C), minval=-sd(D_MODEL), maxval=sd(D_MODEL), dtype=jnp.float32), 'W_uq': jax.random.uniform(ks[2], (D_C, N_HEADS * D_K), minval=-sd(D_C), maxval=sd(D_C), dtype=jnp.float32), 'W_dkv': jax.random.uniform(ks[3], (D_MODEL, D_C), minval=-sd(D_MODEL), maxval=sd(D_MODEL), dtype=jnp.float32), 'W_uk': jax.random.uniform(ks[4], (D_C, N_HEADS * D_K), minval=-sd(D_C), maxval=sd(D_C), dtype=jnp.float32), 'W_uv': jax.random.uniform(ks[5], (D_C, N_HEADS * D_K), minval=-sd(D_C), maxval=sd(D_C), dtype=jnp.float32), 'W_o': jax.random.uniform(ks[6], (N_HEADS * D_K, D_MODEL), minval=-sd(N_HEADS * D_K), maxval=sd(N_HEADS * D_K), dtype=jnp.float32)}
    _L0_attn_all = _L0_attn_setup()
    _L0_attn_in = {k: v for k, v in _L0_attn_all.items() if k in ('W_dq', 'W_uq', 'W_dkv', 'W_uk', 'W_uv', 'W_o')}
    del _L0_attn_all

    def _L0_ffn_setup():
        import jax, jax.numpy as jnp
        import numpy as np
        B, T, C, H, E, MIN_E = (4, 1024, 512, 128, 16, 2)
        IS_CAUSAL = False

        def _forward(hidden_states, sim_matrix, gates, q_proj, k_proj, v_proj, o_proj):
            b, t, c = hidden_states.shape
            n = b * t
            x = hidden_states.reshape(n, c)
            xn = x / jnp.maximum(jnp.linalg.norm(x, axis=-1, keepdims=True), 1e-12)
            sn = sim_matrix / jnp.maximum(jnp.linalg.norm(sim_matrix, axis=0, keepdims=True), 1e-12)
            logits = xn @ sn - jax.nn.sigmoid(gates)
            gated = jax.nn.relu(logits)
            hard = (gated > 0).astype(gated.dtype)
            mask = gated + jax.lax.stop_gradient(hard - gated)
            inactive = jnp.sum(hard, axis=1) == 0
            _, fb_idx = jax.lax.top_k(logits, MIN_E)
            fb = jnp.zeros((n, logits.shape[1]), gated.dtype).at[jnp.arange(n)[:, None], fb_idx].set(1.0)
            put = jax.lax.stop_gradient(inactive[:, None].astype(gated.dtype) * fb)
            mask = mask * (1.0 - put) + put
            masked = jnp.where(mask > 0, gated, -jnp.inf)
            w = jax.nn.softmax(masked, axis=-1)

            def moe_proj(p):
                y = jnp.einsum('nc,ech->neh', x, p)
                return jnp.einsum('ne,neh->nh', w, y)
            q = moe_proj(q_proj).reshape(b, t, -1)
            k = moe_proj(k_proj).reshape(b, t, -1)
            v = moe_proj(v_proj).reshape(b, t, -1)
            h = q.shape[-1]
            scores = jnp.einsum('bth,bsh->bts', q, k) / jnp.sqrt(jnp.asarray(h, q.dtype))
            if IS_CAUSAL and t > 1:
                causal = jnp.tril(jnp.ones((t, t), bool))
                scores = jnp.where(causal[None], scores, -jnp.inf)
            attn = jax.nn.softmax(scores, axis=-1)
            o = jnp.einsum('bts,bsh->bth', attn, v).reshape(n, h)
            z = jnp.einsum('ne,nh->enh', w, o)
            out = jnp.einsum('enh,ehc->nc', z, o_proj)
            return out.reshape(b, t, c)
        key = jax.random.key(seed)
        ks = jax.random.split(key, 6)
        lim_qkv = float(np.sqrt(6.0 / (C + H)))
        inp = {'hidden_states': jax.random.normal(ks[0], (B, T, C), jnp.float32), 'sim_matrix': jax.random.normal(ks[1], (C, E), jnp.float32), 'gates': jnp.zeros((E,), jnp.float32), 'q_proj': jax.random.uniform(ks[2], (E, C, H), jnp.float32, -lim_qkv, lim_qkv), 'k_proj': jax.random.uniform(ks[3], (E, C, H), jnp.float32, -lim_qkv, lim_qkv), 'v_proj': jax.random.uniform(ks[4], (E, C, H), jnp.float32, -lim_qkv, lim_qkv), 'o_proj': jax.random.uniform(ks[5], (E, H, C), jnp.float32, -lim_qkv, lim_qkv)}
        return inp
    _L0_ffn_all = _L0_ffn_setup()
    _L0_ffn_in = {k: v for k, v in _L0_ffn_all.items() if k in ('sim_matrix', 'gates', 'q_proj', 'k_proj', 'v_proj', 'o_proj')}
    del _L0_ffn_all
    return {'x': x, 'ctx_1024': ctx_1024, 'mask_SxS2_bk0': mask_SxS2_bk0, 'L0_xattn_Wq': _L0_xattn_in['Wq'], 'L0_xattn_bq': _L0_xattn_in['bq'], 'L0_xattn_Wk': _L0_xattn_in['Wk'], 'L0_xattn_bk': _L0_xattn_in['bk'], 'L0_xattn_Wv': _L0_xattn_in['Wv'], 'L0_xattn_bv': _L0_xattn_in['bv'], 'L0_attn_W_dq': _L0_attn_in['W_dq'], 'L0_attn_W_uq': _L0_attn_in['W_uq'], 'L0_attn_W_dkv': _L0_attn_in['W_dkv'], 'L0_attn_W_uk': _L0_attn_in['W_uk'], 'L0_attn_W_uv': _L0_attn_in['W_uv'], 'L0_attn_W_o': _L0_attn_in['W_o'], 'L0_ffn_sim_matrix': _L0_ffn_in['sim_matrix'], 'L0_ffn_gates': _L0_ffn_in['gates'], 'L0_ffn_q_proj': _L0_ffn_in['q_proj'], 'L0_ffn_k_proj': _L0_ffn_in['k_proj'], 'L0_ffn_v_proj': _L0_ffn_in['v_proj'], 'L0_ffn_o_proj': _L0_ffn_in['o_proj']}

def reference(x, ctx_1024, mask_SxS2_bk0, L0_xattn_Wq, L0_xattn_bq, L0_xattn_Wk, L0_xattn_bk, L0_xattn_Wv, L0_xattn_bv, L0_attn_W_dq, L0_attn_W_uq, L0_attn_W_dkv, L0_attn_W_uk, L0_attn_W_uv, L0_attn_W_o, L0_ffn_sim_matrix, L0_ffn_gates, L0_ffn_q_proj, L0_ffn_k_proj, L0_ffn_v_proj, L0_ffn_o_proj):
    import jax
    import jax.numpy as jnp

    def _L0_xattn_ref(query, key, value, mask, Wq, bq, Wk, bk, Wv, bv):
        import jax, jax.numpy as jnp
        import numpy as np
        B, S, D = (8, 1024, 512)
        dk = Wq.shape[1]
        q = jnp.einsum('bsd,de->bse', query, Wq) + bq
        k = jnp.einsum('bsd,de->bse', key, Wk) + bk
        v = jnp.einsum('bsd,de->bse', value, Wv) + bv
        scores = jnp.einsum('bqd,bkd->bqk', q, k) / jnp.sqrt(jnp.asarray(dk, q.dtype))
        scores = jnp.where(mask, scores, jnp.asarray(-jnp.inf, scores.dtype))
        attn = jax.nn.softmax(scores, axis=-1)
        return jnp.einsum('bqk,bkd->bqd', attn, v)

    def _L0_attn_ref(x, W_dq, W_uq, W_dkv, W_uk, W_uv, W_o):
        import math
        import jax, jax.numpy as jnp
        import numpy as np
        D_MODEL = 512
        N_HEADS = 16
        D_K = D_MODEL // N_HEADS
        D_C = 128
        B, S = (2, 1024)
        Bx, Sx, _ = x.shape
        c_q = x @ W_dq
        Q = (c_q @ W_uq).reshape(Bx, Sx, N_HEADS, D_K)
        c_kv = x @ W_dkv
        K = (c_kv @ W_uk).reshape(Bx, Sx, N_HEADS, D_K)
        V = (c_kv @ W_uv).reshape(Bx, Sx, N_HEADS, D_K)
        scores = jnp.einsum('bqhd,bkhd->bhqk', Q, K) / math.sqrt(D_K)
        causal = jnp.tril(jnp.ones((Sx, Sx), dtype=bool))
        scores = jnp.where(causal, scores, -jnp.inf)
        attn = jax.nn.softmax(scores, axis=-1)
        out = jnp.einsum('bhqk,bkhd->bqhd', attn, V).reshape(Bx, Sx, N_HEADS * D_K)
        return out @ W_o

    def _L0_ffn_ref(hidden_states, sim_matrix, gates, q_proj, k_proj, v_proj, o_proj):
        import jax, jax.numpy as jnp
        import numpy as np
        B, T, C, H, E, MIN_E = (4, 1024, 512, 128, 16, 2)
        IS_CAUSAL = False

        def _forward(hidden_states, sim_matrix, gates, q_proj, k_proj, v_proj, o_proj):
            b, t, c = hidden_states.shape
            n = b * t
            x = hidden_states.reshape(n, c)
            xn = x / jnp.maximum(jnp.linalg.norm(x, axis=-1, keepdims=True), 1e-12)
            sn = sim_matrix / jnp.maximum(jnp.linalg.norm(sim_matrix, axis=0, keepdims=True), 1e-12)
            logits = xn @ sn - jax.nn.sigmoid(gates)
            gated = jax.nn.relu(logits)
            hard = (gated > 0).astype(gated.dtype)
            mask = gated + jax.lax.stop_gradient(hard - gated)
            inactive = jnp.sum(hard, axis=1) == 0
            _, fb_idx = jax.lax.top_k(logits, MIN_E)
            fb = jnp.zeros((n, logits.shape[1]), gated.dtype).at[jnp.arange(n)[:, None], fb_idx].set(1.0)
            put = jax.lax.stop_gradient(inactive[:, None].astype(gated.dtype) * fb)
            mask = mask * (1.0 - put) + put
            masked = jnp.where(mask > 0, gated, -jnp.inf)
            w = jax.nn.softmax(masked, axis=-1)

            def moe_proj(p):
                y = jnp.einsum('nc,ech->neh', x, p)
                return jnp.einsum('ne,neh->nh', w, y)
            q = moe_proj(q_proj).reshape(b, t, -1)
            k = moe_proj(k_proj).reshape(b, t, -1)
            v = moe_proj(v_proj).reshape(b, t, -1)
            h = q.shape[-1]
            scores = jnp.einsum('bth,bsh->bts', q, k) / jnp.sqrt(jnp.asarray(h, q.dtype))
            if IS_CAUSAL and t > 1:
                causal = jnp.tril(jnp.ones((t, t), bool))
                scores = jnp.where(causal[None], scores, -jnp.inf)
            attn = jax.nn.softmax(scores, axis=-1)
            o = jnp.einsum('bts,bsh->bth', attn, v).reshape(n, h)
            z = jnp.einsum('ne,nh->enh', w, o)
            out = jnp.einsum('enh,ehc->nc', z, o_proj)
            return out.reshape(b, t, c)
        return _forward(hidden_states, sim_matrix, gates, q_proj, k_proj, v_proj, o_proj)
    x = x + _L0_xattn_ref(_layernorm(x, axis=-1), ctx_1024, ctx_1024, mask_SxS2_bk0, L0_xattn_Wq, L0_xattn_bq, L0_xattn_Wk, L0_xattn_bk, L0_xattn_Wv, L0_xattn_bv)
    x = x + _L0_attn_ref(_layernorm(x, axis=-1), L0_attn_W_dq, L0_attn_W_uq, L0_attn_W_dkv, L0_attn_W_uk, L0_attn_W_uv, L0_attn_W_o)
    x = x + _L0_ffn_ref(_layernorm(x, axis=-1), L0_ffn_sim_matrix, L0_ffn_gates, L0_ffn_q_proj, L0_ffn_k_proj, L0_ffn_v_proj, L0_ffn_o_proj)
    return x

_drawn_inputs = setup_inputs


def setup_inputs(seed=0):
    import zlib

    import numpy as np

    out = dict(_drawn_inputs(seed))
    spreads = {'L0_ffn_gates': (0.0, 0.1)}
    factors = {'L0_xattn_bq': 8.0,
     'L0_xattn_bk': 8.0,
     'L0_attn_W_dq': 8.0,
     'L0_attn_W_uq': 8.0,
     'L0_attn_W_uk': 8.0,
     'L0_ffn_q_proj': 2.802,
     'L0_ffn_k_proj': 2.762}
    for name, (base, spread) in spreads.items():
        noise = np.random.default_rng([zlib.crc32(name.encode()), seed]).standard_normal(out[name].shape)
        drawn = base * np.exp(spread * noise) if base else spread * noise
        out[name] = jnp.asarray(drawn.astype(out[name].dtype))
    for name, factor in factors.items():
        out[name] = (out[name] * factor).astype(out[name].dtype)
    return out
```

```python
from contextlib import ExitStack

import concourse.bass as bass
from concourse import mybir

F32 = mybir.dt.float32
F32R = mybir.dt.float32r
I32 = mybir.dt.int32
U8 = mybir.dt.uint8
ALU = mybir.AluOpType
ACT = mybir.ActivationFunctionType
AX = mybir.AxisListType

P = 128
B, S, D = 2, 512, 512
KEYS = 8192
NT = B * S // P
QT = S // P
DC = D // P
KB = 512
NB = KEYS // KB
KC = KB // P
NH, DK = 16, 32
DCQ = 128
E, H = 16, 128
EPS = 1e-5
BIG = 1e30
LOWEST = -3e38
XSCALE = float(D) ** -0.5


class Mem:

    def __init__(self, nc, ctx):
        self.nc, self.ctx = nc, ctx

    def sb(self, name, shape, dt=F32):
        return self.ctx.enter_context(self.nc.sbuf_tensor(name, shape, dt))

    def sem(self, name):
        return self.ctx.enter_context(self.nc.semaphore(name))


def chained(eng, sem):
    count = [0]

    def link(ins):
        count[0] += 1
        ins.then_inc(sem, 1)
        eng.wait_ge(sem, count[0])

    return link


def apart(eng, waited):
    eng.sem_inc(waited, 1)


def layernorm_stats(dve, link, x, stats, mv, varp, rows_ready=None):
    for t in range(NT):
        if rows_ready is not None:
            rows_ready(t)
        link(dve.bn_stats(stats[:, t, :], x[:, t, :]))
    for t in range(NT):
        ins = dve.bn_aggr(mv[:, t, :], stats[:, t, :])
    link(ins)
    return dve.tensor_scalar(varp[:], mv[:, :, 1], EPS, None, ALU.add)


def queries(nc, T, io):
    with ExitStack() as ctx:
        m = Mem(nc, ctx)
        ps, x, ident = T["ps"], T["x"], T["ident"]
        mask = m.sb("mask_all", [P, QT, KEYS], U8)
        wraw = m.sb("wraw", [P, 2, DC, D])
        wT = m.sb("wT", [P, 2, DC, D])
        M = m.sb("M", [P, DC, D])
        xn = m.sb("xn", [P, NT, D])
        xnT = m.sb("xnT", [P, DC, B * S])
        gf = m.sb("gf", [P, 2, 512])
        bqk = m.sb("bqk", [P, 2, DC])
        brow = m.sb("brow", [2 * DC, P])
        prod = m.sb("prod", [P, DC])
        cols = m.sb("cols", [P, 9])
        stats = m.sb("stats", [P, NT, 6])
        mv = m.sb("mv", [P, NT, 2])
        varp = m.sb("varp", [P, NT])
        std = m.sb("std", [P, NT])
        rstd = m.sb("rstd", [P, NT])
        red = m.sb("red", [P, QT, NB])
        act_f = m.sb("act_f", [P, NB])
        before = m.sb("before", [P, NB, NB])
        lower = m.sb("lower", [P, NB, NB])
        rank_f = m.sb("rank_f", [P, NB])

        x_in, w_in, b_in, mask_in = m.sem("x_in"), m.sem("w_in"), m.sem("b_in"), m.sem("mask_in")
        ones_set, ident_set = m.sem("ones_set"), m.sem("ident_set")
        pool_step, dve_step = m.sem("a_pool_step"), m.sem("a_dve_step")
        var_ready, std_ready, xn_ready = m.sem("var_ready"), m.sem("std_ready"), m.sem("xn_ready")
        w_turned, w_copied = m.sem("w_turned"), m.sem("w_copied")
        x_turned, x_copied = m.sem("x_turned"), m.sem("x_copied")
        b_turned, b_copied = m.sem("b_turned"), m.sem("b_copied")
        prod_ready, cols_ready, cols_copied = m.sem("prod_ready"), m.sem("cols_ready"), m.sem("cols_copied")
        g_ready, gf_ready, ghi_ready, glo_ready = m.sem("g_ready"), m.sem("gf_ready"), m.sem("ghi_ready"), m.sem("glo_ready")
        c_ready, red_ready, any_ready = m.sem("c_ready"), m.sem("red_ready"), m.sem("any_ready")

        with nc.Block() as block:

            @block.sync
            def _(sp):
                sp.dma_start(wraw[:, 0], io["Wq"].rearrange("(c p) e -> p c e", p=P)).then_inc(w_in, 16)
                sp.dma_start(wraw[:, 1], io["Wk"].rearrange("(c p) e -> p c e", p=P)).then_inc(w_in, 16)
                sp.dma_start(x[:], io["x"].rearrange("b (t p) d -> p (b t) d", p=P)).then_inc(x_in, 16)
                sp.dma_start(brow[0:DC], io["bq"].rearrange("(c p) -> c p", p=P)).then_inc(b_in, 16)
                sp.dma_start(brow[DC:2 * DC], io["bk"].rearrange("(c p) -> c p", p=P)).then_inc(b_in, 16)
                sp.dma_start(T["Wv"][:], io["Wv"].rearrange("(c p) e -> p c e", p=P)).then_inc(T["weights_in"], 16)
                for i, n in enumerate(("dq", "dkv")):
                    sp.dma_start(T["dqkv"][:, i], io[n].rearrange("(c p) e -> p c e", p=P)).then_inc(T["weights_in"], 16)
                for n in ("uq", "uk", "uv"):
                    sp.dma_start(T[n][:], io[n]).then_inc(T["weights_in"], 16)
                sp.dma_start(T["Wo"][:], io["Wo"].rearrange("(c p) e -> p c e", p=P)).then_inc(T["weights_in"], 16)
                for t in range(QT):
                    sp.dma_start(mask[:, t], io["mask"].rearrange("(t p) k -> t p k", p=P)[t]).then_inc(mask_in, 16)

            @block.gpsimd
            def _(pool):
                link = chained(pool, pool_step)
                link(pool.memset(ident[:], 0.0))
                pool.affine_select(out=ident[:], in_=ident[:], compare_op=ALU.not_equal, fill=1.0, base=0,
                                   pattern=[[-1, P]], channel_multiplier=1).then_inc(ident_set, 1)
                link(pool.memset(lower[:], 0.0))
                link(pool.affine_select(out=lower[:], in_=lower[:], compare_op=ALU.is_ge, fill=1.0, base=0,
                                        pattern=[[-1, NB], [1, NB]], channel_multiplier=0))
                pool.memset(T["m_run"][:], -BIG)
                pool.memset(T["l_run"][:], 0.0)
                pool.memset(T["acc"][:], 0.0).then_inc(ones_set, 1)
                for i in range(2 * DC):
                    half, j = divmod(i, DC)
                    pool.wait_ge(ghi_ready, i + 1)
                    pool.tensor_tensor(T["glo"][:, j, half * 512:half * 512 + 512], gf[:, i % 2],
                                       T["ghi"][:, j, half * 512:half * 512 + 512].bitcast(F32),
                                       ALU.subtract).then_inc(glo_ready, 1)

            @block.scalar
            def _(act):
                act.wait_ge(var_ready, 1)
                act.activation(std[:], varp[:], ACT.Sqrt).then_inc(std_ready, 1)
                for i in range(2 * DC):
                    act.wait_ge(w_turned, i + 1)
                    act.copy(wT[:, i // DC, i % DC], ps[:, i % 2]).then_inc(w_copied, 1)
                for i in range(DC):
                    act.wait_ge(w_turned, 2 * DC + i + 1)
                    act.copy(M[:, i], ps[:, i % 2]).then_inc(w_copied, 1)
                for i in range(2 * DC):
                    half, j = divmod(i, DC)
                    act.wait_ge(gf_ready, i + 1)
                    act.copy(T["ghi"][:, j, half * 512:half * 512 + 512], gf[:, i % 2]).then_inc(ghi_ready, 1)

            @block.vector
            def _(dve):
                link = chained(dve, dve_step)
                link(dve.memset(T["ones"][:], 1.0))
                dve.wait_ge(x_in, 16)
                layernorm_stats(dve, link, x, stats, mv, varp).then_inc(var_ready, 1)
                dve.wait_ge(b_turned, 1)
                dve.tensor_copy(bqk[:].rearrange("p a c -> p (a c)"), ps[:, 4, 32:32 + 2 * DC]).then_inc(b_copied, 1)
                dve.wait_ge(b_copied, 1)
                dve.tensor_tensor(prod[:], bqk[:, 0], bqk[:, 1], ALU.mult).then_inc(prod_ready, 1)
                dve.wait_ge(std_ready, 1)
                link(dve.reciprocal(rstd[:], std[:]))
                for t in range(NT):
                    dve.tensor_scalar(xn[:, t], x[:, t], mv[:, t, 0:1], rstd[:, t:t + 1], ALU.subtract,
                                      ALU.mult).then_inc(xn_ready, 1)
                for t in range(NT):
                    dve.wait_ge(x_turned, t + 1)
                    dve.tensor_copy(xnT[:, :, t * P:(t + 1) * P],
                                    ps[:, 2 + t % 2].rearrange("p (c r) -> p c r", c=DC)).then_inc(x_copied, 1)
                dve.wait_ge(cols_ready, 1)
                dve.tensor_copy(cols[:], ps[:, 4, 0:9]).then_inc(cols_copied, 1)
                dve.wait_ge(cols_copied, 1)
                for i in range(2 * DC):
                    dve.wait_ge(g_ready, i + 1)
                    if i >= 2:
                        dve.wait_ge(glo_ready, i - 1)
                    dve.tensor_scalar(gf[:, i % 2], ps[:, 5 + i % 2], cols[:, i % DC:i % DC + 1], XSCALE, ALU.add,
                                      ALU.mult).then_inc(gf_ready, 1)
                dve.wait_ge(c_ready, 1)
                dve.tensor_scalar(T["c"][:], ps[:, 4, 16:16 + NT], cols[:, 8:9], XSCALE, ALU.add,
                                  ALU.mult).then_inc(dve_step, 1)
                dve.wait_ge(mask_in, 16 * QT)
                for t in range(QT):
                    words = mask[:, t].bitcast(I32).rearrange("p (b w) -> p b w", b=NB)
                    ins = dve.tensor_reduce(red[:, t], words, AX.X, ALU.max)
                ins.then_inc(red_ready, 1)
                dve.wait_ge(any_ready, 1)
                dve.tensor_scalar(act_f[:], ps[:, 7, 0:NB], 0.0, None, ALU.is_gt).then_inc(red_ready, 1)
                dve.wait_ge(red_ready, 2)
                dve.wait_ge(ones_set, 1)
                dve.tensor_copy(T["live"][:, 0], act_f[:]).then_inc(red_ready, 1)
                dve.tensor_tensor(before[:], lower[:], act_f[:].unsqueeze(1).to_broadcast([P, NB, NB]),
                                  ALU.mult).then_inc(red_ready, 1)
                dve.wait_ge(red_ready, 4)
                dve.tensor_reduce(rank_f[:], before[:], AX.X, ALU.add).then_inc(red_ready, 1)
                dve.wait_ge(red_ready, 5)
                dve.tensor_copy(T["live"][:, 1], rank_f[:]).then_inc(red_ready, 1)

            @block.tensor
            def _(pe):
                pe.wait_ge(ident_set, 1)
                pe.wait_ge(b_in, 32)
                pe.transpose(ps[:, 4, 32:32 + 2 * DC], brow[:], ident[0:2 * DC, 0:2 * DC]).then_inc(b_turned, 1)
                for i in range(2 * DC):
                    w, e = divmod(i, DC)
                    pe.wait_ge(w_in, 32)
                    if i >= 2:
                        pe.wait_ge(w_copied, i - 1)
                    for d in range(DC):
                        ins = pe.transpose(ps[:, i % 2, d * P:(d + 1) * P], wraw[:, w, d, e * P:(e + 1) * P], ident[:])
                    ins.then_inc(w_turned, 1)
                for t in range(NT):
                    pe.wait_ge(xn_ready, t + 1)
                    if t >= 2:
                        pe.wait_ge(x_copied, t - 1)
                    for d in range(DC):
                        ins = pe.transpose(ps[:, 2 + t % 2, d * P:(d + 1) * P], xn[:, t, d * P:(d + 1) * P], ident[:])
                    ins.then_inc(x_turned, 1)
                pe.wait_ge(w_copied, 2 * DC)
                for i in range(DC):
                    if i >= 2:
                        pe.wait_ge(w_copied, 2 * DC + i - 1)
                    for e in range(DC):
                        ins = pe.matmul(ps[:, i % 2], wT[:, 0, e, i * P:(i + 1) * P], wT[:, 1, e], start=e == 0,
                                        stop=e == DC - 1)
                    ins.then_inc(w_turned, 1)
                pe.wait_ge(b_copied, 1)
                for w in (1, 0):
                    for j in range(DC):
                        for e in range(DC):
                            col = (1 - w) * DC + j
                            pe.matmul(ps[:, 4, col:col + 1], wT[:, w, e, j * P:(j + 1) * P],
                                      bqk[:, 1 - w, e:e + 1], start=e == 0, stop=e == DC - 1)
                pe.wait_ge(prod_ready, 1)
                for e in range(DC):
                    ins = pe.matmul(ps[:, 4, 8:9], T["ones"][:], prod[:, e:e + 1], start=e == 0, stop=e == DC - 1)
                ins.then_inc(cols_ready, 1)
                pe.wait_ge(w_copied, 3 * DC)
                pe.wait_ge(x_copied, NT)
                for i in range(2 * DC):
                    half, j = divmod(i, DC)
                    if i >= 2:
                        pe.wait_ge(gf_ready, i - 1)
                    for d in range(DC):
                        ins = pe.matmul(ps[:, 5 + i % 2], M[:, d, j * P:(j + 1) * P],
                                        xnT[:, d, half * 512:half * 512 + 512], start=d == 0, stop=d == DC - 1)
                    ins.then_inc(g_ready, 1)
                pe.wait_ge(cols_copied, 1)
                for t in range(NT):
                    for d in range(DC):
                        ins = pe.matmul(ps[:, 4, 16 + t:17 + t], xnT[:, d, t * P:(t + 1) * P],
                                        cols[:, DC + d:DC + d + 1], start=d == 0, stop=d == DC - 1)
                ins.then_inc(c_ready, 1)
                pe.wait_ge(red_ready, 1)
                for t in range(QT):
                    ins = pe.matmul(ps[:, 7, 0:NB], T["ones"][:], red[:, t], start=t == 0, stop=t == QT - 1)
                ins.then_inc(any_ready, 1)


def cross_attention(nc, T, io):
    with ExitStack() as ctx:
        m = Mem(nc, ctx)
        ps, ident, ghi, glo, live = T["ps"], T["ident"], T["ghi"], T["glo"], T["live"]
        m_run, l_run, acc, c = T["m_run"], T["l_run"], T["acc"], T["c"]
        raw = m.sb("ctx_raw", [P, B, KC, D])
        chi = m.sb("ctx_hi", [P, B, KC, D], F32R)
        clo = m.sb("ctx_lo", [P, B, KC, D], F32R)
        cThi = m.sb("ctxT_hi", [P, B, DC, KB], F32R)
        cTlo = m.sb("ctxT_lo", [P, B, DC, KB], F32R)
        mask = m.sb("mask_block", [P, QT, KB], U8)
        bias = m.sb("mask_bias", [P, QT, KB])
        p = m.sb("probs", [P, 2, KB])
        pThi = m.sb("probsT_hi", [P, 2, KB], F32R)
        pTlo = m.sb("probsT_lo", [P, 2, KB], F32R)
        rmax, mnew, nb, dm = (m.sb(n, [P, NT]) for n in ("rmax", "mnew", "nb", "dm"))
        corr, rsum = m.sb("corr", [P, NT]), m.sb("rsum", [P, NT])

        ctx_in = [m.sem(f"ctx_in{s}") for s in range(B)]
        turned = [m.sem(f"ctx_turned{s}") for s in range(B)]
        split = [m.sem(f"ctx_split{s}") for s in range(B)]
        mblk_in, bias_ready = m.sem("mblk_in"), m.sem("bias_ready")
        thi_ready, tlo_ready = m.sem("ctxT_hi_ready"), m.sem("ctxT_lo_ready")
        score_ready, score_read = m.sem("score_ready"), m.sem("score_read")
        m_step, nb_ready = m.sem("m_step"), m.sem("nb_ready")
        p_ready, corr_ready = m.sem("p_ready"), m.sem("corr_ready")
        pt_ready, pthi_ready, ptlo_ready = m.sem("pt_ready"), m.sem("pt_hi_ready"), m.sem("pt_lo_ready")
        pv_ready, acc_done, l_done = m.sem("pv_ready"), m.sem("acc_done"), m.sem("l_done")
        sp_waited, pool_waited, dve_waited = m.sem("sp_waited"), m.sem("pool_waited"), m.sem("dve_waited")
        SCORE, PT, PV, TURN = 0, 2, 4, 6

        def taken(eng, step):
            with eng.Fori(0, NB) as b:
                flag = eng.value_load(live[0:1, 0, bass.ds(b, 1)], min_val=0, max_val=1)
                before = eng.value_load(live[0:1, 1, bass.ds(b, 1)], min_val=0, max_val=NB - 1)
                with eng.If(flag > 0):
                    step(b, before + 1)
                with eng.Else():
                    pass

        with nc.Block() as block:

            @block.sync
            def _(sp):
                for s in range(B):
                    sp.sem_inc(ctx_in[s], 16)
                sp.sem_inc(mblk_in, 16)
                context = io["ctx"].rearrange("s (b k p) d -> s b p k d", k=KC, p=P)
                masks = io["mask"].rearrange("(t p) (b k) -> b p t k", p=P, k=KB)

                def step(b, r):
                    for s in range(B):
                        sp.wait_ge(turned[s], r * DC)
                        apart(sp, sp_waited)
                        sp.wait_ge(split[s], r * 2)
                        apart(sp, sp_waited)
                        sp.dma_start(raw[:, s], context[s, b]).then_inc(ctx_in[s], 16)
                        if s == 0:
                            sp.wait_ge(bias_ready, r)
                            apart(sp, sp_waited)
                            sp.dma_start(mask[:], masks[b]).then_inc(mblk_in, 16)

                taken(sp, step)

            @block.gpsimd
            def _(pool):
                for s in range(B):
                    pool.sem_inc(split[s], 2)
                pool.sem_inc(bias_ready, 1)

                def step(b, r):
                    pool.wait_ge(mblk_in, r * 16 + 16)
                    pool.wait_ge(score_read, r * NT)
                    apart(pool, pool_waited)
                    pool.tensor_scalar(bias[:], mask[:], BIG, -BIG, ALU.mult, ALU.add).then_inc(bias_ready, 1)
                    for s in range(B):
                        pool.wait_ge(ctx_in[s], r * 16 + 16)
                        pool.wait_ge(pv_ready, r * NT)
                        apart(pool, pool_waited)
                        pool.tensor_copy(chi[:, s], raw[:, s]).then_inc(split[s], 1)
                        pool.wait_ge(split[s], r * 2 + 1)
                        pool.tensor_tensor(clo[:, s], raw[:, s], chi[:, s].bitcast(F32),
                                           ALU.subtract).then_inc(split[s], 1)

                taken(pool, step)

            @block.tensor
            def _(pe):
                for s in range(B):
                    pe.sem_inc(turned[s], DC)
                pe.sem_inc(score_ready, NT)
                pe.sem_inc(pt_ready, NT)
                pe.sem_inc(pv_ready, NT)

                def turn(r, s, g):
                    n = s * DC + g
                    pe.wait_ge(ctx_in[s], r * 16 + 16)
                    pe.wait_ge(tlo_ready, r * B * DC + n - 1)
                    for k in range(KC):
                        ins = pe.transpose(ps[:, TURN + g % 2, k * P:(k + 1) * P], raw[:, s, k, g * P:(g + 1) * P], ident[:])
                    ins.then_inc(turned[s], 1)

                def score(r, u):
                    s = u // QT
                    if u % QT == 0:
                        pe.wait_ge(tlo_ready, r * B * DC + (s + 1) * DC)
                    pe.wait_ge(score_read, r * NT + u - 1)
                    n = 0
                    for d in range(DC):
                        for a, b in ((ghi, cThi), (glo, cThi), (ghi, cTlo)):
                            ins = pe.matmul(ps[:, SCORE + u % 2], a[:, d, u * P:(u + 1) * P], b[:, s, d],
                                            start=n == 0, stop=n == 3 * DC - 1)
                            n += 1
                    ins.then_inc(score_ready, 1)

                def turn_probs(r, u):
                    pe.wait_ge(p_ready, r * NT + u + 1)
                    pe.wait_ge(ptlo_ready, r * NT + u - 1)
                    for k in range(KC):
                        ins = pe.transpose(ps[:, PT + u % 2, k * P:(k + 1) * P], p[:, u % 2, k * P:(k + 1) * P], ident[:])
                    ins.then_inc(pt_ready, 1)

                def value(r, u):
                    s = u // QT
                    if u % QT == 0:
                        pe.wait_ge(split[s], r * 2 + 2)
                    pe.wait_ge(ptlo_ready, r * NT + u + 1)
                    pe.wait_ge(acc_done, r * NT + u - 1)
                    n = 0
                    for k in range(KC):
                        for a, b in ((pThi, chi), (pTlo, chi), (pThi, clo)):
                            ins = pe.matmul(ps[:, PV + u % 2], a[:, u % 2, k * P:(k + 1) * P], b[:, s, k],
                                            start=n == 0, stop=n == 3 * KC - 1)
                            n += 1
                    ins.then_inc(pv_ready, 1)

                def step(b, r):
                    for g in range(DC):
                        turn(r, 0, g)
                    for u in range(NT + 2):
                        if u < NT:
                            score(r, u)
                        if u in (1, 2):
                            turn(r, 1, 2 * u - 2)
                            turn(r, 1, 2 * u - 1)
                        if 1 <= u <= NT:
                            turn_probs(r, u - 1)
                        if u >= 2:
                            value(r, u - 2)

                taken(pe, step)

            @block.scalar
            def _(act):
                act.sem_inc(thi_ready, B * DC)
                act.sem_inc(p_ready, NT)
                act.sem_inc(corr_ready, NT)
                act.sem_inc(pthi_ready, NT)

                def context_hi(r, s, g):
                    n = s * DC + g
                    act.wait_ge(turned[s], r * DC + g + 1)
                    if g == 0:
                        act.wait_ge(score_ready, r * NT)
                    act.copy(cThi[:, s, g], ps[:, TURN + g % 2]).then_inc(thi_ready, 1)

                def probs(r, u):
                    act.wait_ge(nb_ready, r * 2 * NT + 2 * u + 2)
                    if u == 0:
                        act.wait_ge(acc_done, r * NT)
                        act.wait_ge(l_done, r * NT)
                    act.activation(p[:, u % 2], p[:, u % 2], ACT.Exp, bias=nb[:, u:u + 1], scale=1.0,
                                   accum_out=rsum[:, u:u + 1]).then_inc(p_ready, 1)
                    act.activation(corr[:, u:u + 1], dm[:, u:u + 1], ACT.Exp).then_inc(corr_ready, 1)

                def probs_hi(r, u):
                    act.wait_ge(pt_ready, r * NT + u + 1)
                    act.wait_ge(pv_ready, r * NT + u - 1)
                    act.copy(pThi[:, u % 2], ps[:, PT + u % 2]).then_inc(pthi_ready, 1)

                def step(b, r):
                    for g in range(DC):
                        context_hi(r, 0, g)
                    for u in range(NT + 1):
                        if u < NT:
                            probs(r, u)
                        if u in (1, 2):
                            context_hi(r, 1, 2 * u - 2)
                            context_hi(r, 1, 2 * u - 1)
                        if u >= 1:
                            probs_hi(r, u - 1)

                taken(act, step)

            @block.vector
            def _(dve):
                dve.sem_inc(tlo_ready, B * DC)
                dve.sem_inc(score_read, NT)
                dve.sem_inc(m_step, 2 * NT)
                dve.sem_inc(nb_ready, 2 * NT)
                dve.sem_inc(ptlo_ready, NT)
                dve.sem_inc(acc_done, NT)
                dve.sem_inc(l_done, NT)

                def context_lo(r, s, g):
                    dve.wait_ge(thi_ready, r * B * DC + s * DC + g + 1)
                    dve.tensor_tensor(cTlo[:, s, g], ps[:, TURN + g % 2], cThi[:, s, g].bitcast(F32),
                                      ALU.subtract).then_inc(tlo_ready, 1)

                def row_max(r, u):
                    if u == 0:
                        dve.wait_ge(bias_ready, r + 1)
                        dve.wait_ge(corr_ready, r * NT)
                    dve.wait_ge(score_ready, r * NT + u + 1)
                    dve.wait_ge(pt_ready, r * NT + u - 1)
                    apart(dve, dve_waited)
                    dve.tensor_tensor_reduce(out=p[:, u % 2], in0=ps[:, SCORE + u % 2], in1=bias[:, u % QT],
                                             scale=1.0, scalar=LOWEST, op0=ALU.add, op1=ALU.max,
                                             accum_out=rmax[:, u:u + 1]).then_inc(score_read, 1)
                    dve.wait_ge(score_read, r * NT + u + 1)
                    dve.scalar_tensor_tensor(out=mnew[:, u:u + 1], in0=rmax[:, u:u + 1], scalar=c[:, u:u + 1],
                                             in1=m_run[:, u:u + 1], op0=ALU.add, op1=ALU.max).then_inc(m_step, 1)
                    dve.wait_ge(m_step, r * 2 * NT + 2 * u + 1)
                    dve.tensor_tensor(nb[:, u:u + 1], c[:, u:u + 1], mnew[:, u:u + 1], ALU.subtract).then_inc(nb_ready, 1)
                    dve.tensor_tensor(dm[:, u:u + 1], m_run[:, u:u + 1], mnew[:, u:u + 1],
                                      ALU.subtract).then_inc(nb_ready, 1)
                    dve.wait_ge(nb_ready, r * 2 * NT + 2 * u + 2)
                    dve.tensor_copy(m_run[:, u:u + 1], mnew[:, u:u + 1]).then_inc(m_step, 1)

                def probs_lo(r, u):
                    dve.wait_ge(pthi_ready, r * NT + u + 1)
                    dve.tensor_tensor(pTlo[:, u % 2], ps[:, PT + u % 2], pThi[:, u % 2].bitcast(F32),
                                      ALU.subtract).then_inc(ptlo_ready, 1)

                def accumulate(r, u):
                    dve.wait_ge(corr_ready, r * NT + u + 1)
                    dve.wait_ge(p_ready, r * NT + u + 1)
                    dve.scalar_tensor_tensor(out=l_run[:, u:u + 1], in0=l_run[:, u:u + 1], scalar=corr[:, u:u + 1],
                                             in1=rsum[:, u:u + 1], op0=ALU.mult, op1=ALU.add).then_inc(l_done, 1)
                    dve.wait_ge(pv_ready, r * NT + u + 1)
                    dve.scalar_tensor_tensor(out=acc[:, u], in0=acc[:, u], scalar=corr[:, u:u + 1],
                                             in1=ps[:, PV + u % 2], op0=ALU.mult, op1=ALU.add).then_inc(acc_done, 1)

                def step(b, r):
                    dve.wait_ge(acc_done, r * NT)
                    dve.wait_ge(m_step, r * 2 * NT)
                    for g in range(DC):
                        context_lo(r, 0, g)
                    for u in range(NT + 2):
                        if u < NT:
                            row_max(r, u)
                        if u in (1, 2):
                            context_lo(r, 1, 2 * u - 2)
                            context_lo(r, 1, 2 * u - 1)
                        if 1 <= u <= NT:
                            probs_lo(r, u - 1)
                        if u >= 2:
                            accumulate(r, u - 2)

                taken(dve, step)


def latents(nc, T, io):
    with ExitStack() as ctx:
        m = Mem(nc, ctx)
        ps, x, ident, acc = T["ps"], T["x"], T["ident"], T["acc"]
        accT = m.sb("accT", [P, 2, DC, P])
        bv = m.sb("bv_rows", [P, D])
        xn = m.sb("xn2", [P, NT, D])
        xnT = m.sb("xn2T", [P, DC, B * S])
        lat = m.sb("latent", [P, 2, 512])
        seen, lsum, linv, scale = (m.sb(n, [P, NT]) for n in ("seen", "lsum", "linv", "scale"))
        stats, mv = m.sb("stats2", [P, NT, 6]), m.sb("mv2", [P, NT, 2])
        varp, std, rstd = (m.sb(n, [P, NT]) for n in ("varp2", "std2", "rstd2"))

        bv_in, bv_added, dve_step = m.sem("bv_in"), m.sem("bv_added"), m.sem("c_dve_step")
        a_turned, a_copied, v_ready, x_ready = m.sem("a_turned"), m.sem("a_copied"), m.sem("wv_ready"), m.sem("x1_ready")
        var_ready, std_ready, xn_ready = m.sem("var2_ready"), m.sem("std2_ready"), m.sem("xn2_ready")
        x_turned, x_copied = m.sem("x2_turned"), m.sem("x2_copied")
        w_split, l_ready, l_copied, lhi_ready, llo_ready = (
            m.sem("w_split"), m.sem("lat_ready"), m.sem("lat_copied"), m.sem("lat_hi_ready"), m.sem("lat_lo_ready"))
        val_ready, val_copied = m.sem("val_ready"), m.sem("val_copied")
        names = ("uq", "uk", "uv")

        with nc.Block() as block:

            @block.sync
            def _(sp):
                sp.dma_start(bv[:], io["bv"].rearrange("(a d) -> a d", a=1).to_broadcast([P, D])).then_inc(bv_in, 16)

            @block.gpsimd
            def _(pool):
                pool.wait_ge(bv_in, 16)
                pool.wait_ge(T["weights_in"], T["weights_total"])
                pool.tensor_tensor(x[:], x[:], bv[:].unsqueeze(1).to_broadcast([P, NT, D]), ALU.add).then_inc(bv_added, 1)
                for n, w in enumerate(names):
                    pool.tensor_copy(T[w + "_hi"][:, 0:D], T[w][:]).then_inc(w_split, 1)
                    pool.wait_ge(w_split, 2 * n + 1)
                    pool.tensor_tensor(T[w + "_lo"][:, 0:D], T[w][:], T[w + "_hi"][:, 0:D].bitcast(F32),
                                       ALU.subtract).then_inc(w_split, 1)
                for w in names[0:2]:
                    pool.memset(T[w + "_hi"][:, D:D + DK].bitcast(F32), 0.0)
                    pool.memset(T[w + "_lo"][:, D:D + DK].bitcast(F32), 0.0)
                for i in range(4):
                    which, half = divmod(i, 2)
                    pool.wait_ge(lhi_ready, i + 1)
                    pool.tensor_tensor(T["lat_lo"][:, which, half * 512:half * 512 + 512], lat[:, i % 2],
                                       T["lat_hi"][:, which, half * 512:half * 512 + 512].bitcast(F32),
                                       ALU.subtract).then_inc(llo_ready, 1)

            @block.scalar
            def _(act):
                for t in range(NT):
                    act.wait_ge(a_turned, t + 1)
                    if t >= 2:
                        act.wait_ge(v_ready, t - 1)
                    act.copy(accT[:, t % 2], ps[:, t % 2].rearrange("p (c r) -> p c r", c=DC)).then_inc(a_copied, 1)
                act.wait_ge(var_ready, 1)
                act.activation(std[:], varp[:], ACT.Sqrt).then_inc(std_ready, 1)
                for t in range(NT):
                    act.wait_ge(x_turned, t + 1)
                    act.copy(xnT[:, :, t * P:(t + 1) * P], ps[:, 4 + t % 2].rearrange("p (c r) -> p c r", c=DC)).then_inc(x_copied, 1)
                for i in range(4):
                    which, half = divmod(i, 2)
                    act.wait_ge(l_copied, i + 1)
                    act.copy(T["lat_hi"][:, which, half * 512:half * 512 + 512], lat[:, i % 2]).then_inc(lhi_ready, 1)

            @block.vector
            def _(dve):
                link = chained(dve, dve_step)
                link(dve.tensor_scalar(seen[:], T["m_run"][:], -0.5 * BIG, None, ALU.is_gt))
                link(dve.tensor_tensor(lsum[:], T["l_run"][:], seen[:], ALU.mult))
                link(dve.reciprocal(linv[:], lsum[:]))
                link(dve.tensor_tensor(scale[:], linv[:], seen[:], ALU.mult))
                dve.wait_ge(bv_added, 1)
                for t in range(NT):
                    dve.wait_ge(v_ready, t + 1)
                    dve.scalar_tensor_tensor(out=x[:, t], in0=ps[:, 2 + t % 2], scalar=scale[:, t:t + 1], in1=x[:, t],
                                             op0=ALU.mult, op1=ALU.add).then_inc(x_ready, 1)
                    dve.wait_ge(x_ready, t + 1)
                    dve.bn_stats(stats[:, t, :], x[:, t, :]).then_inc(dve_step, 1)
                dve.wait_ge(dve_step, 4 + NT)
                for t in range(NT):
                    ins = dve.bn_aggr(mv[:, t, :], stats[:, t, :])
                ins.then_inc(dve_step, 1)
                dve.wait_ge(dve_step, 5 + NT)
                dve.tensor_scalar(varp[:], mv[:, :, 1], EPS, None, ALU.add).then_inc(var_ready, 1)
                dve.wait_ge(std_ready, 1)
                dve.reciprocal(rstd[:], std[:]).then_inc(dve_step, 1)
                dve.wait_ge(dve_step, 6 + NT)
                for t in range(NT):
                    dve.tensor_scalar(xn[:, t], x[:, t], mv[:, t, 0:1], rstd[:, t:t + 1], ALU.subtract,
                                      ALU.mult).then_inc(xn_ready, 1)
                for i in range(4):
                    dve.wait_ge(l_ready, i + 1)
                    if i >= 2:
                        dve.wait_ge(llo_ready, i - 1)
                    dve.tensor_copy(lat[:, i % 2], ps[:, 6 + i % 2]).then_inc(l_copied, 1)
                for t in range(NT):
                    dve.wait_ge(val_ready, t + 1)
                    dve.tensor_copy(T["v"][:, t], ps[:, t % 2]).then_inc(val_copied, 1)

            @block.tensor
            def _(pe):
                def turn_acc(t):
                    if t >= 2:
                        pe.wait_ge(a_copied, t - 1)
                    for d in range(DC):
                        ins = pe.transpose(ps[:, t % 2, d * P:(d + 1) * P], acc[:, t, d * P:(d + 1) * P], ident[:])
                    ins.then_inc(a_turned, 1)

                turn_acc(0)
                pe.wait_ge(T["weights_in"], T["weights_total"])
                for t in range(NT):
                    if t + 1 < NT:
                        turn_acc(t + 1)
                    pe.wait_ge(a_copied, t + 1)
                    if t >= 2:
                        pe.wait_ge(x_ready, t - 1)
                    for d in range(DC):
                        ins = pe.matmul(ps[:, 2 + t % 2], accT[:, t % 2, d], T["Wv"][:, d], start=d == 0, stop=d == DC - 1)
                    ins.then_inc(v_ready, 1)
                for t in range(NT):
                    pe.wait_ge(xn_ready, t + 1)
                    if t >= 2:
                        pe.wait_ge(x_copied, t - 1)
                    for d in range(DC):
                        ins = pe.transpose(ps[:, 4 + t % 2, d * P:(d + 1) * P], xn[:, t, d * P:(d + 1) * P], ident[:])
                    ins.then_inc(x_turned, 1)
                for i in range(4):
                    which, half = divmod(i, 2)
                    pe.wait_ge(x_copied, NT)
                    if i >= 2:
                        pe.wait_ge(l_copied, i - 1)
                    for d in range(DC):
                        ins = pe.matmul(ps[:, 6 + i % 2], T["dqkv"][:, which, d], xnT[:, d, half * 512:half * 512 + 512],
                                        start=d == 0, stop=d == DC - 1)
                    ins.then_inc(l_ready, 1)
                pe.wait_ge(w_split, 6)
                for t in range(NT):
                    pe.wait_ge(llo_ready, 2 + t // QT + 1)
                    if t >= 2:
                        pe.wait_ge(val_copied, t - 1)
                    ckv = (T["lat_hi"][:, 1, t * P:(t + 1) * P], T["lat_lo"][:, 1, t * P:(t + 1) * P])
                    pe.matmul(ps[:, t % 2], ckv[0], T["uv_hi"][:, 0:D], start=True, stop=False)
                    pe.matmul(ps[:, t % 2], ckv[1], T["uv_hi"][:, 0:D], start=False, stop=False)
                    pe.matmul(ps[:, t % 2], ckv[0], T["uv_lo"][:, 0:D], start=False, stop=True).then_inc(val_ready, 1)


def heads(nc, T, io):
    R3 = 3 * DK
    SC = float(DK) ** -0.5
    with ExitStack() as ctx:
        m = Mem(nc, ctx)
        ps, ident = T["ps"], T["ident"]
        w3 = {n: m.sb("w3_" + n, [P, 2, 3, DK], F32R) for n in ("uq_hi", "uq_lo", "uk_hi", "uk_lo")}
        qk = [[m.sb(f"{n}3_{j}", [R3, B * S], F32R) for j in range(2)] for n in ("q", "k")]
        causal = m.sb("causal", [P, S])
        p = m.sb("head_probs", [P, 2, S])
        pT = m.sb("head_probsT", [P, 2, S])
        rmax, nb, rsum = m.sb("head_max", [P, 2, NT]), m.sb("head_nb", [P, 2, NT]), m.sb("head_sum", [P, 2, NT])
        rinv = m.sb("head_inv", [P, 2, NT])

        causal_set, pool_step = m.sem("causal_set"), m.sem("d_pool_step")
        w_ready, proj_ready, hi_ready, lo_ready = m.sem("w3_ready"), m.sem("proj_ready"), m.sem("proj_hi"), m.sem("proj_lo")
        score_ready, score_read, nb_ready = m.sem("hscore_ready"), m.sem("hscore_read"), m.sem("hnb_ready")
        p_ready, pt_ready, pta_ready, ptd_ready = m.sem("hp_ready"), m.sem("hpt_ready"), m.sem("hpt_act"), m.sem("hpt_dve")
        pv_ready, inv_ready, o_ready = m.sem("hpv_ready"), m.sem("hinv_ready"), m.sem("ho_ready")
        pool_waited, dve_waited = m.sem("hpool_waited"), m.sem("hdve_waited")
        SCORE, PT, PV, PROJ = 2, 4, 6, 0
        U = 2 * NT
        ON_DVE = (3,)
        ND, NA = 4 * len(ON_DVE), U - 4 * len(ON_DVE)
        on_dve = [u % QT in ON_DVE for u in range(U)]
        sofar_d = [sum(on_dve[:u]) for u in range(U + 1)]
        sofar_a = [u - sofar_d[u] for u in range(U + 1)]

        def span(u):
            j, t = divmod(u, NT)
            b, q = divmod(t, QT)
            return j, t, b * S, (q + 1) * P

        def pt_moved(eng, r, u):
            k, v = divmod(u, U)
            if on_dve[v]:
                eng.wait_ge(ptd_ready, (r + k) * ND + sofar_d[v] + 1)
            else:
                eng.wait_ge(pta_ready, (r + k) * NA + sofar_a[v] + 1)

        def loop(eng, step):
            with eng.Fori(1, NH // 2 + 1) as r:
                step(r)

        with nc.Block() as block:

            @block.gpsimd
            def _(pool):
                link = chained(pool, pool_step)
                link(pool.memset(causal[:], 0.0))
                pool.affine_select(out=causal[:, S - P:S], in_=causal[:, S - P:S], compare_op=ALU.is_ge, fill=-BIG,
                                   base=0, pattern=[[-1, P]], channel_multiplier=1).then_inc(causal_set, 1)
                pool.sem_inc(w_ready, 2)

                def weights(j, h):
                    apart(pool, pool_waited)
                    for n in w3:
                        ins = pool.tensor_copy(w3[n][:, j], T[n][:, bass.ds(h * DK, DK)].unsqueeze(1).to_broadcast([P, 3, DK]))
                    ins.then_inc(w_ready, 1)

                weights(0, 0)

                def step(r):
                    pool.wait_ge(proj_ready, r * 8 - 4)
                    weights(1, r * 2 - 1)
                    pool.wait_ge(proj_ready, r * 8)
                    weights(0, r * 2)

                loop(pool, step)

            @block.tensor
            def _(pe):
                pe.sem_inc(proj_ready, 4)
                pe.sem_inc(score_ready, U)
                pe.sem_inc(pt_ready, U)
                pe.sem_inc(pv_ready, U)

                def project(n, j, i, w_count):
                    which, half = divmod(i, 2)
                    name = ("uq", "uk")[which]
                    pe.wait_ge(w_ready, w_count)
                    pe.wait_ge(lo_ready, n + i - 1)
                    cols = slice(half * 512, half * 512 + 512)
                    out = ps[0:R3, PROJ + i % 2]
                    whi = w3[name + "_hi"][:, j].rearrange("p a b -> p (a b)")
                    wlo = w3[name + "_lo"][:, j].rearrange("p a b -> p (a b)")
                    pe.matmul(out, whi, T["lat_hi"][:, which, cols], start=True, stop=False)
                    pe.matmul(out, wlo, T["lat_hi"][:, which, cols], start=False, stop=False)
                    pe.matmul(out, whi, T["lat_lo"][:, which, cols], start=False, stop=True).then_inc(proj_ready, 1)

                def score(r, u):
                    j, t, k0, n = span(u)
                    if t == 0:
                        pe.wait_ge(lo_ready, r * 8 + j * 4)
                    pe.wait_ge(score_read, r * U + u - 1)
                    pe.matmul(ps[:, SCORE + u % 2, 0:n], qk[0][j][:, t * P:(t + 1) * P], qk[1][j][:, k0:k0 + n],
                              start=True, stop=True).then_inc(score_ready, 1)

                def turn(r, u):
                    j, t, k0, n = span(u)
                    pe.wait_ge(p_ready, r * U + u + 1)
                    pt_moved(pe, r, u - 2)
                    for k in range(n // P):
                        ins = pe.transpose(ps[:, PT + u % 2, k * P:(k + 1) * P], p[:, u % 2, k * P:(k + 1) * P], ident[:])
                    ins.then_inc(pt_ready, 1)

                def value(r, u, h):
                    j, t, k0, n = span(u)
                    pt_moved(pe, r, u)
                    if t == 0:
                        pe.wait_ge(o_ready, r * 2 + j - 1)
                    for k in range(n // P):
                        ins = pe.matmul(ps[:, PV + j, t * DK:(t + 1) * DK], pT[:, u % 2, k * P:(k + 1) * P],
                                        T["v"][:, k0 // P + k, bass.ds(h * DK, DK)], start=k == 0, stop=k == n // P - 1)
                    ins.then_inc(pv_ready, 1)

                for i in range(4):
                    project(4, 0, i, 3)

                def step(r):
                    for u in range(U + 2):
                        if u < U:
                            score(r, u)
                            if u % NT in (2, 3, 5, 6):
                                j = u // NT
                                i = (2, 3, 5, 6).index(u % NT)
                                project(r * 8 + 4 * j, 1 - j, i, r * 2 + j + 2)
                        if 1 <= u <= U:
                            turn(r, u - 1)
                        if u >= 2:
                            value(r, u - 2, r * 2 - 2 + (u - 2) // NT)

                loop(pe, step)

            @block.scalar
            def _(act):
                act.sem_inc(hi_ready, 4)
                act.sem_inc(p_ready, U)
                act.sem_inc(pta_ready, NA)

                def project_hi(n, first, j, i):
                    which, half = divmod(i, 2)
                    act.wait_ge(proj_ready, n + i + 1)
                    if not first and i == 0:
                        act.wait_ge(score_ready, n * 2)
                    act.copy(qk[which][j][:, half * 512:half * 512 + 512], ps[0:R3, PROJ + i % 2]).then_inc(hi_ready, 1)

                def probs(r, u):
                    j, t, k0, n = span(u)
                    act.wait_ge(nb_ready, r * U + u + 1)
                    if t == 0:
                        act.wait_ge(inv_ready, r * 2 + j - 1)
                    act.activation(p[:, u % 2, 0:n], p[:, u % 2, 0:n], ACT.Exp, bias=nb[:, j, t:t + 1], scale=SC,
                                   accum_out=rsum[:, j, t:t + 1]).then_inc(p_ready, 1)

                def probs_move(r, u):
                    if not on_dve[u]:
                        j, t, k0, n = span(u)
                        act.wait_ge(pt_ready, r * U + u + 1)
                        act.wait_ge(pv_ready, r * U + u - 1)
                        act.copy(pT[:, u % 2, 0:n], ps[:, PT + u % 2, 0:n]).then_inc(pta_ready, 1)

                for i in range(4):
                    project_hi(4, True, 0, i)

                def step(r):
                    for u in range(U + 1):
                        if u < U:
                            probs(r, u)
                            if u % NT in (2, 3, 5, 6):
                                j = u // NT
                                project_hi(r * 8 + 4 * j, False, 1 - j, (2, 3, 5, 6).index(u % NT))
                        if u >= 1:
                            probs_move(r, u - 1)

                loop(act, step)

            @block.vector
            def _(dve):
                dve.sem_inc(lo_ready, 4)
                dve.sem_inc(score_read, U)
                dve.sem_inc(nb_ready, U)
                dve.sem_inc(ptd_ready, ND)
                dve.sem_inc(inv_ready, 2)
                dve.sem_inc(o_ready, 2)
                dve.wait_ge(causal_set, 1)

                def project_lo(n, j, i):
                    which, half = divmod(i, 2)
                    rows = (slice(2 * DK, 3 * DK), slice(DK, 2 * DK))[which]
                    dve.wait_ge(hi_ready, n + i + 1)
                    cols = slice(half * 512, half * 512 + 512)
                    dve.tensor_tensor(qk[which][j][rows, cols], ps[rows, PROJ + i % 2],
                                      qk[which][j][rows, cols].bitcast(F32), ALU.subtract).then_inc(lo_ready, 1)

                def row_max(r, u):
                    j, t, k0, n = span(u)
                    dve.wait_ge(score_ready, r * U + u + 1)
                    dve.wait_ge(pt_ready, r * U + u - 1)
                    apart(dve, dve_waited)
                    dve.tensor_tensor_reduce(out=p[:, u % 2, 0:n], in0=ps[:, SCORE + u % 2, 0:n], in1=causal[:, S - n:S],
                                             scale=1.0, scalar=LOWEST, op0=ALU.add, op1=ALU.max,
                                             accum_out=rmax[:, j, t:t + 1]).then_inc(score_read, 1)
                    dve.wait_ge(score_read, r * U + u + 1)
                    if t == 0:
                        dve.wait_ge(p_ready, r * U + u - NT)
                    dve.tensor_scalar(nb[:, j, t:t + 1], rmax[:, j, t:t + 1], -SC, None, ALU.mult).then_inc(nb_ready, 1)

                def probs_move(r, u):
                    if on_dve[u]:
                        j, t, k0, n = span(u)
                        dve.wait_ge(pt_ready, r * U + u + 1)
                        dve.wait_ge(pv_ready, r * U + u - 1)
                        dve.tensor_copy(pT[:, u % 2, 0:n], ps[:, PT + u % 2, 0:n]).then_inc(ptd_ready, 1)

                def output(r, j, h):
                    dve.wait_ge(p_ready, r * U + (j + 1) * NT)
                    dve.reciprocal(rinv[:, j], rsum[:, j]).then_inc(inv_ready, 1)
                    dve.wait_ge(inv_ready, r * 2 + j + 1)
                    dve.wait_ge(pv_ready, r * U + (j + 1) * NT)
                    dve.tensor_tensor(T["o"][:, :, bass.ds(h * DK, DK)],
                                      ps[:, PV + j, 0:NT * DK].rearrange("p (t e) -> p t e", t=NT),
                                      rinv[:, j].unsqueeze(2).to_broadcast([P, NT, DK]), ALU.mult).then_inc(o_ready, 1)

                for i in range(4):
                    project_lo(4, 0, i)

                def step(r):
                    for u in range(U + 2):
                        if u < U:
                            row_max(r, u)
                            if u % NT in (2, 3, 5, 6):
                                j = u // NT
                                project_lo(r * 8 + 4 * j, 1 - j, (2, 3, 5, 6).index(u % NT))
                        if 1 <= u <= U:
                            probs_move(r, u - 1)
                        if u >= 2 and (u - 2) % NT == NT - 1:
                            output(r, (u - 2) // NT, r * 2 - 2 + (u - 2) // NT)

                loop(dve, step)


def heads_out(nc, T):
    with ExitStack() as ctx:
        m = Mem(nc, ctx)
        ps, x, o, ident = T["ps"], T["x"], T["o"], T["ident"]
        oT = m.sb("oT", [P, 2, DC, P])
        o_turned, o_copied = m.sem("o_turned"), m.sem("o_copied")
        out_ready, x_ready = m.sem("wo_ready"), m.sem("x2_ready")

        with nc.Block() as block:

            @block.scalar
            def _(act):
                for t in range(NT):
                    act.wait_ge(o_turned, t + 1)
                    if t >= 2:
                        act.wait_ge(out_ready, t - 1)
                    act.copy(oT[:, t % 2], ps[:, t % 2].rearrange("p (c r) -> p c r", c=DC)).then_inc(o_copied, 1)

            @block.vector
            def _(dve):
                for t in range(NT):
                    dve.wait_ge(out_ready, t + 1)
                    dve.tensor_tensor(x[:, t], ps[:, 2 + t % 2], x[:, t], ALU.add).then_inc(x_ready, 1)

            @block.tensor
            def _(pe):
                def turn(t):
                    if t >= 2:
                        pe.wait_ge(o_copied, t - 1)
                    for d in range(DC):
                        ins = pe.transpose(ps[:, t % 2, d * P:(d + 1) * P], o[:, t, d * P:(d + 1) * P], ident[:])
                    ins.then_inc(o_turned, 1)

                turn(0)
                for t in range(NT):
                    if t + 1 < NT:
                        turn(t + 1)
                    pe.wait_ge(o_copied, t + 1)
                    if t >= 2:
                        pe.wait_ge(x_ready, t - 1)
                    for d in range(DC):
                        ins = pe.matmul(ps[:, 2 + t % 2], oT[:, t % 2, d], T["Wo"][:, d], start=d == 0, stop=d == DC - 1)
                    ins.then_inc(out_ready, 1)


def experts(nc, T, io):
    Q3 = 3 * H
    with ExitStack() as ctx:
        m = Mem(nc, ctx)
        ps, x, ident, w, y = T["ps"], T["x"], T["ident"], T["w"], T["y"]
        xn, xnT = m.sb("xn3", [P, NT, D]), m.sb("xn3T", [P, DC, B * S])
        raw, oraw = m.sb("expert_raw", [P, 2, DC, 3, H]), m.sb("expert_out_raw", [P, 2, D])
        whi, wlo = m.sb("expert_hi", [P, 2, DC, Q3], F32R), m.sb("expert_lo", [P, 2, DC, Q3], F32R)
        stats, mv = m.sb("stats3", [P, NT, 6]), m.sb("mv3", [P, NT, 2])
        varp, std, rstd = (m.sb(n, [P, NT]) for n in ("varp3", "std3", "rstd3"))
        square, sim, simsq = m.sb("square", [P, D]), m.sb("sim", [P, DC, E]), m.sb("simsq", [P, DC, E])
        gates, egate, sig, norm_e, inv_e = (m.sb(n, [P, E]) for n in ("gates", "egate", "sig", "norm_e", "inv_e"))
        rowsq, norm_n, inv_n = (m.sb(n, [P, NT]) for n in ("rowsq", "norm_n", "inv_n"))
        rev_i, rev = m.sb("rev_i", [P, E], I32), m.sb("rev", [P, E])
        L, L2, key, sel1, sel2, put, on, g, ex = (m.sb(n, [P, NT, E]) for n in (
            "logits", "logits2", "key", "sel1", "sel2", "put", "on", "gated", "gate_exp"))
        top, kmax, idle, gmax, gsum, ginv = (m.sb(n, [P, NT]) for n in ("top", "kmax", "idle", "gmax", "gsum", "ginv"))

        g_in, rev_set, dve_step = m.sem("gate_in"), m.sem("rev_set"), m.sem("e_dve_step")
        var_ready, std_ready, xn_ready, sq_ready = m.sem("var3_ready"), m.sem("std3_ready"), m.sem("xn3_ready"), m.sem("sq_ready")
        turned, hi_ready, lo_ready, f_ready = m.sem("xn3_turned"), m.sem("xn3_hi"), m.sem("xn3_lo"), m.sem("xn3_f32")
        simsq_ready, colsq_ready, logits_ready = m.sem("simsq_ready"), m.sem("colsq_ready"), m.sem("logits_ready")
        norm_ready, logits_read, e_ready, x_asked, x_ready = (m.sem(n) for n in (
            "norm_ready", "logits_read", "egate_ready", "gexp_asked", "gexp_ready"))
        raw_in = [m.sem(f"expert_in{j}") for j in range(2)]
        split = [m.sem(f"expert_split{j}") for j in range(2)]
        y_ready, y_added = m.sem("y_ready"), m.sem("y_added")
        sp_waited, pool_waited = m.sem("esp_waited"), m.sem("epool_waited")
        U = 2 * NT

        def rows(a):
            return a[:].unsqueeze(2).to_broadcast([P, NT, E])

        def cols(a):
            return a[:].unsqueeze(1).to_broadcast([P, NT, E])

        with nc.Block() as block:

            @block.sync
            def _(sp):
                sp.dma_start(sim[:], io["sim"].rearrange("(c p) e -> p c e", p=P)).then_inc(g_in, 16)
                sp.dma_start(gates[:], io["gates"].rearrange("(a e) -> a e", a=1).to_broadcast([P, E])).then_inc(g_in, 16)
                for j in range(2):
                    sp.sem_inc(split[j], 4)
                qkv = [io[n].rearrange("e (c p) h -> e p c h", p=P) for n in ("qp", "kp", "vp")]
                with sp.Fori(1, E // 2 + 1) as r:
                    for j in range(2):
                        e = r * 2 + (j - 2)
                        sp.wait_ge(split[j], r * 4)
                        apart(sp, sp_waited)
                        for n in range(3):
                            sp.dma_start(raw[:, j, :, n], qkv[n][e]).then_inc(raw_in[j], 16)
                        sp.dma_start(oraw[:, j], io["op"][e]).then_inc(raw_in[j], 16)

            @block.gpsimd
            def _(pool):
                pool.iota(rev_i[:], pattern=[[-1, E]], base=E, channel_multiplier=0).then_inc(rev_set, 1)
                pool.wait_ge(rev_set, 1)
                pool.tensor_copy(rev[:], rev_i[:]).then_inc(rev_set, 1)
                pool.memset(y[:], 0.0).then_inc(rev_set, 1)
                with pool.Fori(1, E // 2 + 1) as r:
                    for j in range(2):
                        e = r * 2 + (j - 2)
                        pool.wait_ge(raw_in[j], r * 64)
                        pool.wait_ge(y_ready, r * U + (j * NT - NT))
                        apart(pool, pool_waited)
                        raw_j = raw[:, j].rearrange("p c n h -> p c (n h)")
                        pool.tensor_copy(whi[:, j], raw_j).then_inc(split[j], 1)
                        pool.wait_ge(split[j], r * 4 + 1)
                        pool.tensor_tensor(wlo[:, j], raw_j, whi[:, j].bitcast(F32), ALU.subtract).then_inc(split[j], 1)
                        pool.tensor_copy(T["ohi"][:, bass.ds(e, 1)], oraw[:, j:j + 1]).then_inc(split[j], 1)
                        pool.wait_ge(split[j], r * 4 + 3)
                        pool.tensor_tensor(T["olo"][:, bass.ds(e, 1)], oraw[:, j:j + 1],
                                           T["ohi"][:, bass.ds(e, 1)].bitcast(F32), ALU.subtract).then_inc(split[j], 1)

            @block.scalar
            def _(act):
                act.wait_ge(var_ready, 1)
                act.activation(std[:], varp[:], ACT.Sqrt).then_inc(std_ready, 1)
                for t in range(NT):
                    act.wait_ge(xn_ready, t + 1)
                    if t >= 1:
                        act.wait_ge(sq_ready, t)
                    act.activation(square[:], xn[:, t], ACT.Square, accum_out=rowsq[:, t:t + 1]).then_inc(sq_ready, 1)
                    act.wait_ge(turned, t + 1)
                    tile = slice(t * P, (t + 1) * P)
                    src = ps[:, t % 2].rearrange("p (c r) -> p c r", c=DC)
                    act.copy(T["xnhi"][:, :, tile], src).then_inc(hi_ready, 1)
                    act.copy(xnT[:, :, tile], src).then_inc(f_ready, 1)
                act.wait_ge(sq_ready, NT)
                act.activation(norm_n[:], rowsq[:], ACT.Sqrt).then_inc(norm_ready, 1)
                act.wait_ge(colsq_ready, 1)
                act.activation(norm_e[:], ps[:, 3, 0:E], ACT.Sqrt).then_inc(norm_ready, 1)
                act.wait_ge(g_in, 32)
                act.activation(egate[:], gates[:], ACT.Exp, scale=-1.0).then_inc(e_ready, 1)
                act.wait_ge(x_asked, 1)
                act.activation(ex[:], key[:], ACT.Exp).then_inc(x_ready, 1)

            @block.vector
            def _(dve):
                link = chained(dve, dve_step)
                layernorm_stats(dve, link, x, stats, mv, varp).then_inc(var_ready, 1)
                dve.wait_ge(g_in, 32)
                dve.tensor_tensor(simsq[:], sim[:], sim[:], ALU.mult).then_inc(simsq_ready, 1)
                dve.wait_ge(std_ready, 1)
                link(dve.reciprocal(rstd[:], std[:]))
                for t in range(NT):
                    dve.tensor_scalar(xn[:, t], x[:, t], mv[:, t, 0:1], rstd[:, t:t + 1], ALU.subtract,
                                      ALU.mult).then_inc(xn_ready, 1)
                for t in range(NT):
                    tile = slice(t * P, (t + 1) * P)
                    dve.wait_ge(f_ready, t + 1)
                    dve.wait_ge(hi_ready, t + 1)
                    dve.tensor_tensor(T["xnlo"][:, :, tile], ps[:, t % 2].rearrange("p (c r) -> p c r", c=DC),
                                      T["xnhi"][:, :, tile].bitcast(F32), ALU.subtract).then_inc(lo_ready, 1)
                dve.wait_ge(norm_ready, 2)
                link(dve.tensor_scalar(norm_n[:], norm_n[:], 1e-12, None, ALU.max))
                link(dve.reciprocal(inv_n[:], norm_n[:]))
                link(dve.tensor_scalar(norm_e[:], norm_e[:], 1e-12, None, ALU.max))
                link(dve.reciprocal(inv_e[:], norm_e[:]))
                dve.wait_ge(e_ready, 1)
                link(dve.tensor_scalar(egate[:], egate[:], 1.0, None, ALU.add))
                link(dve.reciprocal(sig[:], egate[:]))
                dve.wait_ge(logits_ready, 1)
                dve.tensor_tensor(L[:], ps[:, 2, 0:NT * E].rearrange("p (t e) -> p t e", t=NT), rows(inv_n),
                                  ALU.mult).then_inc(logits_read, 1)
                dve.wait_ge(logits_read, 1)
                link(dve.tensor_tensor(L[:], L[:], cols(inv_e), ALU.mult))
                link(dve.tensor_tensor(L[:], L[:], cols(sig), ALU.subtract))
                dve.wait_ge(rev_set, 3)
                for logits, sel in ((L, sel1), (L2, sel2)):
                    link(dve.tensor_reduce(top[:], logits[:], AX.X, ALU.max))
                    link(dve.tensor_tensor(key[:], logits[:], rows(top), ALU.is_equal))
                    link(dve.tensor_tensor(key[:], key[:], cols(rev), ALU.mult))
                    if sel is sel1:
                        link(dve.tensor_scalar(idle[:], top[:], 0.0, None, ALU.is_le))
                    link(dve.tensor_reduce(kmax[:], key[:], AX.X, ALU.max))
                    link(dve.tensor_tensor(sel[:], key[:], rows(kmax), ALU.is_equal))
                    if sel is sel1:
                        link(dve.scalar_tensor_tensor(out=L2[:], in0=sel1[:], scalar=-BIG, in1=L[:], op0=ALU.mult,
                                                      op1=ALU.add))
                link(dve.tensor_tensor(put[:], sel1[:], sel2[:], ALU.add))
                link(dve.tensor_tensor(put[:], put[:], rows(idle), ALU.mult))
                link(dve.tensor_scalar(on[:], L[:], 0.0, None, ALU.is_gt))
                link(dve.tensor_tensor(on[:], on[:], put[:], ALU.max))
                link(dve.tensor_scalar(g[:], L[:], 0.0, None, ALU.max))
                link(dve.tensor_scalar(on[:], on[:], BIG, -BIG, ALU.mult, ALU.add))
                link(dve.tensor_tensor(g[:], g[:], on[:], ALU.add))
                link(dve.tensor_reduce(gmax[:], g[:], AX.X, ALU.max))
                dve.tensor_tensor(key[:], g[:], rows(gmax), ALU.subtract).then_inc(x_asked, 1)
                dve.wait_ge(x_ready, 1)
                link(dve.tensor_reduce(gsum[:], ex[:], AX.X, ALU.add))
                link(dve.reciprocal(ginv[:], gsum[:]))
                link(dve.tensor_tensor(w[:], ex[:], rows(ginv), ALU.mult))
                dve.sem_inc(y_added, U)
                with dve.Fori(1, E // 2 + 1) as r:
                    for n in range(U):
                        j, t = divmod(n, NT)
                        dve.wait_ge(y_added, r * U + (n + 1 - NT))
                        dve.wait_ge(y_ready, r * U + (n + 1))
                        dve.scalar_tensor_tensor(out=y[:, t], in0=ps[:, t, 0:Q3], scalar=w[:, t, bass.ds(r * 2 + (j - 2), 1)],
                                                 in1=y[:, t], op0=ALU.mult, op1=ALU.add).then_inc(y_added, 1)

            @block.tensor
            def _(pe):
                pe.sem_inc(y_ready, U)
                for t in range(NT):
                    pe.wait_ge(xn_ready, t + 1)
                    if t >= 2:
                        pe.wait_ge(lo_ready, t - 1)
                    for d in range(DC):
                        ins = pe.transpose(ps[:, t % 2, d * P:(d + 1) * P], xn[:, t, d * P:(d + 1) * P], ident[:])
                    ins.then_inc(turned, 1)
                pe.wait_ge(simsq_ready, 1)
                for d in range(DC):
                    ins = pe.matmul(ps[:, 3, 0:E], T["ones"][:], simsq[:, d], start=d == 0, stop=d == DC - 1)
                ins.then_inc(colsq_ready, 1)
                for t in range(NT):
                    pe.wait_ge(f_ready, t + 1)
                    for d in range(DC):
                        ins = pe.matmul(ps[:, 2, t * E:(t + 1) * E], xnT[:, d, t * P:(t + 1) * P], sim[:, d],
                                        start=d == 0, stop=d == DC - 1)
                ins.then_inc(logits_ready, 1)
                pe.wait_ge(lo_ready, NT)
                pe.wait_ge(norm_ready, 2)
                pe.wait_ge(logits_read, 1)
                with pe.Fori(1, E // 2 + 1) as r:
                    for n in range(U):
                        j, t = divmod(n, NT)
                        if t == 0:
                            pe.wait_ge(split[j], r * 4 + 2)
                        pe.wait_ge(y_added, r * U + (n + 1 - NT))
                        i = 0
                        for d in range(DC):
                            for a, b in ((T["xnhi"], whi), (T["xnlo"], whi), (T["xnhi"], wlo)):
                                ins = pe.matmul(ps[:, t, 0:Q3], a[:, d, t * P:(t + 1) * P], b[:, j, d], start=i == 0,
                                                stop=i == 3 * DC - 1)
                                i += 1
                        ins.then_inc(y_ready, 1)


def expert_attention(nc, T, io, out):
    SC = float(H) ** -0.5
    Z = E // 4
    with ExitStack() as ctx:
        m = Mem(nc, ctx)
        ps, x, ident, w, y = T["ps"], T["x"], T["ident"], T["w"], T["y"]
        qkT = m.sb("qkT", [P, 2, B * S])
        p, pT = m.sb("y_probs", [P, 2, S]), m.sb("y_probsT", [P, 2, S])
        rmax, nb, rsum, rinv = (m.sb("y_" + n, [P, NT]) for n in ("max", "nb", "sum", "inv"))
        o = m.sb("y_out", [P, NT, H])
        z = m.sb("z", [P, 2, E, H])
        zhi, zlo = m.sb("zT_hi", [P, Z, 512], F32R), m.sb("zT_lo", [P, Z, 512], F32R)

        dve_step = m.sem("g_dve_step")
        qk_turned, qk_copied = m.sem("qk_turned"), m.sem("qk_copied")
        s_ready, s_copied, nb_ready, p_ready = m.sem("ys_ready"), m.sem("ys_copied"), m.sem("ynb_ready"), m.sem("yp_ready")
        pt_ready, pt_copied, pv_ready, o_ready = m.sem("ypt_ready"), m.sem("ypt_copied"), m.sem("ypv_ready"), m.sem("yo_ready")
        z_ready = [m.sem("z_ready_dve"), m.sem("z_ready_pool")]
        z_turned, zhi_ready, zlo_ready = m.sem("z_turned"), m.sem("zhi_ready"), m.sem("zlo_ready")
        out_ready, x_ready, stored = m.sem("out_ready"), m.sem("x3_ready"), m.sem("stored")

        with nc.Block() as block:

            @block.sync
            def _(sp):
                rows = out.rearrange("b (t p) d -> (b t) p d", p=P)
                for t in range(NT):
                    sp.wait_ge(x_ready, t + 1)
                    sp.dma_start(rows[t], x[:, t]).then_inc(stored, 16)
                sp.wait_ge(stored, 16 * NT)

            @block.scalar
            def _(act):
                for i in range(2 * B):
                    b, which = divmod(i, 2)
                    act.wait_ge(qk_turned, i + 1)
                    act.copy(qkT[:, which, b * S:(b + 1) * S], ps[:, i % 2]).then_inc(qk_copied, 1)
                for t in range(NT + 1):
                    if t < NT:
                        act.wait_ge(nb_ready, t + 1)
                        if t >= 2:
                            act.wait_ge(pt_ready, t - 1)
                        act.activation(p[:, t % 2], ps[:, 2 + t % 2], ACT.Exp, bias=nb[:, t:t + 1], scale=SC,
                                       accum_out=rsum[:, t:t + 1]).then_inc(p_ready, 1)
                    if t >= 1:
                        act.wait_ge(pt_ready, t)
                        if t >= 3:
                            act.wait_ge(pv_ready, t - 2)
                        act.copy(pT[:, (t - 1) % 2], ps[:, 4 + (t - 1) % 2]).then_inc(pt_copied, 1)
                for t in range(NT):
                    for c in range(Z):
                        act.wait_ge(z_turned, t * Z + c + 1)
                        if t >= 1 and c == 0:
                            act.wait_ge(out_ready, t)
                        act.copy(zhi[:, c], ps[:, c % 4]).then_inc(zhi_ready, 1)

            @block.gpsimd
            def _(pool):
                for t in range(1, NT, 2):
                    pool.wait_ge(o_ready, t + 1)
                    if t >= 2:
                        pool.wait_ge(z_turned, (t - 1) * Z)
                    pool.tensor_tensor(z[:, t % 2], o[:, t].unsqueeze(1).to_broadcast([P, E, H]),
                                       w[:, t].unsqueeze(2).to_broadcast([P, E, H]), ALU.mult).then_inc(z_ready[1], 1)

            @block.vector
            def _(dve):
                for t in range(NT + 2):
                    if t < NT:
                        dve.wait_ge(s_ready, t + 1)
                        dve.tensor_reduce(rmax[:, t:t + 1], ps[:, 2 + t % 2], AX.X, ALU.max).then_inc(dve_step, 1)
                        dve.wait_ge(dve_step, t + 1)
                        dve.tensor_scalar(nb[:, t:t + 1], rmax[:, t:t + 1], -SC, None, ALU.mult).then_inc(nb_ready, 1)
                    if t >= 2:
                        u = t - 2
                        dve.wait_ge(p_ready, u + 1)
                        dve.reciprocal(rinv[:, u:u + 1], rsum[:, u:u + 1]).then_inc(s_copied, 1)
                        dve.wait_ge(s_copied, u + 1)
                        dve.wait_ge(pv_ready, u + 1)
                        dve.tensor_scalar(o[:, u], ps[:, 6 + u % 2, 0:H], rinv[:, u:u + 1], None,
                                          ALU.mult).then_inc(o_ready, 1)

                def products(t):
                    dve.wait_ge(o_ready, t + 1)
                    if t >= 2:
                        dve.wait_ge(z_turned, (t - 1) * Z)
                    dve.tensor_tensor(z[:, t % 2], o[:, t].unsqueeze(1).to_broadcast([P, E, H]),
                                      w[:, t].unsqueeze(2).to_broadcast([P, E, H]), ALU.mult).then_inc(z_ready[0], 1)

                def add_out(t):
                    dve.wait_ge(out_ready, t + 1)
                    dve.tensor_tensor(x[:, t], ps[:, 4 + t % 2], x[:, t], ALU.add).then_inc(x_ready, 1)

                products(0)
                for t in range(NT):
                    for c in range(Z):
                        dve.wait_ge(zhi_ready, t * Z + c + 1)
                        dve.tensor_tensor(zlo[:, c], ps[:, c % 4], zhi[:, c].bitcast(F32), ALU.subtract).then_inc(zlo_ready, 1)
                    if t % 2 and t + 1 < NT:
                        products(t + 1)
                    if t >= 1:
                        add_out(t - 1)
                add_out(NT - 1)

            @block.tensor
            def _(pe):
                for i in range(2 * B):
                    b, which = divmod(i, 2)
                    if i >= 2:
                        pe.wait_ge(qk_copied, i - 1)
                    for k in range(QT):
                        ins = pe.transpose(ps[:, i % 2, k * P:(k + 1) * P], y[:, b * QT + k, which * H:(which + 1) * H], ident[:])
                    ins.then_inc(qk_turned, 1)
                for t in range(NT + 2):
                    if t < NT:
                        b = t // QT
                        pe.wait_ge(qk_copied, 2 * b + 2)
                        if t >= 2:
                            pe.wait_ge(p_ready, t - 1)
                        pe.matmul(ps[:, 2 + t % 2], qkT[:, 0, t * P:(t + 1) * P], qkT[:, 1, b * S:(b + 1) * S],
                                  start=True, stop=True).then_inc(s_ready, 1)
                    if 1 <= t <= NT:
                        u = t - 1
                        pe.wait_ge(p_ready, u + 1)
                        if u >= 2:
                            pe.wait_ge(pt_copied, u - 1)
                        for k in range(QT):
                            ins = pe.transpose(ps[:, 4 + u % 2, k * P:(k + 1) * P], p[:, u % 2, k * P:(k + 1) * P], ident[:])
                        ins.then_inc(pt_ready, 1)
                    if t >= 2:
                        u = t - 2
                        pe.wait_ge(pt_copied, u + 1)
                        if u >= 2:
                            pe.wait_ge(o_ready, u - 1)
                        for k in range(QT):
                            ins = pe.matmul(ps[:, 6 + u % 2, 0:H], pT[:, u % 2, k * P:(k + 1) * P],
                                            y[:, (u // QT) * QT + k, 2 * H:3 * H], start=k == 0, stop=k == QT - 1)
                        ins.then_inc(pv_ready, 1)

                def turn(t):
                    pe.wait_ge(z_ready[t % 2], t // 2 + 1)
                    for c in range(Z):
                        if t >= 1:
                            pe.wait_ge(zlo_ready, (t - 1) * Z + c + 1)
                        for k in range(4):
                            ins = pe.transpose(ps[:, c, k * P:(k + 1) * P], z[:, t % 2, 4 * c + k], ident[:])
                        ins.then_inc(z_turned, 1)

                turn(0)
                for t in range(NT):
                    if t >= 2:
                        pe.wait_ge(x_ready, t - 1)
                    for e in range(E):
                        if e % 4 == 0:
                            pe.wait_ge(zlo_ready, t * Z + e // 4 + 1)
                        cut = slice((e % 4) * P, (e % 4 + 1) * P)
                        for i, (a, b) in enumerate(((zhi, T["ohi"]), (zlo, T["ohi"]), (zhi, T["olo"]))):
                            ins = pe.matmul(ps[:, 4 + t % 2], a[:, e // 4, cut], b[:, e], start=e == 0 and i == 0,
                                            stop=e == E - 1 and i == 2)
                    ins.then_inc(out_ready, 1)
                    if t + 1 < NT:
                        turn(t + 1)


def program(nc, io, out):
    with ExitStack() as ctx:
        m = Mem(nc, ctx)
        T = {"ps": ctx.enter_context(nc.psum_tensor("ps", [P, 8, 512], F32))}
        T["x"] = m.sb("x", [P, NT, D])
        T["ident"] = m.sb("ident", [P, P])
        T["ones"] = m.sb("ones", [P, P])
        T["weights_in"], T["weights_total"] = m.sem("weights_in"), 7 * 16

        with ExitStack() as early:
            m = Mem(nc, early)
            T["acc"] = m.sb("acc", [P, NT, D])
            T["m_run"], T["l_run"] = m.sb("m_run", [P, NT]), m.sb("l_run", [P, NT])
            T["Wv"], T["Wo"] = m.sb("Wv", [P, DC, D]), m.sb("Wo", [P, DC, D])
            T["dqkv"] = m.sb("W_dqkv", [P, 2, DC, DCQ])
            for n in ("uq", "uk", "uv"):
                T[n] = m.sb("W_" + n, [P, D])
            with ExitStack() as front:
                m = Mem(nc, front)
                T["ghi"], T["glo"] = m.sb("g_hi", [P, DC, B * S], F32R), m.sb("g_lo", [P, DC, B * S], F32R)
                T["c"] = m.sb("c", [P, NT])
                T["live"] = m.sb("live", [P, 2, NB], I32)
                queries(nc, T, io)
                cross_attention(nc, T, io)
            with ExitStack() as middle:
                m = Mem(nc, middle)
                T["lat_hi"], T["lat_lo"] = m.sb("lat_hi", [P, 2, B * S], F32R), m.sb("lat_lo", [P, 2, B * S], F32R)
                for n in ("uq", "uk", "uv"):
                    for half in ("_hi", "_lo"):
                        T[n + half] = m.sb("W_" + n + half, [P, D + DK], F32R)
                T["v"], T["o"] = m.sb("v", [P, NT, D]), m.sb("o", [P, NT, D])
                latents(nc, T, io)
                heads(nc, T, io)
                heads_out(nc, T)
        with ExitStack() as late:
            m = Mem(nc, late)
            T["xnhi"], T["xnlo"] = m.sb("xn3T_hi", [P, DC, B * S], F32R), m.sb("xn3T_lo", [P, DC, B * S], F32R)
            T["ohi"], T["olo"] = m.sb("O_hi", [P, E, D], F32R), m.sb("O_lo", [P, E, D], F32R)
            T["w"], T["y"] = m.sb("w", [P, NT, E]), m.sb("y", [P, NT, 3 * H])
            experts(nc, T, io)
            expert_attention(nc, T, io, out)


_INS = {"x": "x", "ctx": "ctx_1024", "mask": "mask_SxS2_bk0", "Wq": "L0_xattn_Wq", "bq": "L0_xattn_bq",
        "Wk": "L0_xattn_Wk", "bk": "L0_xattn_bk", "Wv": "L0_xattn_Wv", "bv": "L0_xattn_bv", "dq": "L0_attn_W_dq",
        "uq": "L0_attn_W_uq", "dkv": "L0_attn_W_dkv", "uk": "L0_attn_W_uk", "uv": "L0_attn_W_uv", "Wo": "L0_attn_W_o",
        "sim": "L0_ffn_sim_matrix", "gates": "L0_ffn_gates", "qp": "L0_ffn_q_proj", "kp": "L0_ffn_k_proj",
        "vp": "L0_ffn_v_proj", "op": "L0_ffn_o_proj"}


def kernel(**inputs):
    import numpy as _np
    import concourse.bacc as _bacc
    from concourse import mybir as _mybir
    from concourse.bass_utils import run_bass_kernel_spmd as _run

    nc = _bacc.Bacc("TRN2", target_bir_lowering=False, num_devices=1)
    arrays, io = {}, {}
    for name, key in _INS.items():
        a = _np.ascontiguousarray(inputs[key])
        arrays[f"in_{name}_dram"] = a
        dt = U8 if a.dtype == _np.bool_ else _mybir.dt.from_np(a.dtype)
        io[name] = nc.dram_tensor(f"in_{name}_dram", a.shape, dt, kind="ExternalInput").ap()
    out = nc.dram_tensor("out_dram", (B, S, D), _mybir.dt.from_np(_np.dtype("float32")), kind="ExternalOutput").ap()
    program(nc, io, out)
    r = _run(nc, [arrays], core_ids=[0])
    return r.results[0]["out_dram"]
```

```python
from contextlib import ExitStack

import concourse.bass as bass
from concourse import mybir

F32 = mybir.dt.float32
F32R = mybir.dt.float32r
I32 = mybir.dt.int32
U8 = mybir.dt.uint8
ALU = mybir.AluOpType
ACT = mybir.ActivationFunctionType
AX = mybir.AxisListType

P = 128
B, S, D = 2, 512, 512
KEYS = 8192
NT = B * S // P
QT = S // P
DC = D // P
KB = 512
NB = KEYS // KB
KC = KB // P
NH, DK = 16, 32
DCQ = 128
E, H = 16, 128
EPS = 1e-5
BIG = 1e30
LOWEST = -3e38
XSCALE = float(D) ** -0.5


class Mem:

    def __init__(self, nc, ctx):
        self.nc, self.ctx = nc, ctx

    def sb(self, name, shape, dt=F32):
        return self.ctx.enter_context(self.nc.sbuf_tensor(name, shape, dt))

    def sem(self, name):
        return self.ctx.enter_context(self.nc.semaphore(name))


def chained(eng, sem):
    count = [0]

    def link(ins):
        count[0] += 1
        ins.then_inc(sem, 1)
        eng.wait_ge(sem, count[0])

    return link


def apart(eng, waited):
    eng.sem_inc(waited, 1)


def layernorm_stats(dve, link, x, stats, mv, varp, rows_ready=None):
    for t in range(NT):
        if rows_ready is not None:
            rows_ready(t)
        link(dve.bn_stats(stats[:, t, :], x[:, t, :]))
    for t in range(NT):
        ins = dve.bn_aggr(mv[:, t, :], stats[:, t, :])
    link(ins)
    return dve.tensor_scalar(varp[:], mv[:, :, 1], EPS, None, ALU.add)


def queries(nc, T, io):
    with ExitStack() as ctx:
        m = Mem(nc, ctx)
        ps, x, ident = T["ps"], T["x"], T["ident"]
        wThi, wTlo = T["ghi"], T["glo"]
        xn = T["acc"]
        mask = m.sb("mask_rows", [P, 2, KEYS], U8)
        wraw, wvraw = m.sb("wraw", [P, 2, DC, D]), m.sb("wv_raw", [P, DC, D])
        Mhi, Mlo = m.sb("M_hi", [P, DC, D], F32R), m.sb("M_lo", [P, DC, D], F32R)
        xnThi, xnTlo = m.sb("xnT_hi", [P, DC, B * S], F32R), m.sb("xnT_lo", [P, DC, B * S], F32R)
        brow, bqk, prod = m.sb("brow", [2 * DC, P]), m.sb("bqk", [P, 2, DC]), m.sb("prod", [P, DC])
        bhl = m.sb("bqk_halves", [P, 2, DC, 2], F32R)
        cols, colsum = m.sb("cols", [P, 2 * DC, 2]), m.sb("colsum", [P, 2 * DC])
        wgcol, bb = m.sb("g_bias", [P, DC]), m.sb("bb", [P, 1])
        chl = m.sb("wqbk_halves", [P, DC, 2], F32R)
        cpair, csum = m.sb("c_pair", [P, NT, 2]), m.sb("c_sum", [P, NT])
        stats, mv = m.sb("stats", [P, NT, 6]), m.sb("mv", [P, NT, 2])
        varp, std, rstd = (m.sb(n, [P, NT]) for n in ("varp", "std", "rstd"))
        red, act_f = m.sb("red", [P, QT, NB]), m.sb("act_f", [P, NB])
        lower, grid = m.sb("lower", [P, NB, NB]), m.sb("grid", [P, NB, NB])
        iota_i, iota, rank, number = m.sb("iota_i", [P, NB], I32), m.sb("iota", [P, NB]), m.sb("rank", [P, NB]), m.sb("number", [P, NB])
        order, total = m.sb("order", [P, NB]), m.sb("total", [P, 1])

        x_in, b_in, wv_in = m.sem("x_in"), m.sem("b_in"), m.sem("wv_in")
        w_in = [m.sem("wq_in"), m.sem("wk_in")]
        mask_in = [m.sem("mask_in0"), m.sem("mask_in1")]
        ones_set, ident_set = m.sem("ones_set"), m.sem("ident_set")
        pool_step, dve_step = m.sem("a_pool_step"), m.sem("a_dve_step")
        var_ready, std_ready, xn_ready = m.sem("var_ready"), m.sem("std_ready"), m.sem("xn_ready")
        w_turned, w_hi, w_lo = m.sem("w_turned"), m.sem("w_hi"), m.sem("w_lo")
        x_turned, x_hi, x_lo = m.sem("x_turned"), m.sem("x_hi"), m.sem("x_lo")
        m_ready, m_hi, m_lo = m.sem("m_ready"), m.sem("m_hi"), m.sem("m_lo")
        b_turned, b_copied, cols_ready = m.sem("b_turned"), m.sem("b_copied"), m.sem("cols_ready")
        bias_ready, chl_ready = m.sem("g_bias_ready"), m.sem("chl_ready")
        g_ready, g_hi, g_lo, c_ready = m.sem("g_ready"), m.sem("g_hi_ready"), m.sem("g_lo_ready"), m.sem("c_ready")
        red_ready, any_ready = m.sem("red_ready"), m.sem("any_ready")
        halves = ((0, 0), (1, 0), (0, 1))

        with nc.Block() as block:

            @block.sync
            def _(sp):
                sp.dma_start(brow[0:DC], io["bq"].rearrange("(c p) -> c p", p=P)).then_inc(b_in, 16)
                sp.dma_start(brow[DC:2 * DC], io["bk"].rearrange("(c p) -> c p", p=P)).then_inc(b_in, 16)
                sp.dma_start(wraw[:, 0], io["Wq"].rearrange("(c p) e -> p c e", p=P)).then_inc(w_in[0], 16)
                sp.dma_start(x[:], io["x"].rearrange("b (t p) d -> p (b t) d", p=P)).then_inc(x_in, 16)
                sp.dma_start(wraw[:, 1], io["Wk"].rearrange("(c p) e -> p c e", p=P)).then_inc(w_in[1], 16)
                for t in range(QT):
                    if t == 2:
                        sp.dma_start(wvraw[:], io["Wv"].rearrange("(c p) e -> p c e", p=P)).then_inc(wv_in, 16)
                    if t >= 2:
                        sp.wait_ge(red_ready, t - 1)
                    sp.dma_start(mask[:, t % 2], io["mask"].rearrange("(t p) k -> t p k", p=P)[t]).then_inc(mask_in[t % 2], 16)
                for i, n in enumerate(("dq", "dkv")):
                    sp.dma_start(T["dqkv"][:, i], io[n].rearrange("(c p) e -> p c e", p=P)).then_inc(T["weights_in"], 16)
                for n in ("uq", "uk", "uv"):
                    sp.dma_start(T[n][:], io[n]).then_inc(T["weights_in"], 16)

            @block.gpsimd
            def _(pool):
                link = chained(pool, pool_step)
                link(pool.memset(ident[:], 0.0))
                pool.affine_select(out=ident[:], in_=ident[:], compare_op=ALU.not_equal, fill=1.0, base=0,
                                   pattern=[[-1, P]], channel_multiplier=1).then_inc(ident_set, 1)
                link(pool.memset(lower[:], 0.0))
                link(pool.affine_select(out=lower[:], in_=lower[:], compare_op=ALU.is_ge, fill=1.0, base=0,
                                        pattern=[[-1, NB], [1, NB]], channel_multiplier=0))
                link(pool.iota(iota_i[:], pattern=[[1, NB]], base=0, channel_multiplier=0))
                pool.tensor_copy(iota[:], iota_i[:]).then_inc(ones_set, 1)
                pool.wait_ge(wv_in, 16)
                link(pool.tensor_copy(T["Wvhi"][:], wvraw[:]))
                pool.tensor_tensor(T["Wvlo"][:], wvraw[:], T["Wvhi"][:].bitcast(F32), ALU.subtract).then_inc(pool_step, 1)

            @block.scalar
            def _(act):
                def weights_hi(i):
                    act.wait_ge(w_turned, i + 1)
                    act.copy(wThi[:, i // 2, (i % 2) * 512:(i % 2) * 512 + 512], ps[:, i % 2]).then_inc(w_hi, 1)

                for i in range(DC):
                    weights_hi(i)
                act.wait_ge(var_ready, 1)
                act.activation(std[:], varp[:], ACT.Sqrt).then_inc(std_ready, 1)
                for i in range(DC, 2 * DC):
                    weights_hi(i)
                for i in range(DC):
                    act.wait_ge(m_ready, i + 1)
                    act.activation(Mhi[:, i], ps[:, 2 + i % 2], ACT.Copy, scale=XSCALE).then_inc(m_hi, 1)
                for t in range(NT):
                    act.wait_ge(x_turned, t + 1)
                    act.copy(xnThi[:, :, t * P:(t + 1) * P], ps[:, t % 2].rearrange("p (c r) -> p c r", c=DC)).then_inc(x_hi, 1)
                act.wait_ge(bias_ready, 1)
                for i in range(2 * DC):
                    half, j = divmod(i, DC)
                    act.wait_ge(g_ready, i + 1)
                    act.activation(T["ghi"][:, j, half * 512:half * 512 + 512], ps[:, 5 + i % 2], ACT.Identity,
                                   bias=wgcol[:, j:j + 1], scale=1.0).then_inc(g_hi, 1)

            @block.vector
            def _(dve):
                link = chained(dve, dve_step)
                link(dve.memset(T["ones"][:], 1.0))
                dve.wait_ge(b_turned, 1)
                dve.tensor_copy(bqk[:].rearrange("p a c -> p (a c)"), ps[:, 4, 32:32 + 2 * DC]).then_inc(b_copied, 1)
                dve.wait_ge(b_copied, 1)
                dve.tensor_tensor(prod[:], bqk[:, 0], bqk[:, 1], ALU.mult).then_inc(b_copied, 1)
                dve.tensor_copy(bhl[:, :, :, 0], bqk[:]).then_inc(b_copied, 1)
                dve.wait_ge(b_copied, 3)
                dve.tensor_tensor(bhl[:, :, :, 1], bqk[:], bhl[:, :, :, 0].bitcast(F32), ALU.subtract).then_inc(b_copied, 1)

                def weights_lo(i):
                    dve.wait_ge(w_hi, i + 1)
                    at = slice((i % 2) * 512, (i % 2) * 512 + 512)
                    dve.tensor_tensor(wTlo[:, i // 2, at], ps[:, i % 2], wThi[:, i // 2, at].bitcast(F32),
                                      ALU.subtract).then_inc(w_lo, 1)

                for i in range(DC):
                    weights_lo(i)
                dve.wait_ge(x_in, 16)
                layernorm_stats(dve, link, x, stats, mv, varp).then_inc(var_ready, 1)
                for i in range(DC, 2 * DC):
                    weights_lo(i)
                dve.wait_ge(std_ready, 1)
                link(dve.reciprocal(rstd[:], std[:]))
                for t in range(NT):
                    dve.tensor_scalar(xn[:, t], x[:, t], mv[:, t, 0:1], rstd[:, t:t + 1], ALU.subtract,
                                      ALU.mult).then_inc(xn_ready, 1)
                for i in range(DC):
                    dve.wait_ge(m_hi, i + 1)
                    dve.scalar_tensor_tensor(out=Mlo[:, i], in0=ps[:, 2 + i % 2], scalar=XSCALE, in1=Mhi[:, i].bitcast(F32),
                                             op0=ALU.mult, op1=ALU.subtract).then_inc(m_lo, 1)
                dve.wait_ge(cols_ready, 1)
                link(dve.tensor_copy(cols[:].rearrange("p a b -> p (a b)"), ps[:, 4, 0:4 * DC]))
                link(dve.tensor_copy(bb[:], ps[:, 4, 4 * DC:4 * DC + 1]))
                link(dve.tensor_tensor(colsum[:], cols[:, :, 0], cols[:, :, 1], ALU.add))
                dve.tensor_scalar(wgcol[:], colsum[:, 0:DC], XSCALE, None, ALU.mult).then_inc(bias_ready, 1)
                link(dve.tensor_copy(chl[:, :, 0], colsum[:, DC:2 * DC]))
                dve.tensor_tensor(chl[:, :, 1], colsum[:, DC:2 * DC], chl[:, :, 0].bitcast(F32),
                                  ALU.subtract).then_inc(chl_ready, 1)
                for t in range(NT):
                    dve.wait_ge(x_hi, t + 1)
                    at = slice(t * P, (t + 1) * P)
                    dve.tensor_tensor(xnTlo[:, :, at], ps[:, t % 2].rearrange("p (c r) -> p c r", c=DC),
                                      xnThi[:, :, at].bitcast(F32), ALU.subtract).then_inc(x_lo, 1)
                for t in range(QT):
                    dve.wait_ge(mask_in[t % 2], 16 * (t // 2) + 16)
                    words = mask[:, t % 2].bitcast(I32).rearrange("p (b w) -> p b w", b=NB)
                    dve.tensor_reduce(red[:, t], words, AX.X, ALU.max).then_inc(red_ready, 1)
                dve.wait_ge(bias_ready, 1)

                def g_low(i):
                    half, j = divmod(i, DC)
                    at = slice(half * 512, half * 512 + 512)
                    dve.wait_ge(g_hi, i + 1)
                    dve.scalar_tensor_tensor(out=T["glo"][:, j, at], in0=ps[:, 5 + i % 2], scalar=wgcol[:, j:j + 1],
                                             in1=T["ghi"][:, j, at].bitcast(F32), op0=ALU.add,
                                             op1=ALU.subtract).then_inc(g_lo, 1)

                for i in range(2 * DC - 4):
                    g_low(i)
                dve.wait_ge(any_ready, 1)
                dve.wait_ge(ones_set, 1)
                link(dve.tensor_scalar(act_f[:], ps[:, 7, 0:NB], 0.0, None, ALU.is_gt))
                link(dve.tensor_tensor(grid[:], lower[:], act_f[:].unsqueeze(1).to_broadcast([P, NB, NB]), ALU.mult))
                link(dve.tensor_reduce(rank[:], grid[:], AX.X, ALU.add))
                link(dve.tensor_tensor(number[:], act_f[:], iota[:], ALU.mult))
                link(dve.tensor_reduce(total[:], act_f[:], AX.X, ALU.add))
                link(dve.tensor_tensor(grid[:], rank[:].unsqueeze(1).to_broadcast([P, NB, NB]),
                                       iota[:].unsqueeze(2).to_broadcast([P, NB, NB]), ALU.is_equal))
                link(dve.tensor_tensor(grid[:], grid[:], number[:].unsqueeze(1).to_broadcast([P, NB, NB]), ALU.mult))
                link(dve.tensor_reduce(order[:], grid[:], AX.X, ALU.add))
                link(dve.tensor_copy(T["live"][:, 0:NB], order[:]))
                link(dve.tensor_copy(T["live"][:, NB:NB + 1], total[:]))
                for i in range(2 * DC - 4, 2 * DC):
                    g_low(i)
                dve.wait_ge(c_ready, 1)
                link(dve.tensor_copy(cpair[:].rearrange("p t b -> p (t b)"), ps[:, 4, 64:64 + 2 * NT]))
                link(dve.tensor_tensor(csum[:], cpair[:, :, 0], cpair[:, :, 1], ALU.add))
                dve.tensor_scalar(T["c"][:], csum[:], bb[:, 0:1], XSCALE, ALU.add, ALU.mult).then_inc(dve_step, 1)

            @block.tensor
            def _(pe):
                pe.wait_ge(ident_set, 1)
                pe.wait_ge(b_in, 32)
                pe.transpose(ps[:, 4, 32:32 + 2 * DC], brow[:], ident[0:2 * DC, 0:2 * DC]).then_inc(b_turned, 1)
                for i in range(2 * DC):
                    w, e = divmod(i, DC)
                    pe.wait_ge(w_in[w], 16)
                    if i >= 2:
                        pe.wait_ge(w_lo, i - 1)
                    for d in range(DC):
                        ins = pe.transpose(ps[:, i % 2, d * P:(d + 1) * P], wraw[:, w, d, e * P:(e + 1) * P], ident[:])
                    ins.then_inc(w_turned, 1)
                wT = [[[h[:, (w * DC + e) // 2, (e % 2) * 512:(e % 2) * 512 + 512] for e in range(DC)] for w in range(2)]
                      for h in (wThi, wTlo)]
                pe.wait_ge(w_lo, 2 * DC)
                for i in range(DC):
                    if i >= 2:
                        pe.wait_ge(m_lo, i - 1)
                    n = 0
                    for e in range(DC):
                        for a, b in halves:
                            ins = pe.matmul(ps[:, 2 + i % 2], wT[a][0][e][:, i * P:(i + 1) * P], wT[b][1][e], start=n == 0,
                                            stop=n == 3 * DC - 1)
                            n += 1
                    ins.then_inc(m_ready, 1)
                pe.wait_ge(b_copied, 4)
                for w in (1, 0):
                    for j in range(DC):
                        col = 2 * ((1 - w) * DC + j)
                        for e in range(DC):
                            for a in range(2):
                                pe.matmul(ps[:, 4, col:col + 2], wT[a][w][e][:, j * P:(j + 1) * P], bhl[:, 1 - w, e],
                                          start=e == 0 and a == 0, stop=e == DC - 1 and a == 1)
                for e in range(DC):
                    ins = pe.matmul(ps[:, 4, 4 * DC:4 * DC + 1], T["ones"][:], prod[:, e:e + 1], start=e == 0, stop=e == DC - 1)
                ins.then_inc(cols_ready, 1)
                for t in range(NT):
                    pe.wait_ge(xn_ready, t + 1)
                    if t >= 2:
                        pe.wait_ge(x_lo, t - 1)
                    for d in range(DC):
                        ins = pe.transpose(ps[:, t % 2, d * P:(d + 1) * P], xn[:, t, d * P:(d + 1) * P], ident[:])
                    ins.then_inc(x_turned, 1)
                pe.wait_ge(m_lo, DC)
                for i in range(2 * DC):
                    half, j = divmod(i, DC)
                    if j == 0:
                        pe.wait_ge(x_lo, (half + 1) * QT)
                    if i >= 2:
                        pe.wait_ge(g_lo, i - 1)
                    if i == 3:
                        pe.wait_ge(red_ready, QT)
                        for t in range(QT):
                            ins = pe.matmul(ps[:, 7, 0:NB], T["ones"][:], red[:, t], start=t == 0, stop=t == QT - 1)
                        ins.then_inc(any_ready, 1)
                    M, xT, n = (Mhi, Mlo), (xnThi, xnTlo), 0
                    for d in range(DC):
                        for a, b in halves:
                            ins = pe.matmul(ps[:, 5 + i % 2], M[a][:, d, j * P:(j + 1) * P],
                                            xT[b][:, d, half * 512:half * 512 + 512], start=n == 0, stop=n == 3 * DC - 1)
                            n += 1
                    ins.then_inc(g_ready, 1)
                pe.wait_ge(chl_ready, 1)
                for t in range(NT):
                    for d in range(DC):
                        for a, h in enumerate((xnThi, xnTlo)):
                            ins = pe.matmul(ps[:, 4, 64 + 2 * t:66 + 2 * t], h[:, d, t * P:(t + 1) * P], chl[:, d],
                                            start=d == 0 and a == 0, stop=d == DC - 1 and a == 1)
                ins.then_inc(c_ready, 1)


def cross_attention(nc, T, io):
    with ExitStack() as ctx:
        m = Mem(nc, ctx)
        ps, ident, ghi, glo, live = T["ps"], T["ident"], T["ghi"], T["glo"], T["live"]
        m_run, l_run, acc, c = T["m_run"], T["l_run"], T["acc"], T["c"]
        raw = m.sb("ctx_raw", [P, B, KC, D])
        chi = m.sb("ctx_hi", [P, B, KC, D], F32R)
        clo = m.sb("ctx_lo", [P, B, KC, D], F32R)
        cThi = m.sb("ctxT_hi", [P, B, DC, KB], F32R)
        cTlo = m.sb("ctxT_lo", [P, B, DC, KB], F32R)
        mask = m.sb("mask_block", [P, QT, KB], U8)
        bias = m.sb("mask_bias", [P, QT, KB])
        p = m.sb("probs", [P, 2, KB])
        pThi = m.sb("probsT_hi", [P, 2, KB], F32R)
        pTlo = m.sb("probsT_lo", [P, 2, KB], F32R)
        rmax, mnew, nb, dm = (m.sb(n, [P, NT]) for n in ("rmax", "mnew", "nb", "dm"))
        corr, rsum = m.sb("corr", [P, NT]), m.sb("rsum", [P, NT])

        ctx_in = [m.sem(f"ctx_in{s}") for s in range(B)]
        turned = [m.sem(f"ctx_turned{s}") for s in range(B)]
        split = [m.sem(f"ctx_split{s}") for s in range(B)]
        mblk_in, bias_ready = m.sem("mblk_in"), m.sem("bias_ready")
        thi_ready, tlo_ready = m.sem("ctxT_hi_ready"), m.sem("ctxT_lo_ready")
        score_ready, score_read = m.sem("score_ready"), m.sem("score_read")
        state_set = m.sem("state_set")
        m_step, nb_ready = m.sem("m_step"), m.sem("nb_ready")
        p_ready, corr_ready = m.sem("p_ready"), m.sem("corr_ready")
        pt_ready, pthi_ready, ptlo_ready = m.sem("pt_ready"), m.sem("pt_hi_ready"), m.sem("pt_lo_ready")
        pv_ready, acc_done, l_done = m.sem("pv_ready"), m.sem("acc_done"), m.sem("l_done")
        SCORE, PT, PV, TURN = 0, 2, 4, 6

        def taken(eng, step):
            count = eng.value_load(live[0:1, NB:NB + 1], min_val=0, max_val=NB)
            with eng.Fori(1, NB + 1) as r:
                with eng.If(count > r - 1):
                    step(r)
                with eng.Else():
                    pass

        with nc.Block() as block:

            @block.sync
            def _(sp):
                for s in range(B):
                    sp.sem_inc(ctx_in[s], 16)
                sp.sem_inc(mblk_in, 16)
                context = io["ctx"].rearrange("s (b k p) d -> s b p k d", k=KC, p=P)
                masks = io["mask"].rearrange("(t p) (b k) -> b p t k", p=P, k=KB)

                def load(r):
                    b = sp.value_load(live[0:1, bass.ds(r - 1, 1)], min_val=0, max_val=NB - 1)
                    for s in range(B):
                        sp.wait_ge(turned[s], r * DC)
                        apart(sp, T["waited"])
                        sp.wait_ge(split[s], r * 2)
                        apart(sp, T["waited"])
                        sp.dma_start(raw[:, s], context[s, b]).then_inc(ctx_in[s], 16)
                        if s == 0:
                            sp.wait_ge(bias_ready, r)
                            apart(sp, T["waited"])
                            sp.dma_start(mask[:], masks[b]).then_inc(mblk_in, 16)

                taken(sp, load)

            @block.gpsimd
            def _(pool):
                for s in range(B):
                    pool.sem_inc(split[s], 2)
                pool.sem_inc(bias_ready, 1)
                pool.memset(m_run[:], -BIG).then_inc(state_set, 1)
                pool.memset(l_run[:], 0.0).then_inc(state_set, 1)
                pool.memset(acc[:], 0.0).then_inc(state_set, 1)

                def step(r):
                    pool.wait_ge(mblk_in, r * 16 + 16)
                    pool.wait_ge(score_read, r * NT)
                    apart(pool, T["waited"])
                    pool.tensor_scalar(bias[:], mask[:], BIG, -BIG, ALU.mult, ALU.add).then_inc(bias_ready, 1)
                    for s in range(B):
                        pool.wait_ge(ctx_in[s], r * 16 + 16)
                        pool.wait_ge(pv_ready, r * NT)
                        apart(pool, T["waited"])
                        pool.tensor_copy(chi[:, s], raw[:, s]).then_inc(split[s], 1)
                        pool.wait_ge(split[s], r * 2 + 1)
                        pool.tensor_tensor(clo[:, s], raw[:, s], chi[:, s].bitcast(F32),
                                           ALU.subtract).then_inc(split[s], 1)

                taken(pool, step)

            @block.tensor
            def _(pe):
                for s in range(B):
                    pe.sem_inc(turned[s], DC)
                pe.sem_inc(score_ready, NT)
                pe.sem_inc(pt_ready, NT)
                pe.sem_inc(pv_ready, NT)

                def turn(r, s, g):
                    n = s * DC + g
                    pe.wait_ge(ctx_in[s], r * 16 + 16)
                    pe.wait_ge(tlo_ready, r * B * DC + n - 1)
                    for k in range(KC):
                        ins = pe.transpose(ps[:, TURN + g % 2, k * P:(k + 1) * P], raw[:, s, k, g * P:(g + 1) * P], ident[:])
                    ins.then_inc(turned[s], 1)

                def score(r, u):
                    s = u // QT
                    if u % QT == 0:
                        pe.wait_ge(tlo_ready, r * B * DC + (s + 1) * DC)
                    pe.wait_ge(score_read, r * NT + u - 1)
                    n = 0
                    for d in range(DC):
                        for a, b in ((ghi, cThi), (glo, cThi), (ghi, cTlo)):
                            ins = pe.matmul(ps[:, SCORE + u % 2], a[:, d, u * P:(u + 1) * P], b[:, s, d],
                                            start=n == 0, stop=n == 3 * DC - 1)
                            n += 1
                    ins.then_inc(score_ready, 1)

                def turn_probs(r, u):
                    pe.wait_ge(p_ready, r * NT + u + 1)
                    pe.wait_ge(ptlo_ready, r * NT + u - 1)
                    for k in range(KC):
                        ins = pe.transpose(ps[:, PT + u % 2, k * P:(k + 1) * P], p[:, u % 2, k * P:(k + 1) * P], ident[:])
                    ins.then_inc(pt_ready, 1)

                def value(r, u):
                    s = u // QT
                    if u % QT == 0:
                        pe.wait_ge(split[s], r * 2 + 2)
                    pe.wait_ge(ptlo_ready, r * NT + u + 1)
                    pe.wait_ge(acc_done, r * NT + u - 1)
                    n = 0
                    for k in range(KC):
                        for a, b in ((pThi, chi), (pTlo, chi), (pThi, clo)):
                            ins = pe.matmul(ps[:, PV + u % 2], a[:, u % 2, k * P:(k + 1) * P], b[:, s, k],
                                            start=n == 0, stop=n == 3 * KC - 1)
                            n += 1
                    ins.then_inc(pv_ready, 1)

                def step(r):
                    for g in range(DC):
                        turn(r, 0, g)
                    for u in range(NT + 2):
                        if u < NT:
                            score(r, u)
                        if u in (1, 2):
                            turn(r, 1, 2 * u - 2)
                            turn(r, 1, 2 * u - 1)
                        if 1 <= u <= NT:
                            turn_probs(r, u - 1)
                        if u >= 2:
                            value(r, u - 2)

                taken(pe, step)

            @block.scalar
            def _(act):
                act.sem_inc(thi_ready, B * DC)
                act.sem_inc(p_ready, NT)
                act.sem_inc(corr_ready, NT)
                act.sem_inc(pthi_ready, NT)

                def context_hi(r, s, g):
                    n = s * DC + g
                    act.wait_ge(turned[s], r * DC + g + 1)
                    if g == 0:
                        act.wait_ge(score_ready, r * NT)
                    act.copy(cThi[:, s, g], ps[:, TURN + g % 2]).then_inc(thi_ready, 1)

                def probs(r, u):
                    act.wait_ge(nb_ready, r * 2 * NT + 2 * u + 2)
                    if u == 0:
                        act.wait_ge(acc_done, r * NT)
                        act.wait_ge(l_done, r * NT)
                    act.activation(p[:, u % 2], p[:, u % 2], ACT.Exp, bias=nb[:, u:u + 1], scale=1.0,
                                   accum_out=rsum[:, u:u + 1]).then_inc(p_ready, 1)
                    act.activation(corr[:, u:u + 1], dm[:, u:u + 1], ACT.Exp).then_inc(corr_ready, 1)

                def probs_hi(r, u):
                    act.wait_ge(pt_ready, r * NT + u + 1)
                    act.wait_ge(pv_ready, r * NT + u - 1)
                    act.copy(pThi[:, u % 2], ps[:, PT + u % 2]).then_inc(pthi_ready, 1)

                def step(r):
                    for g in range(DC):
                        context_hi(r, 0, g)
                    for u in range(NT + 1):
                        if u < NT:
                            probs(r, u)
                        if u in (1, 2):
                            context_hi(r, 1, 2 * u - 2)
                            context_hi(r, 1, 2 * u - 1)
                        if u >= 1:
                            probs_hi(r, u - 1)

                taken(act, step)

            @block.vector
            def _(dve):
                dve.wait_ge(state_set, 3)
                dve.sem_inc(tlo_ready, B * DC)
                dve.sem_inc(score_read, NT)
                dve.sem_inc(m_step, 2 * NT)
                dve.sem_inc(nb_ready, 2 * NT)
                dve.sem_inc(ptlo_ready, NT)
                dve.sem_inc(acc_done, NT)
                dve.sem_inc(l_done, NT)

                def context_lo(r, s, g):
                    dve.wait_ge(thi_ready, r * B * DC + s * DC + g + 1)
                    dve.tensor_tensor(cTlo[:, s, g], ps[:, TURN + g % 2], cThi[:, s, g].bitcast(F32),
                                      ALU.subtract).then_inc(tlo_ready, 1)

                def row_max(r, u):
                    if u == 0:
                        dve.wait_ge(bias_ready, r + 1)
                        dve.wait_ge(corr_ready, r * NT)
                    dve.wait_ge(score_ready, r * NT + u + 1)
                    dve.wait_ge(pt_ready, r * NT + u - 1)
                    apart(dve, T["waited"])
                    dve.tensor_tensor_reduce(out=p[:, u % 2], in0=ps[:, SCORE + u % 2], in1=bias[:, u % QT],
                                             scale=1.0, scalar=LOWEST, op0=ALU.add, op1=ALU.max,
                                             accum_out=rmax[:, u:u + 1]).then_inc(score_read, 1)
                    dve.wait_ge(score_read, r * NT + u + 1)
                    dve.scalar_tensor_tensor(out=mnew[:, u:u + 1], in0=rmax[:, u:u + 1], scalar=c[:, u:u + 1],
                                             in1=m_run[:, u:u + 1], op0=ALU.add, op1=ALU.max).then_inc(m_step, 1)
                    dve.wait_ge(m_step, r * 2 * NT + 2 * u + 1)
                    dve.tensor_tensor(nb[:, u:u + 1], c[:, u:u + 1], mnew[:, u:u + 1], ALU.subtract).then_inc(nb_ready, 1)
                    dve.tensor_tensor(dm[:, u:u + 1], m_run[:, u:u + 1], mnew[:, u:u + 1],
                                      ALU.subtract).then_inc(nb_ready, 1)
                    dve.wait_ge(nb_ready, r * 2 * NT + 2 * u + 2)
                    dve.tensor_copy(m_run[:, u:u + 1], mnew[:, u:u + 1]).then_inc(m_step, 1)

                def probs_lo(r, u):
                    dve.wait_ge(pthi_ready, r * NT + u + 1)
                    dve.tensor_tensor(pTlo[:, u % 2], ps[:, PT + u % 2], pThi[:, u % 2].bitcast(F32),
                                      ALU.subtract).then_inc(ptlo_ready, 1)

                def accumulate(r, u):
                    dve.wait_ge(corr_ready, r * NT + u + 1)
                    dve.wait_ge(p_ready, r * NT + u + 1)
                    dve.scalar_tensor_tensor(out=l_run[:, u:u + 1], in0=l_run[:, u:u + 1], scalar=corr[:, u:u + 1],
                                             in1=rsum[:, u:u + 1], op0=ALU.mult, op1=ALU.add).then_inc(l_done, 1)
                    dve.wait_ge(pv_ready, r * NT + u + 1)
                    dve.scalar_tensor_tensor(out=acc[:, u], in0=acc[:, u], scalar=corr[:, u:u + 1],
                                             in1=ps[:, PV + u % 2], op0=ALU.mult, op1=ALU.add).then_inc(acc_done, 1)

                def step(r):
                    dve.wait_ge(acc_done, r * NT)
                    dve.wait_ge(m_step, r * 2 * NT)
                    for g in range(DC):
                        context_lo(r, 0, g)
                    for u in range(NT + 2):
                        if u < NT:
                            row_max(r, u)
                        if u in (1, 2):
                            context_lo(r, 1, 2 * u - 2)
                            context_lo(r, 1, 2 * u - 1)
                        if 1 <= u <= NT:
                            probs_lo(r, u - 1)
                        if u >= 2:
                            accumulate(r, u - 2)

                taken(dve, step)


def latents(nc, T, io):
    with ExitStack() as ctx:
        m = Mem(nc, ctx)
        ps, x, ident, acc = T["ps"], T["x"], T["ident"], T["acc"]
        xn, xnT = T["o"], T["acc"]
        aThi, aTlo = m.sb("accT_hi", [P, 2, DC, P], F32R), m.sb("accT_lo", [P, 2, DC, P], F32R)
        bv = m.sb("bv_rows", [P, D])
        lhi, llo = m.sb("lat_hi", [P, 2, B * S], F32R), m.sb("lat_lo", [P, 2, B * S], F32R)
        whi = [m.sb(f"W_{n}_hi", [P, D], F32R) for n in ("uq", "uk", "uv")]
        wlo = [m.sb(f"W_{n}_lo", [P, D], F32R) for n in ("uq", "uk", "uv")]
        seen, lsum, linv, scale = (m.sb(n, [P, NT]) for n in ("seen", "lsum", "linv", "scale"))
        stats, mv = m.sb("stats2", [P, NT, 6]), m.sb("mv2", [P, NT, 2])
        varp, std, rstd = (m.sb(n, [P, NT]) for n in ("varp2", "std2", "rstd2"))

        bv_in, bv_added, dve_step = m.sem("bv_in"), m.sem("bv_added"), m.sem("c_dve_step")
        a_turned, a_hi, a_lo, v_ready, x_ready = (m.sem(n) for n in ("a_turned", "a_hi", "a_lo", "wv_ready", "x1_ready"))
        var_ready, std_ready, xn_ready = m.sem("var2_ready"), m.sem("std2_ready"), m.sem("xn2_ready")
        x_turned, x_copied = m.sem("x2_turned"), m.sem("x2_copied")
        w_split, l_ready, lhi_ready, llo_ready = (
            m.sem("w_split"), m.sem("lat_ready"), m.sem("lat_hi_ready"), m.sem("lat_lo_ready"))
        val_ready, val_copied = m.sem("val_ready"), m.sem("val_copied")
        qk_ready, qk_hi, qk_lo = m.sem("qk_ready"), m.sem("qk_hi"), m.sem("qk_lo")
        halves = ((0, 0), (1, 0), (0, 1))
        GROUPS = [(which, c, half) for half in range(2) for which in range(2) for c in range(DC)]

        def columns(c_row):
            return xnT[:].rearrange("p t d -> p (t d)").rearrange("p (c r) -> p c r", c=DC)[:, :, c_row * P:(c_row + 1) * P]

        with nc.Block() as block:

            @block.sync
            def _(sp):
                sp.dma_start(bv[:], io["bv"].rearrange("(a d) -> a d", a=1).to_broadcast([P, D])).then_inc(bv_in, 16)

            @block.gpsimd
            def _(pool):
                pool.wait_ge(bv_in, 16)
                pool.wait_ge(T["weights_in"], T["weights_total"])
                pool.tensor_tensor(x[:], x[:], bv[:].unsqueeze(1).to_broadcast([P, NT, D]), ALU.add).then_inc(bv_added, 1)
                for n, w in enumerate(("uq", "uk", "uv")):
                    pool.tensor_copy(whi[n][:], T[w][:]).then_inc(w_split, 1)
                    pool.wait_ge(w_split, 2 * n + 1)
                    pool.tensor_tensor(wlo[n][:], T[w][:], whi[n][:].bitcast(F32), ALU.subtract).then_inc(w_split, 1)

            @block.scalar
            def _(act):
                for t in range(NT):
                    act.wait_ge(a_turned, t + 1)
                    if t >= 2:
                        act.wait_ge(v_ready, t - 1)
                    act.copy(aThi[:, t % 2], ps[:, t % 2].rearrange("p (c r) -> p c r", c=DC)).then_inc(a_hi, 1)
                act.wait_ge(var_ready, 1)
                act.activation(std[:], varp[:], ACT.Sqrt).then_inc(std_ready, 1)
                for t in range(NT):
                    act.wait_ge(x_turned, t + 1)
                    act.copy(columns(t), ps[:, 4 + t % 2].rearrange("p (c r) -> p c r", c=DC)).then_inc(x_copied, 1)
                for i in range(4):
                    half, which = divmod(i, 2)
                    act.wait_ge(l_ready, i + 1)
                    act.copy(lhi[:, which, half * 512:half * 512 + 512], ps[:, 6 + i % 2]).then_inc(lhi_ready, 1)
                for n, (which, c, half) in enumerate(GROUPS):
                    act.wait_ge(qk_ready, n + 1)
                    act.copy(T["qkT"][which][0][:, c, half * 512:half * 512 + 512], ps[:, n % 4]).then_inc(qk_hi, 1)
                    if n % 2:
                        t = n // 2
                        act.wait_ge(val_ready, t + 1)
                        act.copy(T["v"][:, t], ps[:, 4 + t % 2]).then_inc(val_copied, 1)

            @block.vector
            def _(dve):
                link = chained(dve, dve_step)
                link(dve.tensor_scalar(seen[:], T["m_run"][:], -0.5 * BIG, None, ALU.is_gt))
                link(dve.tensor_tensor(lsum[:], T["l_run"][:], seen[:], ALU.mult))
                link(dve.reciprocal(linv[:], lsum[:]))
                link(dve.tensor_tensor(scale[:], linv[:], seen[:], ALU.mult))

                def acc_lo(t):
                    dve.wait_ge(a_hi, t + 1)
                    dve.tensor_tensor(aTlo[:, t % 2], ps[:, t % 2].rearrange("p (c r) -> p c r", c=DC),
                                      aThi[:, t % 2].bitcast(F32), ALU.subtract).then_inc(a_lo, 1)

                acc_lo(0)
                dve.wait_ge(bv_added, 1)
                for t in range(NT):
                    if t + 1 < NT:
                        acc_lo(t + 1)
                    dve.wait_ge(v_ready, t + 1)
                    dve.scalar_tensor_tensor(out=x[:, t], in0=ps[:, 2 + t % 2], scalar=scale[:, t:t + 1], in1=x[:, t],
                                             op0=ALU.mult, op1=ALU.add).then_inc(x_ready, 1)
                    dve.wait_ge(x_ready, t + 1)
                    dve.bn_stats(stats[:, t, :], x[:, t, :]).then_inc(dve_step, 1)
                dve.wait_ge(dve_step, 4 + NT)
                for t in range(NT):
                    ins = dve.bn_aggr(mv[:, t, :], stats[:, t, :])
                ins.then_inc(dve_step, 1)
                dve.wait_ge(dve_step, 5 + NT)
                dve.tensor_scalar(varp[:], mv[:, :, 1], EPS, None, ALU.add).then_inc(var_ready, 1)
                dve.wait_ge(std_ready, 1)
                dve.reciprocal(rstd[:], std[:]).then_inc(dve_step, 1)
                dve.wait_ge(dve_step, 6 + NT)
                for t in range(NT):
                    dve.tensor_scalar(xn[:, t], x[:, t], mv[:, t, 0:1], rstd[:, t:t + 1], ALU.subtract,
                                      ALU.mult).then_inc(xn_ready, 1)
                for i in range(4):
                    half, which = divmod(i, 2)
                    at = slice(half * 512, half * 512 + 512)
                    dve.wait_ge(lhi_ready, i + 1)
                    dve.tensor_tensor(llo[:, which, at], ps[:, 6 + i % 2], lhi[:, which, at].bitcast(F32),
                                      ALU.subtract).then_inc(llo_ready, 1)
                for n, (which, c, half) in enumerate(GROUPS):
                    at = slice(half * 512, half * 512 + 512)
                    dve.wait_ge(qk_hi, n + 1)
                    dve.tensor_tensor(T["qkT"][which][1][:, c, at], ps[:, n % 4], T["qkT"][which][0][:, c, at].bitcast(F32),
                                      ALU.subtract).then_inc(qk_lo, 1)

            @block.tensor
            def _(pe):
                def turn_acc(t):
                    if t >= 2:
                        pe.wait_ge(a_lo, t - 1)
                    for d in range(DC):
                        ins = pe.transpose(ps[:, t % 2, d * P:(d + 1) * P], acc[:, t, d * P:(d + 1) * P], ident[:])
                    ins.then_inc(a_turned, 1)

                turn_acc(0)
                for t in range(NT):
                    if t + 1 < NT:
                        turn_acc(t + 1)
                    pe.wait_ge(a_lo, t + 1)
                    if t >= 2:
                        pe.wait_ge(x_ready, t - 1)
                    aT, wv, n = (aThi, aTlo), (T["Wvhi"], T["Wvlo"]), 0
                    for d in range(DC):
                        for a, b in halves:
                            ins = pe.matmul(ps[:, 2 + t % 2], aT[a][:, t % 2, d], wv[b][:, d], start=n == 0,
                                            stop=n == 3 * DC - 1)
                            n += 1
                    ins.then_inc(v_ready, 1)
                for t in range(NT):
                    pe.wait_ge(xn_ready, t + 1)
                    if t >= 2:
                        pe.wait_ge(x_copied, t - 1)
                    for d in range(DC):
                        ins = pe.transpose(ps[:, 4 + t % 2, d * P:(d + 1) * P], xn[:, t, d * P:(d + 1) * P], ident[:])
                    ins.then_inc(x_turned, 1)
                pe.wait_ge(T["weights_in"], T["weights_total"])
                for i in range(4):
                    half, which = divmod(i, 2)
                    pe.wait_ge(x_copied, (half + 1) * QT)
                    if i >= 2:
                        pe.wait_ge(llo_ready, i - 1)
                    for d in range(DC):
                        at = slice(d * B * S + half * 512, d * B * S + half * 512 + 512)
                        ins = pe.matmul(ps[:, 6 + i % 2], T["dqkv"][:, which, d], xnT[:].rearrange("p t d -> p (t d)")[:, at],
                                        start=d == 0, stop=d == DC - 1)
                    ins.then_inc(l_ready, 1)
                pe.wait_ge(w_split, 6)
                l = (lhi, llo)
                for n, (which, c, half) in enumerate(GROUPS):
                    pe.wait_ge(llo_ready, 2 * half + which + 1)
                    if n >= 4:
                        pe.wait_ge(qk_lo, n - 3)
                    for k, (a, b) in enumerate(halves):
                        ins = pe.matmul(ps[:, n % 4], (whi, wlo)[a][which][:, c * P:(c + 1) * P],
                                        l[b][:, which, half * 512:half * 512 + 512], start=k == 0, stop=k == 2)
                    ins.then_inc(qk_ready, 1)
                    if n % 2:
                        t = n // 2
                        pe.wait_ge(llo_ready, 2 + 2 * (t // QT))
                        if t >= 2:
                            pe.wait_ge(val_copied, t - 1)
                        for k, (a, b) in enumerate(halves):
                            ins = pe.matmul(ps[:, 4 + t % 2], l[a][:, 1, t * P:(t + 1) * P], (whi, wlo)[b][2][:],
                                            start=k == 0, stop=k == 2)
                        ins.then_inc(val_ready, 1)


def heads(nc, T, io):
    HC = P // DK
    STEPS = NH // HC
    SC = float(DK) ** -0.5
    AHEAD = 2
    UNITS = [(b, g) for b in range(B) for g in range(3)]
    TILES = ((0,), (1,), (2, 3))
    NU = len(UNITS)
    LOADS = 6 * 16
    with ExitStack() as ctx:
        m = Mem(nc, ctx)
        ps, ident = T["ps"], T["ident"]
        q3 = [m.sb(f"q3_{j}", [3 * DK + 2, B * S], F32R) for j in range(HC)]
        k3 = [m.sb(f"k3_{j}", [3 * DK + 2, B * S], F32R) for j in range(HC)]
        closed = T["place"][:, 0:2]
        closed_r, ident_r = m.sb("closed_r", [P, 2, P], F32R), m.sb("ident_r", [P, P], F32R)
        pT = [[m.sb(f"head_probsT{b}{g}", [P, (512, 384, 384)[g]]) for g in range(3)] for b in range(B)]
        rmax = m.sb("head_max", [P, 2, NT])
        mrow = [[m.sb(f"max_row_{h}{j}", [NT, P], F32R) for h in ("hi", "lo")] for j in range(2)]
        vh = m.sb("head_v", [P, 2, NT, DK + 1])
        wraw, same = T["Wo"], m.sb("same", [P, HC * NT])
        oT = T["acc"][:].rearrange("p t d -> p (t d)").rearrange("p (c r) -> p c r", c=DC)
        sums_of = T["o"][:].rearrange("p t d -> p (t d)").rearrange("p (c r) -> p c r", c=DC)

        pool_step, const_set, wo_in = m.sem("d_pool_step"), m.sem("head_consts"), m.sem("wo_in")
        ones_set, sums_in = m.sem("k_ones_set"), m.sem("sums_in")
        qk_in = [m.sem(f"qk_in{j}") for j in range(HC)]
        max_in = [m.sem(f"max_in{j}") for j in range(HC)]
        row_ready, row_read, max_turned, max_split = (m.sem(n) for n in ("row_ready", "row_read", "max_turned", "max_split"))
        unit_ready, p_ready, v_set = m.sem("unit_ready"), m.sem("hp_ready"), m.sem("head_v_set")
        pv_ready, o_copied, l_read = m.sem("hpv_ready"), m.sem("ho_copied"), m.sem("hl_read")
        ROW, UNIT, TURN, PV = 0, 2, 5, 6

        def chunk(r, k):
            return bass.ds(r + (k // HC - 1), 1)

        def steps(eng, body):
            with eng.Fori(1, STEPS) as r:
                body(r, 2 * HC)
            body(STEPS, HC)

        with nc.Block() as block:

            @block.sync
            def _(sp):
                order = ((0, 0, 1), (0, 1, 0))

                def load(r, k):
                    j = k % HC
                    sp.wait_ge(unit_ready, r * (HC * NU) + (k - HC + 1) * NU)
                    apart(sp, T["waited"])
                    for which in range(2):
                        for i in range(3):
                            src = T["qkT"][which][order[which][i]][j * DK:(j + 1) * DK, chunk(r, k)]
                            sp.dma_start((q3, k3)[which][j][i * DK:(i + 1) * DK].bitcast(F32),
                                         src.rearrange("p a b -> p (a b)").bitcast(F32)).then_inc(qk_in[j], 16)

                def max_rows(r, k):
                    j = k % HC
                    sp.wait_ge(max_split, r * (2 * HC) + 2 * (k + 1))
                    apart(sp, T["waited"])
                    for h in range(2):
                        sp.dma_start(q3[j][3 * DK + h:3 * DK + h + 1].bitcast(F32), mrow[k % 2][h][:].bitcast(F32)).then_inc(max_in[j], 16)

                for k in range(AHEAD + 1):
                    load(1, k)
                sp.dma_start(wraw[:], io["Wo"].rearrange("(c p) e -> p c e", p=P)).then_inc(wo_in, 16)
                for k in range(AHEAD):
                    max_rows(1, k)

                def body(r, last):
                    for k in range(HC):
                        if k + AHEAD + 1 < last:
                            load(r, k + AHEAD + 1)
                        if k + AHEAD < last:
                            max_rows(r, k + AHEAD)

                steps(sp, body)
                for c in range(STEPS):
                    for k in range(HC):
                        sp.wait_ge(l_read, (c + 1) * (B * HC) + (k + 1) * B)
                        at = c * HC * NT + k * NT
                        sp.dma_start(T["sums"][at:at + NT], sums_of[k * DK:k * DK + 1, c]).then_inc(sums_in, 16)
                sp.wait_ge(sums_in, 16 * NH)

            @block.gpsimd
            def _(pool):
                link = chained(pool, pool_step)
                pool.sem_inc(v_set, HC)
                link(pool.memset(closed, 0.0))
                for i, sign in enumerate((1, -1)):
                    link(pool.affine_select(out=closed[:, i], in_=closed[:, i], compare_op=ALU.is_ge, fill=-BIG, base=0,
                                            pattern=[[sign, P]], channel_multiplier=-sign))
                pool.tensor_copy(closed_r[:], closed[:]).then_inc(const_set, 1)
                link(pool.tensor_copy(ident_r[:], ident[:]))
                pool.memset(vh[:, :, :, DK:DK + 1], 1.0).then_inc(const_set, 1)

                def value(r, k):
                    pool.wait_ge(pv_ready, r * (HC * NU) + (k - 1) * NU)
                    apart(pool, T["waited"])
                    at = r * P + (k * DK - P)
                    pool.tensor_copy(vh[:, k % 2, :, 0:DK], T["v"][:, :, bass.ds(at, DK)]).then_inc(v_set, 1)

                for k in range(AHEAD):
                    value(1, k)
                pool.wait_ge(v_set, HC + AHEAD)
                pool.wait_ge(wo_in, 16)
                link(pool.tensor_copy(T["Wohi"][:], wraw[:]))
                link(pool.tensor_tensor(T["Wolo"][:], wraw[:], T["Wohi"][:].bitcast(F32), ALU.subtract))
                link(pool.tensor_copy(same[:], ident[:, 0:HC * NT]))
                for c in range(1, STEPS):
                    link(pool.tensor_tensor(same[:], same[:], ident[:, c * HC * NT:(c + 1) * HC * NT], ALU.add))
                link(pool.tensor_copy(T["place"][:].rearrange("p t (k e) -> p t k e", e=DK),
                                      same[:].rearrange("p (k t) -> p t k", t=NT).unsqueeze(3).to_broadcast([P, NT, HC, DK])))

                def body(r, last):
                    for k in range(HC):
                        if k + AHEAD < last:
                            value(r, k + AHEAD)

                steps(pool, body)

            @block.tensor
            def _(pe):
                pe.sem_inc(row_ready, HC * NT)
                pe.sem_inc(max_turned, HC)
                pe.sem_inc(unit_ready, HC * NU)
                pe.sem_inc(pv_ready, HC * NU)
                pe.wait_ge(const_set, 2)

                def row(r, k, t):
                    j, b, q = k % HC, t // QT, t % QT
                    if t == 0:
                        pe.wait_ge(qk_in[j], r * LOADS + (k // HC) * LOADS)
                    pe.wait_ge(row_read, r * (HC * NT) + (k * NT + t - 1))
                    bank = ps[:, ROW + t % 2]
                    pe.matmul(bank[:, 0:(q + 1) * P], q3[j][0:3 * DK, t * P:(t + 1) * P],
                              k3[j][0:3 * DK, b * S:b * S + (q + 1) * P], start=True, stop=False)
                    pe.matmul(bank[:, q * P:(q + 1) * P], closed_r[:, 0], ident_r[:], start=False,
                              stop=True).then_inc(row_ready, 1)

                def turn_max(r, k):
                    pe.wait_ge(row_read, r * (HC * NT) + (k + 1) * NT)
                    pe.wait_ge(max_split, r * (2 * HC) + 2 * k)
                    pe.transpose(ps[0:NT, TURN, 0:P], rmax[:, k % 2], ident[:]).then_inc(max_turned, 1)

                def unit(r, k, v):
                    k, v = k + v // NU, v % NU
                    j, (b, g) = k % HC, UNITS[v]
                    if v == 0:
                        pe.wait_ge(max_in[j], r * 32 + (k // HC) * 32)
                    pe.wait_ge(p_ready, r * (HC * NU) + (k * NU + v - 2))
                    col = 0
                    for kt in TILES[g]:
                        n, k0 = S - kt * P, b * S + kt * P
                        pe.matmul(ps[:, UNIT + g, col:col + n], k3[j][:, k0:k0 + P], q3[j][:, k0:k0 + n], start=True, stop=False)
                        ins = pe.matmul(ps[:, UNIT + g, col:col + P], closed_r[:, 1], ident_r[:], start=False, stop=True)
                        col += n
                    ins.then_inc(unit_ready, 1)

                def value(r, k, v):
                    b, g = UNITS[v]
                    pe.wait_ge(p_ready, r * (HC * NU) + (k * NU + v + 1))
                    if g == 0:
                        if b == 0:
                            pe.wait_ge(v_set, r * HC + (k + 1))
                        pe.wait_ge(o_copied, r * (B * HC) + (k - 1) * B + b + 1)
                        pe.wait_ge(l_read, r * (B * HC) + (k - 1) * B + b + 1)
                    col = 0
                    for kt in TILES[g]:
                        n = S - kt * P
                        ins = pe.matmul(ps[0:DK + 1, PV + b, kt * P:S], vh[:, k % 2, b * QT + kt], pT[b][g][:, col:col + n],
                                        start=kt == 0, stop=kt == QT - 1)
                        col += n
                    ins.then_inc(pv_ready, 1)

                for k in range(AHEAD):
                    for t in range(NT):
                        row(1, k, t)
                    turn_max(1, k)
                pe.wait_ge(ones_set, HC)
                unit(1, 0, 0)
                unit(1, 0, 1)

                def body(r, last):
                    for k in range(HC):
                        for v in range(NU):
                            if k * NU + v + 2 < last * NU and (k < HC - 1 or v + 2 < NU or last > HC):
                                unit(r, k, v + 2)
                            if k + AHEAD < last:
                                for t in ((0, 1), (2, 3), (4, 5), (6,), (7,), ())[v]:
                                    row(r, k + AHEAD, t)
                            value(r, k, v)
                        if k + AHEAD < last:
                            turn_max(r, k + AHEAD)

                steps(pe, body)

            @block.scalar
            def _(act):
                act.sem_inc(p_ready, HC * NU)
                act.sem_inc(o_copied, HC * B)

                def probs(r, k, v):
                    k, v = k + v // NU, v % NU
                    b, g = UNITS[v]
                    n = sum(S - kt * P for kt in TILES[g])
                    act.wait_ge(unit_ready, r * (HC * NU) + (k * NU + v + 1))
                    act.wait_ge(pv_ready, r * (HC * NU) + ((k - 1) * NU + v + 1))
                    act.activation(pT[b][g][:, 0:n], ps[:, UNIT + g, 0:n], ACT.Exp, scale=SC).then_inc(p_ready, 1)

                def output(r, k, b):
                    act.wait_ge(pv_ready, r * (HC * NU) + (k * NU + (b + 1) * 3))
                    rows = slice(k * DK, (k + 1) * DK)
                    act.copy(oT[rows, chunk(r, k), b * S:(b + 1) * S], ps[0:DK, PV + b].unsqueeze(1)).then_inc(o_copied, 1)

                for j in range(HC):
                    act.copy(k3[j][3 * DK:3 * DK + 2].rearrange("a (t p) -> a t p", p=P),
                             T["ones"][3 * DK:3 * DK + 2].unsqueeze(1).to_broadcast([2, NT, P])).then_inc(ones_set, 1)
                probs(1, 0, 0)
                probs(1, 0, 1)

                def body(r, last):
                    for k in range(HC):
                        for v in range(NU):
                            if k < HC - 1 or v + 2 < NU or last > HC:
                                probs(r, k, v + 2)
                            if v == 3:
                                output(r, k, 0)
                        output(r, k, 1)

                steps(act, body)

            @block.vector
            def _(dve):
                dve.sem_inc(row_read, HC * NT)
                dve.sem_inc(max_split, 2 * HC)
                dve.sem_inc(l_read, HC * B)

                def row_max(r, k, t):
                    n = (t % QT + 1) * P
                    dve.wait_ge(row_ready, r * (HC * NT) + (k * NT + t + 1))
                    dve.tensor_reduce(rmax[:, k % 2, t:t + 1], ps[:, ROW + t % 2, 0:n], AX.X, ALU.max).then_inc(row_read, 1)

                def split_max(r, k):
                    j = k % HC
                    dve.wait_ge(max_turned, r * HC + (k + 1))
                    dve.tensor_scalar(mrow[k % 2][0][:], ps[0:NT, TURN, 0:P], -1.0, None, ALU.mult).then_inc(max_split, 1)
                    dve.wait_ge(max_split, r * (2 * HC) + 2 * k + 1)
                    dve.scalar_tensor_tensor(out=mrow[k % 2][1][:], in0=ps[0:NT, TURN, 0:P], scalar=-1.0,
                                             in1=mrow[k % 2][0][:].bitcast(F32), op0=ALU.mult, op1=ALU.subtract).then_inc(max_split, 1)

                def sums(r, k, b):
                    dve.wait_ge(pv_ready, r * (HC * NU) + (k * NU + (b + 1) * 3))
                    dve.tensor_copy(sums_of[k * DK:k * DK + 1, chunk(r, k), b * S:(b + 1) * S],
                                    ps[DK:DK + 1, PV + b].unsqueeze(1)).then_inc(l_read, 1)

                for k in range(AHEAD):
                    for t in range(NT):
                        row_max(1, k, t)
                    split_max(1, k)

                def body(r, last):
                    for k in range(HC):
                        for t in range(NT):
                            if k + AHEAD < last:
                                row_max(r, k + AHEAD, t)
                            if t == 5:
                                sums(r, k, 0)
                        sums(r, k, 1)
                        if k + AHEAD < last:
                            split_max(r, k + AHEAD)

                steps(dve, body)


def heads_out(nc, T):
    with ExitStack() as ctx:
        m = Mem(nc, ctx)
        ps, x, xn = T["ps"], T["x"], T["xn3"]
        oT = T["acc"][:].rearrange("p t d -> p (t d)").rearrange("p (c r) -> p c r", c=DC)
        inv, chunked = m.sb("sums_inv", [P, P]), m.sb("sums_inv_chunked", [P, DC, P])
        oThi, oTlo = m.sb("oT_hi", [P, 2, DC, P], F32R), m.sb("oT_lo", [P, 2, DC, P], F32R)
        stats, mv = m.sb("stats3", [P, NT, 6]), m.sb("mv3", [P, NT, 2])
        varp, std, rstd = (m.sb(n, [P, NT]) for n in ("varp3", "std3", "rstd3"))
        o_hi, o_lo = m.sem("o_hi"), m.sem("o_lo")
        inv_ready, spread, o_scaled = m.sem("inv_ready"), m.sem("inv_spread"), m.sem("o_scaled")
        out_ready, x_ready, dve_step = m.sem("wo_ready"), m.sem("x2_ready"), m.sem("o_dve_step")
        var_ready, std_ready = m.sem("var3_ready"), m.sem("std3_ready")

        def tile(t):
            return slice(t * P, (t + 1) * P)

        with nc.Block() as block:

            @block.scalar
            def _(act):
                for t in range(NT):
                    act.wait_ge(o_scaled, t + 1)
                    if t >= 2:
                        act.wait_ge(out_ready, t - 1)
                    act.copy(oThi[:, t % 2], oT[:, :, tile(t)]).then_inc(o_hi, 1)
                act.wait_ge(var_ready, 1)
                act.activation(std[:], varp[:], ACT.Sqrt).then_inc(std_ready, 1)

            @block.vector
            def _(dve):
                dve.memset(chunked[:], 0.0).then_inc(inv_ready, 1)
                dve.reciprocal(inv[:], T["sums"][:]).then_inc(inv_ready, 1)
                dve.wait_ge(inv_ready, 2)
                HR = P // DC
                for c in range(DC):
                    dve.tensor_copy(chunked[c * HR:(c + 1) * HR, c], inv[c * HR:(c + 1) * HR]).then_inc(inv_ready, 1)

                def scaled(t):
                    dve.wait_ge(spread, t + 1)
                    dve.tensor_tensor(oT[:, :, tile(t)], oT[:, :, tile(t)], ps[:, 4 + t % 4].rearrange("p (c r) -> p c r", c=DC),
                                      ALU.mult).then_inc(o_scaled, 1)

                def turned_lo(t):
                    dve.wait_ge(o_hi, t + 1)
                    dve.tensor_tensor(oTlo[:, t % 2], oT[:, :, tile(t)], oThi[:, t % 2].bitcast(F32),
                                      ALU.subtract).then_inc(o_lo, 1)

                scaled(0)
                scaled(1)
                turned_lo(0)
                for t in range(NT):
                    if t + 2 < NT:
                        scaled(t + 2)
                    if t + 1 < NT:
                        turned_lo(t + 1)
                    dve.wait_ge(out_ready, t + 1)
                    dve.tensor_tensor(x[:, t], ps[:, 2 + t % 2], x[:, t], ALU.add).then_inc(x_ready, 1)
                    dve.wait_ge(x_ready, t + 1)
                    dve.bn_stats(stats[:, t, :], x[:, t, :]).then_inc(dve_step, 1)
                dve.wait_ge(dve_step, NT)
                for t in range(NT):
                    ins = dve.bn_aggr(mv[:, t, :], stats[:, t, :])
                ins.then_inc(dve_step, 1)
                dve.wait_ge(dve_step, NT + 1)
                dve.tensor_scalar(varp[:], mv[:, :, 1], EPS, None, ALU.add).then_inc(var_ready, 1)
                dve.wait_ge(std_ready, 1)
                dve.reciprocal(rstd[:], std[:]).then_inc(dve_step, 1)
                dve.wait_ge(dve_step, NT + 2)
                for t in range(NT):
                    ins = dve.tensor_scalar(xn[:, t], x[:, t], mv[:, t, 0:1], rstd[:, t:t + 1], ALU.subtract, ALU.mult)
                ins.then_inc(dve_step, 1)

            @block.tensor
            def _(pe):
                def spread_inv(t):
                    if t >= 4:
                        pe.wait_ge(o_scaled, t - 3)
                    pe.matmul(ps[:, 4 + t % 4], T["place"][:, t], chunked[:].rearrange("p c r -> p (c r)"), start=True,
                              stop=True).then_inc(spread, 1)

                pe.wait_ge(inv_ready, 2 + DC)
                for t in range(3):
                    spread_inv(t)
                for t in range(NT):
                    if t + 3 < NT:
                        spread_inv(t + 3)
                    pe.wait_ge(o_lo, t + 1)
                    if t >= 2:
                        pe.wait_ge(x_ready, t - 1)
                    o, wo, n = (oThi, oTlo), (T["Wohi"], T["Wolo"]), 0
                    for d in range(DC):
                        for a, b in ((0, 0), (1, 0), (0, 1)):
                            ins = pe.matmul(ps[:, 2 + t % 2], o[a][:, t % 2, d], wo[b][:, d], start=n == 0,
                                            stop=n == 3 * DC - 1)
                            n += 1
                    ins.then_inc(out_ready, 1)


def experts(nc, T, io):
    Q3 = 3 * H
    with ExitStack() as ctx:
        m = Mem(nc, ctx)
        ps, x, ident, w, y = T["ps"], T["x"], T["ident"], T["w"], T["y"]
        xn, xnT = T["xn3"], m.sb("xn3T", [P, DC, B * S])
        raw, oraw = m.sb("expert_raw", [P, 2, DC, 3, H]), m.sb("expert_out_raw", [P, 2, D])
        whi, wlo = m.sb("expert_hi", [P, 2, DC, Q3], F32R), m.sb("expert_lo", [P, 2, DC, Q3], F32R)
        square, sim, simsq = m.sb("square", [P, D]), m.sb("sim", [P, DC, E]), m.sb("simsq", [P, DC, E])
        gates, egate, sig, norm_e, inv_e = (m.sb(n, [P, E]) for n in ("gates", "egate", "sig", "norm_e", "inv_e"))
        rowsq, norm_n, inv_n = (m.sb(n, [P, NT]) for n in ("rowsq", "norm_n", "inv_n"))
        rev_i, rev = m.sb("rev_i", [P, E], I32), m.sb("rev", [P, E])
        L, L2, key, sel1, sel2, put, on, g, ex = (m.sb(n, [P, NT, E]) for n in (
            "logits", "logits2", "key", "sel1", "sel2", "put", "on", "gated", "gate_exp"))
        top, kmax, idle, gmax, gsum, ginv = (m.sb(n, [P, NT]) for n in ("top", "kmax", "idle", "gmax", "gsum", "ginv"))

        g_in, rev_set, dve_step = m.sem("gate_in"), m.sem("rev_set"), m.sem("e_dve_step")
        sq_ready = m.sem("sq_ready")
        turned, hi_ready, lo_ready, f_ready = m.sem("xn3_turned"), m.sem("xn3_hi"), m.sem("xn3_lo"), m.sem("xn3_f32")
        simsq_ready, colsq_ready, logits_ready = m.sem("simsq_ready"), m.sem("colsq_ready"), m.sem("logits_ready")
        norm_ready, logits_read, e_ready, x_asked, x_ready = (m.sem(n) for n in (
            "norm_ready", "logits_read", "egate_ready", "gexp_asked", "gexp_ready"))
        raw_in = [m.sem(f"expert_in{j}") for j in range(2)]
        split = [m.sem(f"expert_split{j}") for j in range(2)]
        y_ready, y_added = m.sem("y_ready"), m.sem("y_added")
        U = 2 * NT

        def rows(a):
            return a[:].unsqueeze(2).to_broadcast([P, NT, E])

        def cols(a):
            return a[:].unsqueeze(1).to_broadcast([P, NT, E])

        with nc.Block() as block:

            @block.sync
            def _(sp):
                sp.dma_start(sim[:], io["sim"].rearrange("(c p) e -> p c e", p=P)).then_inc(g_in, 16)
                sp.dma_start(gates[:], io["gates"].rearrange("(a e) -> a e", a=1).to_broadcast([P, E])).then_inc(g_in, 16)
                for j in range(2):
                    sp.sem_inc(split[j], 4)
                qkv = [io[n].rearrange("e (c p) h -> e p c h", p=P) for n in ("qp", "kp", "vp")]
                with sp.Fori(1, E // 2 + 1) as r:
                    for j in range(2):
                        e = r * 2 + (j - 2)
                        sp.wait_ge(split[j], r * 4)
                        apart(sp, T["waited"])
                        for n in range(3):
                            sp.dma_start(raw[:, j, :, n], qkv[n][e]).then_inc(raw_in[j], 16)
                        sp.dma_start(oraw[:, j], io["op"][e]).then_inc(raw_in[j], 16)

            @block.gpsimd
            def _(pool):
                pool.iota(rev_i[:], pattern=[[-1, E]], base=E, channel_multiplier=0).then_inc(rev_set, 1)
                pool.wait_ge(rev_set, 1)
                pool.tensor_copy(rev[:], rev_i[:]).then_inc(rev_set, 1)
                pool.memset(y[:], 0.0).then_inc(rev_set, 1)
                with pool.Fori(1, E // 2 + 1) as r:
                    for j in range(2):
                        e = r * 2 + (j - 2)
                        pool.wait_ge(raw_in[j], r * 64)
                        pool.wait_ge(y_ready, r * U + (j * NT - NT))
                        apart(pool, T["waited"])
                        raw_j = raw[:, j].rearrange("p c n h -> p c (n h)")
                        pool.tensor_copy(whi[:, j], raw_j).then_inc(split[j], 1)
                        pool.wait_ge(split[j], r * 4 + 1)
                        pool.tensor_tensor(wlo[:, j], raw_j, whi[:, j].bitcast(F32), ALU.subtract).then_inc(split[j], 1)
                        pool.tensor_copy(T["ohi"][:, bass.ds(e, 1)], oraw[:, j:j + 1]).then_inc(split[j], 1)
                        pool.wait_ge(split[j], r * 4 + 3)
                        pool.tensor_tensor(T["olo"][:, bass.ds(e, 1)], oraw[:, j:j + 1],
                                           T["ohi"][:, bass.ds(e, 1)].bitcast(F32), ALU.subtract).then_inc(split[j], 1)

            @block.scalar
            def _(act):
                for t in range(NT):
                    act.wait_ge(turned, t + 1)
                    tile = slice(t * P, (t + 1) * P)
                    src = ps[:, t % 2].rearrange("p (c r) -> p c r", c=DC)
                    act.copy(T["xnhi"][:, :, tile], src).then_inc(hi_ready, 1)
                    act.copy(xnT[:, :, tile], src).then_inc(f_ready, 1)
                for t in range(NT):
                    if t >= 1:
                        act.wait_ge(sq_ready, t)
                    act.activation(square[:], xn[:, t], ACT.Square, accum_out=rowsq[:, t:t + 1]).then_inc(sq_ready, 1)
                act.wait_ge(sq_ready, NT)
                act.activation(norm_n[:], rowsq[:], ACT.Sqrt).then_inc(norm_ready, 1)
                act.wait_ge(colsq_ready, 1)
                act.activation(norm_e[:], ps[:, 3, 0:E], ACT.Sqrt).then_inc(norm_ready, 1)
                act.wait_ge(g_in, 32)
                act.activation(egate[:], gates[:], ACT.Exp, scale=-1.0).then_inc(e_ready, 1)
                act.wait_ge(x_asked, 1)
                act.activation(ex[:], key[:], ACT.Exp).then_inc(x_ready, 1)

            @block.vector
            def _(dve):
                link = chained(dve, dve_step)
                dve.wait_ge(g_in, 32)
                dve.tensor_tensor(simsq[:], sim[:], sim[:], ALU.mult).then_inc(simsq_ready, 1)
                for t in range(NT):
                    tile = slice(t * P, (t + 1) * P)
                    dve.wait_ge(f_ready, t + 1)
                    dve.wait_ge(hi_ready, t + 1)
                    dve.tensor_tensor(T["xnlo"][:, :, tile], ps[:, t % 2].rearrange("p (c r) -> p c r", c=DC),
                                      T["xnhi"][:, :, tile].bitcast(F32), ALU.subtract).then_inc(lo_ready, 1)
                dve.wait_ge(norm_ready, 2)
                link(dve.tensor_scalar(norm_n[:], norm_n[:], 1e-12, None, ALU.max))
                link(dve.reciprocal(inv_n[:], norm_n[:]))
                link(dve.tensor_scalar(norm_e[:], norm_e[:], 1e-12, None, ALU.max))
                link(dve.reciprocal(inv_e[:], norm_e[:]))
                dve.wait_ge(e_ready, 1)
                link(dve.tensor_scalar(egate[:], egate[:], 1.0, None, ALU.add))
                link(dve.reciprocal(sig[:], egate[:]))
                dve.wait_ge(logits_ready, 1)
                dve.tensor_tensor(L[:], ps[:, 2, 0:NT * E].rearrange("p (t e) -> p t e", t=NT), rows(inv_n),
                                  ALU.mult).then_inc(logits_read, 1)
                dve.wait_ge(logits_read, 1)
                link(dve.tensor_tensor(L[:], L[:], cols(inv_e), ALU.mult))
                link(dve.tensor_tensor(L[:], L[:], cols(sig), ALU.subtract))
                dve.wait_ge(rev_set, 3)
                for logits, sel in ((L, sel1), (L2, sel2)):
                    link(dve.tensor_reduce(top[:], logits[:], AX.X, ALU.max))
                    link(dve.tensor_tensor(key[:], logits[:], rows(top), ALU.is_equal))
                    link(dve.tensor_tensor(key[:], key[:], cols(rev), ALU.mult))
                    if sel is sel1:
                        link(dve.tensor_scalar(idle[:], top[:], 0.0, None, ALU.is_le))
                    link(dve.tensor_reduce(kmax[:], key[:], AX.X, ALU.max))
                    link(dve.tensor_tensor(sel[:], key[:], rows(kmax), ALU.is_equal))
                    if sel is sel1:
                        link(dve.scalar_tensor_tensor(out=L2[:], in0=sel1[:], scalar=-BIG, in1=L[:], op0=ALU.mult,
                                                      op1=ALU.add))
                link(dve.tensor_tensor(put[:], sel1[:], sel2[:], ALU.add))
                link(dve.tensor_tensor(put[:], put[:], rows(idle), ALU.mult))
                link(dve.tensor_scalar(on[:], L[:], 0.0, None, ALU.is_gt))
                link(dve.tensor_tensor(on[:], on[:], put[:], ALU.max))
                link(dve.tensor_scalar(g[:], L[:], 0.0, None, ALU.max))
                link(dve.tensor_scalar(on[:], on[:], BIG, -BIG, ALU.mult, ALU.add))
                link(dve.tensor_tensor(g[:], g[:], on[:], ALU.add))
                link(dve.tensor_reduce(gmax[:], g[:], AX.X, ALU.max))
                dve.tensor_tensor(key[:], g[:], rows(gmax), ALU.subtract).then_inc(x_asked, 1)
                dve.wait_ge(x_ready, 1)
                link(dve.tensor_reduce(gsum[:], ex[:], AX.X, ALU.add))
                link(dve.reciprocal(ginv[:], gsum[:]))
                link(dve.tensor_tensor(w[:], ex[:], rows(ginv), ALU.mult))
                dve.sem_inc(y_added, U)
                with dve.Fori(1, E // 2 + 1) as r:
                    for n in range(U):
                        j, t = divmod(n, NT)
                        dve.wait_ge(y_added, r * U + (n + 1 - NT))
                        dve.wait_ge(y_ready, r * U + (n + 1))
                        dve.scalar_tensor_tensor(out=y[:, t], in0=ps[:, (t + 4) % 8, 0:Q3], scalar=w[:, t, bass.ds(r * 2 + (j - 2), 1)],
                                                 in1=y[:, t], op0=ALU.mult, op1=ALU.add).then_inc(y_added, 1)

            @block.tensor
            def _(pe):
                pe.sem_inc(y_ready, U)
                for t in range(NT):
                    if t >= 2:
                        pe.wait_ge(lo_ready, t - 1)
                    for d in range(DC):
                        ins = pe.transpose(ps[:, t % 2, d * P:(d + 1) * P], xn[:, t, d * P:(d + 1) * P], ident[:])
                    ins.then_inc(turned, 1)
                pe.wait_ge(simsq_ready, 1)
                for d in range(DC):
                    ins = pe.matmul(ps[:, 3, 0:E], T["ones"][:], simsq[:, d], start=d == 0, stop=d == DC - 1)
                ins.then_inc(colsq_ready, 1)
                for t in range(NT):
                    pe.wait_ge(f_ready, t + 1)
                    for d in range(DC):
                        ins = pe.matmul(ps[:, 2, t * E:(t + 1) * E], xnT[:, d, t * P:(t + 1) * P], sim[:, d],
                                        start=d == 0, stop=d == DC - 1)
                ins.then_inc(logits_ready, 1)
                pe.wait_ge(lo_ready, NT)
                with pe.Fori(1, E // 2 + 1) as r:
                    for n in range(U):
                        j, t = divmod(n, NT)
                        if t == 0:
                            pe.wait_ge(split[j], r * 4 + 2)
                        if n == 4:
                            pe.wait_ge(norm_ready, 2)
                            pe.wait_ge(logits_read, 1)
                        pe.wait_ge(y_added, r * U + (n + 1 - NT))
                        i = 0
                        for d in range(DC):
                            for a, b in ((T["xnhi"], whi), (T["xnlo"], whi), (T["xnhi"], wlo)):
                                ins = pe.matmul(ps[:, (t + 4) % 8, 0:Q3], a[:, d, t * P:(t + 1) * P], b[:, j, d], start=i == 0,
                                                stop=i == 3 * DC - 1)
                                i += 1
                        ins.then_inc(y_ready, 1)


def expert_attention(nc, T, io, out):
    SC = float(H) ** -0.5
    Z = E // 4
    with ExitStack() as ctx:
        m = Mem(nc, ctx)
        ps, x, ident, w, y = T["ps"], T["x"], T["ident"], T["w"], T["y"]
        qkT = m.sb("qkT", [P, 2, B * S])
        p, pT = m.sb("y_probs", [P, 2, S]), m.sb("y_probsT", [P, 2, S])
        rmax, nb, rsum, rinv = (m.sb("y_" + n, [P, NT]) for n in ("max", "nb", "sum", "inv"))
        o = m.sb("y_out", [P, NT, H])
        z = m.sb("z", [P, 2, E, H])
        zhi, zlo = m.sb("zT_hi", [P, Z, 512], F32R), m.sb("zT_lo", [P, Z, 512], F32R)

        dve_step = m.sem("g_dve_step")
        qk_turned, qk_copied = m.sem("qk_turned"), m.sem("qk_copied")
        s_ready, s_copied, nb_ready, p_ready = m.sem("ys_ready"), m.sem("ys_copied"), m.sem("ynb_ready"), m.sem("yp_ready")
        pt_ready, pt_copied, pv_ready, o_ready = m.sem("ypt_ready"), m.sem("ypt_copied"), m.sem("ypv_ready"), m.sem("yo_ready")
        z_ready = [m.sem("z_ready_dve"), m.sem("z_ready_pool")]
        z_turned, zhi_ready, zlo_ready = m.sem("z_turned"), m.sem("zhi_ready"), m.sem("zlo_ready")
        out_ready, x_ready, stored = m.sem("out_ready"), m.sem("x3_ready"), m.sem("stored")

        with nc.Block() as block:

            @block.sync
            def _(sp):
                rows = out.rearrange("b (t p) d -> (b t) p d", p=P)
                for t in range(NT):
                    sp.wait_ge(x_ready, t + 1)
                    sp.dma_start(rows[t], x[:, t]).then_inc(stored, 16)
                sp.wait_ge(stored, 16 * NT)

            @block.scalar
            def _(act):
                for i in range(2 * B):
                    b, which = divmod(i, 2)
                    act.wait_ge(qk_turned, i + 1)
                    act.copy(qkT[:, which, b * S:(b + 1) * S], ps[:, i % 2]).then_inc(qk_copied, 1)
                for t in range(NT + 1):
                    if t < NT:
                        act.wait_ge(nb_ready, t + 1)
                        if t >= 2:
                            act.wait_ge(pt_ready, t - 1)
                        act.activation(p[:, t % 2], ps[:, 2 + t % 2], ACT.Exp, bias=nb[:, t:t + 1], scale=SC,
                                       accum_out=rsum[:, t:t + 1]).then_inc(p_ready, 1)
                    if t >= 1:
                        act.wait_ge(pt_ready, t)
                        if t >= 3:
                            act.wait_ge(pv_ready, t - 2)
                        act.copy(pT[:, (t - 1) % 2], ps[:, 4 + (t - 1) % 2]).then_inc(pt_copied, 1)
                for t in range(NT):
                    for c in range(Z):
                        act.wait_ge(z_turned, t * Z + c + 1)
                        if t >= 1 and c == 0:
                            act.wait_ge(out_ready, t)
                        act.copy(zhi[:, c], ps[:, c % 4]).then_inc(zhi_ready, 1)

            @block.gpsimd
            def _(pool):
                for t in range(1, NT, 2):
                    pool.wait_ge(o_ready, t + 1)
                    if t >= 2:
                        pool.wait_ge(z_turned, (t - 1) * Z)
                    pool.tensor_tensor(z[:, t % 2], o[:, t].unsqueeze(1).to_broadcast([P, E, H]),
                                       w[:, t].unsqueeze(2).to_broadcast([P, E, H]), ALU.mult).then_inc(z_ready[1], 1)

            @block.vector
            def _(dve):
                for t in range(NT + 2):
                    if t < NT:
                        dve.wait_ge(s_ready, t + 1)
                        dve.tensor_reduce(rmax[:, t:t + 1], ps[:, 2 + t % 2], AX.X, ALU.max).then_inc(dve_step, 1)
                        dve.wait_ge(dve_step, t + 1)
                        dve.tensor_scalar(nb[:, t:t + 1], rmax[:, t:t + 1], -SC, None, ALU.mult).then_inc(nb_ready, 1)
                    if t >= 2:
                        u = t - 2
                        dve.wait_ge(p_ready, u + 1)
                        dve.reciprocal(rinv[:, u:u + 1], rsum[:, u:u + 1]).then_inc(s_copied, 1)
                        dve.wait_ge(s_copied, u + 1)
                        dve.wait_ge(pv_ready, u + 1)
                        dve.tensor_scalar(o[:, u], ps[:, 6 + u % 2, 0:H], rinv[:, u:u + 1], None,
                                          ALU.mult).then_inc(o_ready, 1)

                def products(t):
                    dve.wait_ge(o_ready, t + 1)
                    if t >= 2:
                        dve.wait_ge(z_turned, (t - 1) * Z)
                    dve.tensor_tensor(z[:, t % 2], o[:, t].unsqueeze(1).to_broadcast([P, E, H]),
                                      w[:, t].unsqueeze(2).to_broadcast([P, E, H]), ALU.mult).then_inc(z_ready[0], 1)

                def add_out(t):
                    dve.wait_ge(out_ready, t + 1)
                    dve.tensor_tensor(x[:, t], ps[:, 4 + t % 2], x[:, t], ALU.add).then_inc(x_ready, 1)

                products(0)
                for t in range(NT):
                    for c in range(Z):
                        dve.wait_ge(zhi_ready, t * Z + c + 1)
                        dve.tensor_tensor(zlo[:, c], ps[:, c % 4], zhi[:, c].bitcast(F32), ALU.subtract).then_inc(zlo_ready, 1)
                    if t % 2 and t + 1 < NT:
                        products(t + 1)
                    if t >= 1:
                        add_out(t - 1)
                add_out(NT - 1)

            @block.tensor
            def _(pe):
                for i in range(2 * B):
                    b, which = divmod(i, 2)
                    if i >= 2:
                        pe.wait_ge(qk_copied, i - 1)
                    for k in range(QT):
                        ins = pe.transpose(ps[:, i % 2, k * P:(k + 1) * P], y[:, b * QT + k, which * H:(which + 1) * H], ident[:])
                    ins.then_inc(qk_turned, 1)
                for t in range(NT + 2):
                    if t < NT:
                        b = t // QT
                        pe.wait_ge(qk_copied, 2 * b + 2)
                        if t >= 2:
                            pe.wait_ge(p_ready, t - 1)
                        pe.matmul(ps[:, 2 + t % 2], qkT[:, 0, t * P:(t + 1) * P], qkT[:, 1, b * S:(b + 1) * S],
                                  start=True, stop=True).then_inc(s_ready, 1)
                    if 1 <= t <= NT:
                        u = t - 1
                        pe.wait_ge(p_ready, u + 1)
                        if u >= 2:
                            pe.wait_ge(pt_copied, u - 1)
                        for k in range(QT):
                            ins = pe.transpose(ps[:, 4 + u % 2, k * P:(k + 1) * P], p[:, u % 2, k * P:(k + 1) * P], ident[:])
                        ins.then_inc(pt_ready, 1)
                    if t >= 2:
                        u = t - 2
                        pe.wait_ge(pt_copied, u + 1)
                        if u >= 2:
                            pe.wait_ge(o_ready, u - 1)
                        for k in range(QT):
                            ins = pe.matmul(ps[:, 6 + u % 2, 0:H], pT[:, u % 2, k * P:(k + 1) * P],
                                            y[:, (u // QT) * QT + k, 2 * H:3 * H], start=k == 0, stop=k == QT - 1)
                        ins.then_inc(pv_ready, 1)

                def turn(t):
                    pe.wait_ge(z_ready[t % 2], t // 2 + 1)
                    for c in range(Z):
                        if t >= 1:
                            pe.wait_ge(zlo_ready, (t - 1) * Z + c + 1)
                        for k in range(4):
                            ins = pe.transpose(ps[:, c, k * P:(k + 1) * P], z[:, t % 2, 4 * c + k], ident[:])
                        ins.then_inc(z_turned, 1)

                turn(0)
                for t in range(NT):
                    if t >= 2:
                        pe.wait_ge(x_ready, t - 1)
                    for e in range(E):
                        if e % 4 == 0:
                            pe.wait_ge(zlo_ready, t * Z + e // 4 + 1)
                        cut = slice((e % 4) * P, (e % 4 + 1) * P)
                        for i, (a, b) in enumerate(((zhi, T["ohi"]), (zlo, T["ohi"]), (zhi, T["olo"]))):
                            ins = pe.matmul(ps[:, 4 + t % 2], a[:, e // 4, cut], b[:, e], start=e == 0 and i == 0,
                                            stop=e == E - 1 and i == 2)
                    ins.then_inc(out_ready, 1)
                    if t + 1 < NT:
                        turn(t + 1)


def program(nc, io, out):
    with ExitStack() as ctx:
        m = Mem(nc, ctx)
        T = {"ps": ctx.enter_context(nc.psum_tensor("ps", [P, 8, 512], F32))}
        T["x"] = m.sb("x", [P, NT, D])
        T["ident"] = m.sb("ident", [P, P])
        T["ones"] = m.sb("ones", [P, P])
        T["waited"] = m.sem("waited")
        T["weights_in"], T["weights_total"] = m.sem("weights_in"), 5 * 16

        T["xn3"] = T["acc"] = m.sb("acc", [P, NT, D])

        with ExitStack() as early:
            m = Mem(nc, early)
            T["m_run"], T["l_run"] = m.sb("m_run", [P, NT]), m.sb("l_run", [P, NT])
            latent_weights = m.sb("latent_weights", [P, 5, D])
            T["dqkv"] = latent_weights[:, 0:2].rearrange("p i (c e) -> p i c e", e=DCQ)
            T["uq"], T["uk"], T["uv"] = (latent_weights[:, 2 + i] for i in range(3))
            T["Wvhi"], T["Wvlo"] = m.sb("Wv_hi", [P, DC, D], F32R), m.sb("Wv_lo", [P, DC, D], F32R)
            T["sums"], T["place"] = m.sb("head_sums", [P, P]), m.sb("place", [P, NT, P])
            with ExitStack() as front:
                m = Mem(nc, front)
                T["ghi"], T["glo"] = m.sb("g_hi", [P, DC, B * S], F32R), m.sb("g_lo", [P, DC, B * S], F32R)
                T["c"] = m.sb("c", [P, NT])
                T["live"] = m.sb("live", [P, NB + 1], I32)
                queries(nc, T, io)
                cross_attention(nc, T, io)
            m = Mem(nc, early)
            T["v"], T["o"] = m.sb("v", [P, NT, D]), m.sb("o", [P, NT, D])
            T["qkT"] = [[m.sb(f"{n}T_{h}", [P, DC, B * S], F32R) for h in ("hi", "lo")] for n in ("q", "k")]
            latents(nc, T, io)
            T["Wohi"], T["Wolo"] = T["Wvhi"], T["Wvlo"]
            T["Wo"] = latent_weights[:, 0:DC]
            heads(nc, T, io)
            heads_out(nc, T)
        with ExitStack() as late:
            m = Mem(nc, late)
            T["xnhi"], T["xnlo"] = m.sb("xn3T_hi", [P, DC, B * S], F32R), m.sb("xn3T_lo", [P, DC, B * S], F32R)
            T["ohi"], T["olo"] = m.sb("O_hi", [P, E, D], F32R), m.sb("O_lo", [P, E, D], F32R)
            T["w"], T["y"] = m.sb("w", [P, NT, E]), m.sb("y", [P, NT, 3 * H])
            experts(nc, T, io)
            expert_attention(nc, T, io, out)


_INS = {"x": "x", "ctx": "ctx_1024", "mask": "mask_SxS2_bk0", "Wq": "L0_xattn_Wq", "bq": "L0_xattn_bq",
        "Wk": "L0_xattn_Wk", "bk": "L0_xattn_bk", "Wv": "L0_xattn_Wv", "bv": "L0_xattn_bv", "dq": "L0_attn_W_dq",
        "uq": "L0_attn_W_uq", "dkv": "L0_attn_W_dkv", "uk": "L0_attn_W_uk", "uv": "L0_attn_W_uv", "Wo": "L0_attn_W_o",
        "sim": "L0_ffn_sim_matrix", "gates": "L0_ffn_gates", "qp": "L0_ffn_q_proj", "kp": "L0_ffn_k_proj",
        "vp": "L0_ffn_v_proj", "op": "L0_ffn_o_proj"}


def kernel(**inputs):
    import numpy as _np
    import concourse.bacc as _bacc
    from concourse import mybir as _mybir
    from concourse.bass_utils import run_bass_kernel_spmd as _run

    nc = _bacc.Bacc("TRN2", target_bir_lowering=False, num_devices=1)
    arrays, io = {}, {}
    for name, key in _INS.items():
        a = _np.ascontiguousarray(inputs[key])
        arrays[f"in_{name}_dram"] = a
        dt = U8 if a.dtype == _np.bool_ else _mybir.dt.from_np(a.dtype)
        io[name] = nc.dram_tensor(f"in_{name}_dram", a.shape, dt, kind="ExternalInput").ap()
    out = nc.dram_tensor("out_dram", (B, S, D), _mybir.dt.from_np(_np.dtype("float32")), kind="ExternalOutput").ap()
    program(nc, io, out)
    r = _run(nc, [arrays], core_ids=[0])
    return r.results[0]["out_dram"]
```

```python
from contextlib import ExitStack

import concourse.bass as bass
from concourse import mybir

F32 = mybir.dt.float32
F32R = mybir.dt.float32r
I32 = mybir.dt.int32
U8 = mybir.dt.uint8
ALU = mybir.AluOpType
ACT = mybir.ActivationFunctionType
AX = mybir.AxisListType

P = 128
B, S, D = 2, 512, 512
KEYS = 8192
NT = B * S // P
QT = S // P
DC = D // P
KB = 512
NB = KEYS // KB
KC = KB // P
NH, DK = 16, 32
DCQ = 128
E, H = 16, 128
EPS = 1e-5
BIG = 1e30
LOWEST = -3e38
XSCALE = float(D) ** -0.5


class Mem:

    def __init__(self, nc, ctx):
        self.nc, self.ctx = nc, ctx

    def sb(self, name, shape, dt=F32):
        return self.ctx.enter_context(self.nc.sbuf_tensor(name, shape, dt))

    def sem(self, name):
        return self.ctx.enter_context(self.nc.semaphore(name))


def chained(eng, sem):
    count = [0]

    def link(ins):
        count[0] += 1
        ins.then_inc(sem, 1)
        eng.wait_ge(sem, count[0])

    return link


def apart(eng, waited):
    eng.sem_inc(waited, 1)


def layernorm_stats(dve, link, x, stats, mv, varp, rows_ready=None):
    for t in range(NT):
        if rows_ready is not None:
            rows_ready(t)
        link(dve.bn_stats(stats[:, t, :], x[:, t, :]))
    for t in range(NT):
        ins = dve.bn_aggr(mv[:, t, :], stats[:, t, :])
    link(ins)
    return dve.tensor_scalar(varp[:], mv[:, :, 1], EPS, None, ALU.add)


def queries(nc, T, io):
    with ExitStack() as ctx:
        m = Mem(nc, ctx)
        ps, x, ident = T["ps"], T["x"], T["ident"]
        wThi, wTlo = T["ghi"], T["glo"]
        xn = T["acc"]
        mask = m.sb("mask_rows", [P, 2, KEYS], U8)
        wraw, wvraw = m.sb("wraw", [P, 2, DC, D]), m.sb("wv_raw", [P, DC, D])
        Mhi, Mlo = m.sb("M_hi", [P, DC, D], F32R), m.sb("M_lo", [P, DC, D], F32R)
        xnThi, xnTlo = m.sb("xnT_hi", [P, DC, B * S], F32R), m.sb("xnT_lo", [P, DC, B * S], F32R)
        brows, dot, colsum = m.sb("bias_rows", [P, 2, D]), m.sb("dot", [P, D]), m.sb("colsum", [P, 2 * DC])
        wgcol, bb = m.sb("g_bias", [P, DC]), m.sb("bb", [P, 1])
        chl = m.sb("wqbk_halves", [P, DC, 2], F32R)
        cpair, csum = m.sb("c_pair", [P, NT, 2]), m.sb("c_sum", [P, NT])
        stats, mv = m.sb("stats", [P, NT, 6]), m.sb("mv", [P, NT, 2])
        varp, std, rstd = (m.sb(n, [P, NT]) for n in ("varp", "std", "rstd"))
        red, act_f = m.sb("red", [P, QT, NB]), m.sb("act_f", [P, NB])
        lower, grid = m.sb("lower", [P, NB, NB]), m.sb("grid", [P, NB, NB])
        iota_i, iota, rank, number = m.sb("iota_i", [P, NB], I32), m.sb("iota", [P, NB]), m.sb("rank", [P, NB]), m.sb("number", [P, NB])
        order, total = m.sb("order", [P, NB]), m.sb("total", [P, 1])

        closed = m.sb("closed_raw", [P, 2, P])
        bv, bv_in = m.sb("bv_rows", [P, D]), m.sem("bv_in")
        x_in, b_in, wv_in = m.sem("x_in"), m.sem("b_in"), m.sem("wv_in")
        w_in = [m.sem("wq_in"), m.sem("wk_in")]
        mask_in = [m.sem("mask_in0"), m.sem("mask_in1")]
        ones_set, ident_set = m.sem("ones_set"), m.sem("ident_set")
        pool_step, dve_step = m.sem("a_pool_step"), m.sem("a_dve_step")
        var_ready, std_ready, xn_ready = m.sem("var_ready"), m.sem("std_ready"), m.sem("xn_ready")
        w_turned, w_hi, w_lo = m.sem("w_turned"), m.sem("w_hi"), m.sem("w_lo")
        x_turned, x_hi, x_lo = m.sem("x_turned"), m.sem("x_hi"), m.sem("x_lo")
        m_ready, m_hi, m_lo = m.sem("m_ready"), m.sem("m_hi"), m.sem("m_lo")
        bias_ready, chl_ready = m.sem("g_bias_ready"), m.sem("chl_ready")
        g_ready, g_hi, g_lo, c_ready = m.sem("g_ready"), m.sem("g_hi_ready"), m.sem("g_lo_ready"), m.sem("c_ready")
        red_ready, any_ready = m.sem("red_ready"), m.sem("any_ready")
        halves = ((0, 0), (1, 0), (0, 1))

        with nc.Block() as block:

            @block.sync
            def _(sp):
                sp.dma_start(wraw[:, 0], io["Wq"].rearrange("(c p) e -> p c e", p=P)).then_inc(w_in[0], 16)
                sp.dma_start(x[:], io["x"].rearrange("b (t p) d -> p (b t) d", p=P)).then_inc(x_in, 16)
                sp.dma_start(wraw[:, 1], io["Wk"].rearrange("(c p) e -> p c e", p=P)).then_inc(w_in[1], 16)
                for i, n in enumerate(("bq", "bk")):
                    sp.dma_start(brows[:, i], io[n].rearrange("(a d) -> a d", a=1).to_broadcast([P, D])).then_inc(b_in, 16)
                sp.dma_start(bv[:], io["bv"].rearrange("(a d) -> a d", a=1).to_broadcast([P, D])).then_inc(bv_in, 16)
                for t in range(QT):
                    if t == 2:
                        sp.dma_start(wvraw[:], io["Wv"].rearrange("(c p) e -> p c e", p=P)).then_inc(wv_in, 16)
                    if t >= 2:
                        sp.wait_ge(red_ready, t - 1)
                    sp.dma_start(mask[:, t % 2], io["mask"].rearrange("(t p) k -> t p k", p=P)[t]).then_inc(mask_in[t % 2], 16)
                for i, n in enumerate(("dq", "dkv")):
                    sp.dma_start(T["dqkv"][:, i], io[n].rearrange("(c p) e -> p c e", p=P)).then_inc(T["weights_in"], 16)
                for n in ("uq", "uk", "uv"):
                    sp.dma_start(T[n][:], io[n]).then_inc(T["weights_in"], 16)

            @block.gpsimd
            def _(pool):
                link = chained(pool, pool_step)
                link(pool.memset(ident[:], 0.0))
                pool.affine_select(out=ident[:], in_=ident[:], compare_op=ALU.not_equal, fill=1.0, base=0,
                                   pattern=[[-1, P]], channel_multiplier=1).then_inc(ident_set, 1)
                link(pool.memset(lower[:], 0.0))
                link(pool.affine_select(out=lower[:], in_=lower[:], compare_op=ALU.is_ge, fill=1.0, base=0,
                                        pattern=[[-1, NB], [1, NB]], channel_multiplier=0))
                link(pool.iota(iota_i[:], pattern=[[1, NB]], base=0, channel_multiplier=0))
                pool.tensor_copy(iota[:], iota_i[:]).then_inc(ones_set, 1)
                link(pool.memset(closed[:], 0.0))
                for i, sign in enumerate((1, -1)):
                    link(pool.affine_select(out=closed[:, i], in_=closed[:, i], compare_op=ALU.is_ge, fill=-BIG, base=0,
                                            pattern=[[sign, P]], channel_multiplier=-sign))
                link(pool.tensor_copy(T["closed"][:], closed[:]))
                link(pool.tensor_copy(T["ident_r"][:], ident[:]))
                pool.wait_ge(xn_ready, NT)
                pool.wait_ge(bv_in, 16)
                link(pool.tensor_tensor(x[:], x[:], bv[:].unsqueeze(1).to_broadcast([P, NT, D]), ALU.add))
                pool.wait_ge(wv_in, 16)
                link(pool.tensor_copy(T["Wvhi"][:], wvraw[:]))
                pool.tensor_tensor(T["Wvlo"][:], wvraw[:], T["Wvhi"][:].bitcast(F32), ALU.subtract).then_inc(pool_step, 1)

            @block.scalar
            def _(act):
                def weights_hi(i):
                    act.wait_ge(w_turned, i + 1)
                    act.copy(wThi[:, i // 2, (i % 2) * 512:(i % 2) * 512 + 512], ps[:, i % 2]).then_inc(w_hi, 1)

                for i in range(DC):
                    weights_hi(i)
                act.wait_ge(var_ready, 1)
                act.activation(std[:], varp[:], ACT.Sqrt).then_inc(std_ready, 1)
                for i in range(DC, 2 * DC):
                    weights_hi(i)
                for i in range(DC):
                    act.wait_ge(m_ready, i + 1)
                    act.activation(Mhi[:, i], ps[:, 2 + i % 2], ACT.Copy, scale=XSCALE).then_inc(m_hi, 1)
                    for t in (2 * i, 2 * i + 1):
                        act.wait_ge(x_turned, t + 1)
                        act.copy(xnThi[:, :, t * P:(t + 1) * P], ps[:, t % 2].rearrange("p (c r) -> p c r", c=DC)).then_inc(x_hi, 1)
                act.wait_ge(bias_ready, 1)
                for i in range(2 * DC):
                    half, j = divmod(i, DC)
                    act.wait_ge(g_ready, i + 1)
                    act.activation(T["ghi"][:, j, half * 512:half * 512 + 512], ps[:, 5 + i % 2], ACT.Identity,
                                   bias=wgcol[:, j:j + 1], scale=1.0).then_inc(g_hi, 1)

            @block.vector
            def _(dve):
                link = chained(dve, dve_step)
                link(dve.memset(T["ones"][:], 1.0))

                def weights_lo(i):
                    dve.wait_ge(w_hi, i + 1)
                    at = slice((i % 2) * 512, (i % 2) * 512 + 512)
                    dve.tensor_tensor(wTlo[:, i // 2, at], ps[:, i % 2], wThi[:, i // 2, at].bitcast(F32),
                                      ALU.subtract).then_inc(w_lo, 1)

                for i in range(DC):
                    weights_lo(i)
                dve.wait_ge(x_in, 16)
                layernorm_stats(dve, link, x, stats, mv, varp).then_inc(var_ready, 1)
                for i in range(DC, 2 * DC):
                    weights_lo(i)
                dve.wait_ge(std_ready, 1)
                link(dve.reciprocal(rstd[:], std[:]))
                for t in range(NT):
                    dve.tensor_scalar(xn[:, t], x[:, t], mv[:, t, 0:1], rstd[:, t:t + 1], ALU.subtract,
                                      ALU.mult).then_inc(xn_ready, 1)
                def seen(t):
                    dve.wait_ge(mask_in[t % 2], 16 * (t // 2) + 16)
                    words = mask[:, t % 2].bitcast(I32).rearrange("p (b w) -> p b w", b=NB)
                    dve.tensor_reduce(red[:, t], words, AX.X, ALU.max).then_inc(red_ready, 1)

                def dots(which):
                    for j in range(DC):
                        link(dve.tensor_tensor_reduce(out=dot[:], in0=wraw[:, 1 - which, j], in1=brows[:, which], scale=1.0,
                                                      scalar=0.0, op0=ALU.mult, op1=ALU.add,
                                                      accum_out=colsum[:, which * DC + j:which * DC + j + 1]))

                dve.wait_ge(b_in, 32)
                dots(0)
                dve.tensor_scalar(wgcol[:], colsum[:, 0:DC], XSCALE, None, ALU.mult).then_inc(bias_ready, 1)
                for i in range(DC):
                    dve.wait_ge(m_hi, i + 1)
                    dve.scalar_tensor_tensor(out=Mlo[:, i], in0=ps[:, 2 + i % 2], scalar=XSCALE, in1=Mhi[:, i].bitcast(F32),
                                             op0=ALU.mult, op1=ALU.subtract).then_inc(m_lo, 1)
                    for t in (2 * i, 2 * i + 1):
                        dve.wait_ge(x_hi, t + 1)
                        at = slice(t * P, (t + 1) * P)
                        dve.tensor_tensor(xnTlo[:, :, at], ps[:, t % 2].rearrange("p (c r) -> p c r", c=DC),
                                          xnThi[:, :, at].bitcast(F32), ALU.subtract).then_inc(x_lo, 1)
                    if i < 2:
                        seen(i)
                def chl_halves():
                    dots(1)
                    link(dve.tensor_tensor_reduce(out=dot[:], in0=brows[:, 0], in1=brows[:, 1], scale=1.0, scalar=0.0, op0=ALU.mult,
                                                  op1=ALU.add, accum_out=bb[:]))
                    link(dve.tensor_copy(chl[:, :, 0], colsum[:, DC:2 * DC]))
                    dve.tensor_tensor(chl[:, :, 1], colsum[:, DC:2 * DC], chl[:, :, 0].bitcast(F32),
                                      ALU.subtract).then_inc(chl_ready, 1)

                dve.wait_ge(bias_ready, 1)

                def g_low(i):                dve.wait_ge(bias_ready, 1)

                def g_low(i):
                    half, j = divmod(i, DC)
                    at = slice(half * 512, half * 512 + 512)
                    dve.wait_ge(g_hi, i + 1)
                    dve.scalar_tensor_tensor(out=T["glo"][:, j, at], in0=ps[:, 5 + i % 2], scalar=wgcol[:, j:j + 1],
                                             in1=T["ghi"][:, j, at].bitcast(F32), op0=ALU.add,
                                             op1=ALU.subtract).then_inc(g_lo, 1)

                for i in range(2 * DC):
                    g_low(i)
                    if i in (0, 2):
                        seen(2 + i // 2)
                    if i == 3:
                        chl_halves()
                dve.wait_ge(any_ready, 1)
                dve.wait_ge(ones_set, 1)
                link(dve.tensor_scalar(act_f[:], ps[:, 7, 0:NB], 0.0, None, ALU.is_gt))
                link(dve.tensor_tensor(grid[:], lower[:], act_f[:].unsqueeze(1).to_broadcast([P, NB, NB]), ALU.mult))
                link(dve.tensor_reduce(rank[:], grid[:], AX.X, ALU.add))
                link(dve.tensor_tensor(number[:], act_f[:], iota[:], ALU.mult))
                link(dve.tensor_reduce(total[:], act_f[:], AX.X, ALU.add))
                link(dve.tensor_tensor(grid[:], rank[:].unsqueeze(1).to_broadcast([P, NB, NB]),
                                       iota[:].unsqueeze(2).to_broadcast([P, NB, NB]), ALU.is_equal))
                link(dve.tensor_tensor(grid[:], grid[:], number[:].unsqueeze(1).to_broadcast([P, NB, NB]), ALU.mult))
                link(dve.tensor_reduce(order[:], grid[:], AX.X, ALU.add))
                link(dve.memset(T["live"][:], 0))
                link(dve.tensor_copy(T["live"][:, 0:NB], order[:]))
                link(dve.tensor_copy(T["live"][:, NB + 1:NB + 2], total[:]))
                dve.wait_ge(c_ready, 1)
                link(dve.tensor_copy(cpair[:].rearrange("p t b -> p (t b)"), ps[:, 4, 64:64 + 2 * NT]))
                link(dve.tensor_tensor(csum[:], cpair[:, :, 0], cpair[:, :, 1], ALU.add))
                dve.tensor_scalar(T["c"][:], csum[:], bb[:, 0:1], XSCALE, ALU.add, ALU.mult).then_inc(dve_step, 1)

            @block.tensor
            def _(pe):
                pe.wait_ge(ident_set, 1)
                for i in range(2 * DC):
                    w, e = divmod(i, DC)
                    pe.wait_ge(w_in[w], 16)
                    if i >= 2:
                        pe.wait_ge(w_lo, i - 1)
                    for d in range(DC):
                        ins = pe.transpose(ps[:, i % 2, d * P:(d + 1) * P], wraw[:, w, d, e * P:(e + 1) * P], ident[:])
                    ins.then_inc(w_turned, 1)
                wT = [[[h[:, (w * DC + e) // 2, (e % 2) * 512:(e % 2) * 512 + 512] for e in range(DC)] for w in range(2)]
                      for h in (wThi, wTlo)]
                pe.wait_ge(w_lo, 2 * DC)
                for i in range(DC):
                    if i >= 2:
                        pe.wait_ge(m_lo, i - 1)
                    n = 0
                    for e in range(DC):
                        for a, b in halves:
                            ins = pe.matmul(ps[:, 2 + i % 2], wT[a][0][e][:, i * P:(i + 1) * P], wT[b][1][e], start=n == 0,
                                            stop=n == 3 * DC - 1)
                            n += 1
                    ins.then_inc(m_ready, 1)
                    for t in (2 * i, 2 * i + 1):
                        pe.wait_ge(xn_ready, t + 1)
                        if t >= 2:
                            pe.wait_ge(x_lo, t - 1)
                        for d in range(DC):
                            ins = pe.transpose(ps[:, t % 2, d * P:(d + 1) * P], xn[:, t, d * P:(d + 1) * P], ident[:])
                        ins.then_inc(x_turned, 1)
                pe.wait_ge(m_lo, DC)
                for i in range(2 * DC):
                    half, j = divmod(i, DC)
                    if j == 0:
                        pe.wait_ge(x_lo, (half + 1) * QT)
                    if i >= 2:
                        pe.wait_ge(g_lo, i - 1)
                    if i == 6:
                        pe.wait_ge(red_ready, QT)
                        for t in range(QT):
                            ins = pe.matmul(ps[:, 7, 0:NB], T["ones"][:], red[:, t], start=t == 0, stop=t == QT - 1)
                        ins.then_inc(any_ready, 1)
                    M, xT, n = (Mhi, Mlo), (xnThi, xnTlo), 0
                    for d in range(DC):
                        for a, b in halves:
                            ins = pe.matmul(ps[:, 5 + i % 2], M[a][:, d, j * P:(j + 1) * P],
                                            xT[b][:, d, half * 512:half * 512 + 512], start=n == 0, stop=n == 3 * DC - 1)
                            n += 1
                    ins.then_inc(g_ready, 1)
                pe.wait_ge(chl_ready, 1)
                for t in range(NT):
                    for d in range(DC):
                        for a, h in enumerate((xnThi, xnTlo)):
                            ins = pe.matmul(ps[:, 4, 64 + 2 * t:66 + 2 * t], h[:, d, t * P:(t + 1) * P], chl[:, d],
                                            start=d == 0 and a == 0, stop=d == DC - 1 and a == 1)
                ins.then_inc(c_ready, 1)


def cross_attention(nc, T, io):
    with ExitStack() as ctx:
        m = Mem(nc, ctx)
        ps, ident, ghi, glo, live = T["ps"], T["ident"], T["ghi"], T["glo"], T["live"]
        m_run, l_run, acc, c = T["m_run"], T["l_run"], T["acc"], T["c"]
        raw = m.sb("ctx_raw", [P, B, KC, D])
        chi = m.sb("ctx_hi", [P, B, KC, D], F32R)
        clo = m.sb("ctx_lo", [P, B, KC, D], F32R)
        cThi = m.sb("ctxT_hi", [P, B, DC, KB], F32R)
        cTlo = m.sb("ctxT_lo", [P, B, DC, KB], F32R)
        mask = m.sb("mask_block", [P, QT, KB], U8)
        bias = m.sb("mask_bias", [P, QT, KB])
        p = m.sb("probs", [P, 2, KB])
        pThi = m.sb("probsT_hi", [P, 2, KB], F32R)
        pTlo = m.sb("probsT_lo", [P, 2, KB], F32R)
        rmax, mnew, nb, dm = (m.sb(n, [P, NT]) for n in ("rmax", "mnew", "nb", "dm"))
        corr, rsum = m.sb("corr", [P, NT]), m.sb("rsum", [P, NT])

        ctx_in = [m.sem(f"ctx_in{s}") for s in range(B)]
        turned = [m.sem(f"ctx_turned{s}") for s in range(B)]
        split = [m.sem(f"ctx_split{s}") for s in range(B)]
        mblk_in, bias_ready = m.sem("mblk_in"), m.sem("bias_ready")
        thi_ready, tlo_ready = m.sem("ctxT_hi_ready"), m.sem("ctxT_lo_ready")
        score_ready, score_read = m.sem("score_ready"), m.sem("score_read")
        state_set = m.sem("state_set")
        m_step, nb_ready = m.sem("m_step"), m.sem("nb_ready")
        p_ready, corr_ready = m.sem("p_ready"), m.sem("corr_ready")
        pt_ready, pthi_ready, ptlo_ready = m.sem("pt_ready"), m.sem("pt_hi_ready"), m.sem("pt_lo_ready")
        pv_ready, acc_done, l_done = m.sem("pv_ready"), m.sem("acc_done"), m.sem("l_done")
        SCORE, PT, PV, TURN = 0, 2, 4, 6
        TURNS = {1: ((0, 1, 0), (0, 1, 1)), 2: ((0, 1, 2), (0, 1, 3)), 5: ((1, 0, 0), (1, 0, 1)), 6: ((1, 0, 2), (1, 0, 3))}

        GROUP = 4

        def taken(eng, step):
            count = eng.value_load(live[0:1, NB + 1:NB + 2], min_val=0, max_val=NB)
            with eng.Fori(0, NB // GROUP) as g:
                group = g * GROUP
                with eng.If(count > group):
                    with eng.Fori(1, GROUP + 1) as k:
                        with eng.If(count > group + k - 1):
                            step(group + k)
                        with eng.Else():
                            pass
                with eng.Else():
                    pass
            return count

        with nc.Block() as block:

            @block.sync
            def _(sp):
                for s in range(B):
                    sp.sem_inc(ctx_in[s], 16)
                sp.sem_inc(mblk_in, 16)
                context = io["ctx"].rearrange("s (b k p) d -> s b p k d", k=KC, p=P)
                masks = io["mask"].rearrange("(t p) (b k) -> b p t k", p=P, k=KB)

                def load(r):
                    b = sp.value_load(live[0:1, bass.ds(r, 1)], min_val=0, max_val=NB - 1)
                    first = isinstance(r, int)
                    for s in range(B):
                        if not first:
                            sp.wait_ge(turned[s], r * DC + DC)
                            apart(sp, T["waited"])
                            sp.wait_ge(split[s], r * 2 + 2)
                            apart(sp, T["waited"])
                        sp.dma_start(raw[:, s], context[s, b]).then_inc(ctx_in[s], 16)
                        if s == 0:
                            if not first:
                                sp.wait_ge(bias_ready, r + 1)
                                apart(sp, T["waited"])
                            sp.dma_start(mask[:], masks[b]).then_inc(mblk_in, 16)

                load(0)
                count = taken(sp, load)
                for done in (*ctx_in, mblk_in):
                    sp.wait_ge(done, count * 16 + 32)
                    apart(sp, T["waited"])

            @block.gpsimd
            def _(pool):
                for s in range(B):
                    pool.sem_inc(split[s], 2)
                pool.sem_inc(bias_ready, 1)
                pool.memset(m_run[:], -BIG).then_inc(state_set, 1)
                pool.memset(l_run[:], 0.0).then_inc(state_set, 1)
                pool.memset(acc[:], 0.0).then_inc(state_set, 1)

                def step(r):
                    pool.wait_ge(mblk_in, r * 16 + 16)
                    pool.wait_ge(score_read, r * NT)
                    apart(pool, T["waited"])
                    pool.tensor_scalar(bias[:], mask[:], BIG, -BIG, ALU.mult, ALU.add).then_inc(bias_ready, 1)
                    for s in range(B):
                        pool.wait_ge(ctx_in[s], r * 16 + 16)
                        pool.wait_ge(pv_ready, r * NT)
                        apart(pool, T["waited"])
                        pool.tensor_copy(chi[:, s], raw[:, s]).then_inc(split[s], 1)
                        pool.wait_ge(split[s], r * 2 + 1)
                        pool.tensor_tensor(clo[:, s], raw[:, s], chi[:, s].bitcast(F32),
                                           ALU.subtract).then_inc(split[s], 1)

                taken(pool, step)

            @block.tensor
            def _(pe):
                for s in range(B):
                    pe.sem_inc(turned[s], DC)
                pe.sem_inc(score_ready, NT)
                pe.sem_inc(pt_ready, NT)
                pe.sem_inc(pv_ready, NT)

                def turn(r, s, g):
                    n = s * DC + g
                    pe.wait_ge(ctx_in[s], r * 16 + 16)
                    pe.wait_ge(tlo_ready, r * B * DC + n - 1)
                    for k in range(KC):
                        ins = pe.transpose(ps[:, TURN + g % 2, k * P:(k + 1) * P], raw[:, s, k, g * P:(g + 1) * P], ident[:])
                    ins.then_inc(turned[s], 1)

                def score(r, u):
                    s = u // QT
                    if u % QT == 0:
                        pe.wait_ge(tlo_ready, r * B * DC + (s + 1) * DC)
                    pe.wait_ge(score_read, r * NT + u - 1)
                    n = 0
                    for d in range(DC):
                        for a, b in ((ghi, cThi), (glo, cThi), (ghi, cTlo)):
                            ins = pe.matmul(ps[:, SCORE + u % 2], a[:, d, u * P:(u + 1) * P], b[:, s, d],
                                            start=n == 0, stop=n == 3 * DC - 1)
                            n += 1
                    ins.then_inc(score_ready, 1)

                def turn_probs(r, u):
                    pe.wait_ge(p_ready, r * NT + u + 1)
                    pe.wait_ge(ptlo_ready, r * NT + u - 1)
                    for k in range(KC):
                        ins = pe.transpose(ps[:, PT + u % 2, k * P:(k + 1) * P], p[:, u % 2, k * P:(k + 1) * P], ident[:])
                    ins.then_inc(pt_ready, 1)

                def value(r, u):
                    s = u // QT
                    if u % QT == 0:
                        pe.wait_ge(split[s], r * 2 + 2)
                    pe.wait_ge(ptlo_ready, r * NT + u + 1)
                    pe.wait_ge(acc_done, r * NT + u - 1)
                    n = 0
                    for k in range(KC):
                        for a, b in ((pThi, chi), (pTlo, chi), (pThi, clo)):
                            ins = pe.matmul(ps[:, PV + u % 2], a[:, u % 2, k * P:(k + 1) * P], b[:, s, k],
                                            start=n == 0, stop=n == 3 * KC - 1)
                            n += 1
                    ins.then_inc(pv_ready, 1)

                def step(r):
                    for u in range(NT + 2):
                        if u < NT:
                            score(r, u)
                        for k in TURNS.get(u, ()):
                            turn(r + k[0], *k[1:])
                        if 1 <= u <= NT:
                            turn_probs(r, u - 1)
                        if u >= 2:
                            value(r, u - 2)

                for g in range(DC):
                    turn(1, 0, g)
                taken(pe, step)

            @block.scalar
            def _(act):
                act.sem_inc(thi_ready, B * DC)
                act.sem_inc(p_ready, NT)
                act.sem_inc(corr_ready, NT)
                act.sem_inc(pthi_ready, NT)

                def context_hi(r, s, g):
                    act.wait_ge(turned[s], r * DC + g + 1)
                    if g == 0:
                        act.wait_ge(score_ready, r * NT + (QT - NT if s == 0 else 0))
                    act.copy(cThi[:, s, g], ps[:, TURN + g % 2]).then_inc(thi_ready, 1)

                def probs(r, u):
                    act.wait_ge(nb_ready, r * 2 * NT + 2 * u + 2)
                    if u == 0:
                        act.wait_ge(acc_done, r * NT)
                        act.wait_ge(l_done, r * NT)
                    act.activation(p[:, u % 2], p[:, u % 2], ACT.Exp, bias=nb[:, u:u + 1], scale=1.0,
                                   accum_out=rsum[:, u:u + 1]).then_inc(p_ready, 1)
                    act.activation(corr[:, u:u + 1], dm[:, u:u + 1], ACT.Exp).then_inc(corr_ready, 1)

                def probs_hi(r, u):
                    act.wait_ge(pt_ready, r * NT + u + 1)
                    act.wait_ge(pv_ready, r * NT + u - 1)
                    act.copy(pThi[:, u % 2], ps[:, PT + u % 2]).then_inc(pthi_ready, 1)

                def step(r):
                    for u in range(NT + 1):
                        if u < NT:
                            probs(r, u)
                        for k in TURNS.get(u, ()):
                            context_hi(r + k[0], *k[1:])
                        if u >= 1:
                            probs_hi(r, u - 1)

                for g in range(DC):
                    context_hi(1, 0, g)
                taken(act, step)

            @block.vector
            def _(dve):
                dve.wait_ge(state_set, 3)
                dve.sem_inc(tlo_ready, B * DC)
                dve.sem_inc(score_read, NT)
                dve.sem_inc(m_step, 2 * NT)
                dve.sem_inc(nb_ready, 2 * NT)
                dve.sem_inc(ptlo_ready, NT)
                dve.sem_inc(acc_done, NT)
                dve.sem_inc(l_done, NT)

                def context_lo(r, s, g):
                    dve.wait_ge(thi_ready, r * B * DC + s * DC + g + 1)
                    dve.tensor_tensor(cTlo[:, s, g], ps[:, TURN + g % 2], cThi[:, s, g].bitcast(F32),
                                      ALU.subtract).then_inc(tlo_ready, 1)

                def row_max(r, u):
                    if u == 0:
                        dve.wait_ge(bias_ready, r + 1)
                        dve.wait_ge(corr_ready, r * NT)
                    dve.wait_ge(score_ready, r * NT + u + 1)
                    dve.wait_ge(pt_ready, r * NT + u - 1)
                    apart(dve, T["waited"])
                    dve.tensor_tensor_reduce(out=p[:, u % 2], in0=ps[:, SCORE + u % 2], in1=bias[:, u % QT],
                                             scale=1.0, scalar=LOWEST, op0=ALU.add, op1=ALU.max,
                                             accum_out=rmax[:, u:u + 1]).then_inc(score_read, 1)
                    dve.wait_ge(score_read, r * NT + u + 1)
                    dve.scalar_tensor_tensor(out=mnew[:, u:u + 1], in0=rmax[:, u:u + 1], scalar=c[:, u:u + 1],
                                             in1=m_run[:, u:u + 1], op0=ALU.add, op1=ALU.max).then_inc(m_step, 1)
                    dve.wait_ge(m_step, r * 2 * NT + 2 * u + 1)
                    dve.tensor_tensor(nb[:, u:u + 1], c[:, u:u + 1], mnew[:, u:u + 1], ALU.subtract).then_inc(nb_ready, 1)
                    dve.tensor_tensor(dm[:, u:u + 1], m_run[:, u:u + 1], mnew[:, u:u + 1],
                                      ALU.subtract).then_inc(nb_ready, 1)
                    dve.wait_ge(nb_ready, r * 2 * NT + 2 * u + 2)
                    dve.tensor_copy(m_run[:, u:u + 1], mnew[:, u:u + 1]).then_inc(m_step, 1)

                def probs_lo(r, u):
                    dve.wait_ge(pthi_ready, r * NT + u + 1)
                    dve.tensor_tensor(pTlo[:, u % 2], ps[:, PT + u % 2], pThi[:, u % 2].bitcast(F32),
                                      ALU.subtract).then_inc(ptlo_ready, 1)

                def accumulate(r, u):
                    dve.wait_ge(corr_ready, r * NT + u + 1)
                    dve.wait_ge(p_ready, r * NT + u + 1)
                    dve.scalar_tensor_tensor(out=l_run[:, u:u + 1], in0=l_run[:, u:u + 1], scalar=corr[:, u:u + 1],
                                             in1=rsum[:, u:u + 1], op0=ALU.mult, op1=ALU.add).then_inc(l_done, 1)
                    dve.wait_ge(pv_ready, r * NT + u + 1)
                    dve.scalar_tensor_tensor(out=acc[:, u], in0=acc[:, u], scalar=corr[:, u:u + 1],
                                             in1=ps[:, PV + u % 2], op0=ALU.mult, op1=ALU.add).then_inc(acc_done, 1)

                def step(r):
                    dve.wait_ge(acc_done, r * NT)
                    dve.wait_ge(m_step, r * 2 * NT)
                    for u in range(NT + 2):
                        if u < NT:
                            row_max(r, u)
                        for k in TURNS.get(u, ()):
                            context_lo(r + k[0], *k[1:])
                        if 1 <= u <= NT:
                            probs_lo(r, u - 1)
                        if u >= 2:
                            accumulate(r, u - 2)

                for g in range(DC):
                    context_lo(1, 0, g)
                taken(dve, step)


def latents(nc, T, io):
    with ExitStack() as ctx:
        m = Mem(nc, ctx)
        ps, x, ident, acc = T["ps"], T["x"], T["ident"], T["acc"]
        xn, xnT = T["o"], T["v"]
        aThi, aTlo = m.sb("accT_hi", [P, 2, DC, P], F32R), m.sb("accT_lo", [P, 2, DC, P], F32R)
        lhi, llo = m.sb("lat_hi", [P, 2, B * S], F32R), m.sb("lat_lo", [P, 2, B * S], F32R)
        whi = [m.sb(f"W_{n}_hi", [P, D], F32R) for n in ("uq", "uk", "uv")]
        wlo = [m.sb(f"W_{n}_lo", [P, D], F32R) for n in ("uq", "uk", "uv")]
        seen, lsum, linv, scale = (m.sb(n, [P, NT]) for n in ("seen", "lsum", "linv", "scale"))
        stats, mv = m.sb("stats2", [P, NT, 6]), m.sb("mv2", [P, NT, 2])
        varp, std, rstd = (m.sb(n, [P, NT]) for n in ("varp2", "std2", "rstd2"))

        dve_step = m.sem("c_dve_step")
        a_turned, a_hi, a_lo, v_ready, x_ready = (m.sem(n) for n in ("a_turned", "a_hi", "a_lo", "wv_ready", "x1_ready"))
        var_ready, std_ready, xn_ready = m.sem("var2_ready"), m.sem("std2_ready"), m.sem("xn2_ready")
        x_turned, x_copied = m.sem("x2_turned"), m.sem("x2_copied")
        w_split, l_ready, lhi_ready, llo_ready = (
            m.sem("w_split"), m.sem("lat_ready"), m.sem("lat_hi_ready"), m.sem("lat_lo_ready"))
        val_ready, val_copied = m.sem("val_ready"), m.sem("val_copied")
        qk_ready, qk_hi, qk_lo = m.sem("qk_ready"), m.sem("qk_hi"), m.sem("qk_lo")
        halves = ((0, 0), (1, 0), (0, 1))
        GROUPS = [(which, c, half) for half in range(2) for which in range(2) for c in range(DC)]

        def columns(c_row):
            return xnT[:].rearrange("p t d -> p (t d)").rearrange("p (c r) -> p c r", c=DC)[:, :, c_row * P:(c_row + 1) * P]

        with nc.Block() as block:

            @block.gpsimd
            def _(pool):
                pool.wait_ge(T["weights_in"], T["weights_total"])
                for n, w in enumerate(("uq", "uk", "uv")):
                    pool.tensor_copy(whi[n][:], T[w][:]).then_inc(w_split, 1)
                    pool.wait_ge(w_split, 2 * n + 1)
                    pool.tensor_tensor(wlo[n][:], T[w][:], whi[n][:].bitcast(F32), ALU.subtract).then_inc(w_split, 1)

            @block.scalar
            def _(act):
                def acc_hi(t):
                    act.wait_ge(a_turned, t + 1)
                    if t >= 2:
                        act.wait_ge(v_ready, t - 1)
                    act.copy(aThi[:, t % 2], ps[:, t % 2].rearrange("p (c r) -> p c r", c=DC)).then_inc(a_hi, 1)

                acc_hi(0)
                for t in range(NT + 2):
                    if t + 1 < NT:
                        acc_hi(t + 1)
                    if t < NT:
                        act.wait_ge(var_ready, t + 1)
                        act.activation(std[:, t:t + 1], varp[:, t:t + 1], ACT.Sqrt).then_inc(std_ready, 1)
                    if t >= 2:
                        u = t - 2
                        act.wait_ge(x_turned, u + 1)
                        act.copy(columns(u), ps[:, 4 + u % 2].rearrange("p (c r) -> p c r", c=DC)).then_inc(x_copied, 1)
                for i in range(4):
                    half, which = divmod(i, 2)
                    act.wait_ge(l_ready, i + 1)
                    act.copy(lhi[:, which, half * 512:half * 512 + 512], ps[:, 6 + i % 2]).then_inc(lhi_ready, 1)
                for n, (which, c, half) in enumerate(GROUPS):
                    act.wait_ge(qk_ready, n + 1)
                    act.copy(T["qkT"][which][0][:, c, half * 512:half * 512 + 512], ps[:, n % 4]).then_inc(qk_hi, 1)
                    if n % 2:
                        t = n // 2
                        act.wait_ge(val_ready, t + 1)
                        act.copy(T["v"][:, t], ps[:, 4 + t % 2]).then_inc(val_copied, 1)

            @block.vector
            def _(dve):
                link = chained(dve, dve_step)
                link(dve.tensor_scalar(seen[:], T["m_run"][:], -0.5 * BIG, None, ALU.is_gt))
                link(dve.tensor_tensor(lsum[:], T["l_run"][:], seen[:], ALU.mult))
                link(dve.reciprocal(linv[:], lsum[:]))
                link(dve.tensor_tensor(scale[:], linv[:], seen[:], ALU.mult))

                def acc_lo(t):
                    dve.wait_ge(a_hi, t + 1)
                    dve.tensor_tensor(aTlo[:, t % 2], ps[:, t % 2].rearrange("p (c r) -> p c r", c=DC),
                                      aThi[:, t % 2].bitcast(F32), ALU.subtract).then_inc(a_lo, 1)

                acc_lo(0)
                for t in range(NT + 1):
                    if t + 1 < NT:
                        acc_lo(t + 1)
                    if t < NT:
                        dve.wait_ge(v_ready, t + 1)
                        dve.scalar_tensor_tensor(out=x[:, t], in0=ps[:, 2 + t % 2], scalar=scale[:, t:t + 1], in1=x[:, t],
                                                 op0=ALU.mult, op1=ALU.add).then_inc(x_ready, 1)
                        dve.wait_ge(x_ready, t + 1)
                        link(dve.bn_stats(stats[:, t, :], x[:, t, :]))
                        link(dve.bn_aggr(mv[:, t, :], stats[:, t, :]))
                        dve.tensor_scalar(varp[:, t:t + 1], mv[:, t, 1:2], EPS, None, ALU.add).then_inc(var_ready, 1)
                    if t >= 1:
                        u = t - 1
                        dve.wait_ge(std_ready, u + 1)
                        link(dve.reciprocal(rstd[:, u:u + 1], std[:, u:u + 1]))
                        dve.tensor_scalar(xn[:, u], x[:, u], mv[:, u, 0:1], rstd[:, u:u + 1], ALU.subtract,
                                          ALU.mult).then_inc(xn_ready, 1)
                for i in range(4):
                    half, which = divmod(i, 2)
                    at = slice(half * 512, half * 512 + 512)
                    dve.wait_ge(lhi_ready, i + 1)
                    dve.tensor_tensor(llo[:, which, at], ps[:, 6 + i % 2], lhi[:, which, at].bitcast(F32),
                                      ALU.subtract).then_inc(llo_ready, 1)
                for n, (which, c, half) in enumerate(GROUPS):
                    at = slice(half * 512, half * 512 + 512)
                    dve.wait_ge(qk_hi, n + 1)
                    dve.tensor_tensor(T["qkT"][which][1][:, c, at], ps[:, n % 4], T["qkT"][which][0][:, c, at].bitcast(F32),
                                      ALU.subtract).then_inc(qk_lo, 1)

            @block.tensor
            def _(pe):
                def turn_acc(t):
                    if t >= 2:
                        pe.wait_ge(a_lo, t - 1)
                    for d in range(DC):
                        ins = pe.transpose(ps[:, t % 2, d * P:(d + 1) * P], acc[:, t, d * P:(d + 1) * P], ident[:])
                    ins.then_inc(a_turned, 1)

                def turn_norm(t):
                    pe.wait_ge(xn_ready, t + 1)
                    if t >= 2:
                        pe.wait_ge(x_copied, t - 1)
                    for d in range(DC):
                        ins = pe.transpose(ps[:, 4 + t % 2, d * P:(d + 1) * P], xn[:, t, d * P:(d + 1) * P], ident[:])
                    ins.then_inc(x_turned, 1)

                turn_acc(0)
                for t in range(NT):
                    if t + 1 < NT:
                        turn_acc(t + 1)
                    pe.wait_ge(a_lo, t + 1)
                    if t >= 2:
                        pe.wait_ge(x_ready, t - 1)
                    aT, wv, n = (aThi, aTlo), (T["Wvhi"], T["Wvlo"]), 0
                    for d in range(DC):
                        for a, b in halves:
                            ins = pe.matmul(ps[:, 2 + t % 2], aT[a][:, t % 2, d], wv[b][:, d], start=n == 0,
                                            stop=n == 3 * DC - 1)
                            n += 1
                    ins.then_inc(v_ready, 1)
                    if t >= 2:
                        turn_norm(t - 2)
                turn_norm(NT - 2)
                turn_norm(NT - 1)
                pe.wait_ge(T["weights_in"], T["weights_total"])
                for i in range(4):
                    half, which = divmod(i, 2)
                    pe.wait_ge(x_copied, (half + 1) * QT)
                    if i >= 2:
                        pe.wait_ge(llo_ready, i - 1)
                    for d in range(DC):
                        at = slice(d * B * S + half * 512, d * B * S + half * 512 + 512)
                        ins = pe.matmul(ps[:, 6 + i % 2], T["dqkv"][:, which, d], xnT[:].rearrange("p t d -> p (t d)")[:, at],
                                        start=d == 0, stop=d == DC - 1)
                    ins.then_inc(l_ready, 1)
                pe.wait_ge(w_split, 6)
                l = (lhi, llo)
                for n, (which, c, half) in enumerate(GROUPS):
                    pe.wait_ge(llo_ready, 2 * half + which + 1)
                    if n >= 4:
                        pe.wait_ge(qk_lo, n - 3)
                    for k, (a, b) in enumerate(halves):
                        ins = pe.matmul(ps[:, n % 4], (whi, wlo)[a][which][:, c * P:(c + 1) * P],
                                        l[b][:, which, half * 512:half * 512 + 512], start=k == 0, stop=k == 2)
                    ins.then_inc(qk_ready, 1)
                    if n % 2:
                        t = n // 2
                        pe.wait_ge(llo_ready, 2 + 2 * (t // QT))
                        if t >= 2:
                            pe.wait_ge(val_copied, t - 1)
                        for k, (a, b) in enumerate(halves):
                            ins = pe.matmul(ps[:, 4 + t % 2], l[a][:, 1, t * P:(t + 1) * P], (whi, wlo)[b][2][:],
                                            start=k == 0, stop=k == 2)
                        ins.then_inc(val_ready, 1)


def heads(nc, T, io):
    HC = P // DK
    STEPS = NH // HC
    SC = float(DK) ** -0.5
    AHEAD = 2
    UNITS = [(b, g) for b in range(B) for g in range(3)]
    TILES = ((0,), (1,), (2, 3))
    NU = len(UNITS)
    LOADS = 6 * 16
    with ExitStack() as ctx:
        m = Mem(nc, ctx)
        ps, ident = T["ps"], T["ident"]
        q3 = [m.sb(f"q3_{j}", [3 * DK + 2, B * S], F32R) for j in range(HC)]
        k3 = [m.sb(f"k3_{j}", [3 * DK + 2, B * S], F32R) for j in range(HC)]
        closed_r, ident_r = T["closed"], T["ident_r"]
        pT = [[m.sb(f"head_probsT{b}{g}", [P, (512, 384, 384)[g]]) for g in range(3)] for b in range(B)]
        rmax = m.sb("head_max", [P, 2, NT])
        mrow = [[m.sb(f"max_row_{h}{j}", [NT, P], F32R) for h in ("hi", "lo")] for j in range(2)]
        vh = m.sb("head_v", [P, 2, NT, DK + 1])
        wraw, same = T["Wo"], m.sb("same", [P, HC * NT])
        oT = T["acc"][:].rearrange("p t d -> p (t d)").rearrange("p (c r) -> p c r", c=DC)
        sums_of = T["o"][:].rearrange("p t d -> p (t d)").rearrange("p (c r) -> p c r", c=DC)

        pool_step, const_set, wo_in = m.sem("d_pool_step"), m.sem("head_consts"), m.sem("wo_in")
        ones_set, sums_in = m.sem("k_ones_set"), m.sem("sums_in")
        qk_in = [m.sem(f"qk_in{j}") for j in range(HC)]
        max_in = [m.sem(f"max_in{j}") for j in range(HC)]
        row_ready, row_read, max_turned, max_split = (m.sem(n) for n in ("row_ready", "row_read", "max_turned", "max_split"))
        unit_ready, p_ready, v_set = m.sem("unit_ready"), m.sem("hp_ready"), m.sem("head_v_set")
        pv_ready, o_copied, l_read = m.sem("hpv_ready"), m.sem("ho_copied"), m.sem("hl_read")
        ROW, UNIT, TURN, PV = 0, 2, 5, 6

        def chunk(r, k):
            return bass.ds(r + (k // HC - 1), 1)

        def steps(eng, body):
            with eng.Fori(1, STEPS) as r:
                body(r, 2 * HC)
            body(STEPS, HC)

        with nc.Block() as block:

            @block.sync
            def _(sp):
                order = ((0, 0, 1), (0, 1, 0))

                def load(r, k):
                    j = k % HC
                    sp.wait_ge(unit_ready, r * (HC * NU) + (k - HC + 1) * NU)
                    apart(sp, T["waited"])
                    for which in range(2):
                        for i in range(3):
                            src = T["qkT"][which][order[which][i]][j * DK:(j + 1) * DK, chunk(r, k)]
                            sp.dma_start((q3, k3)[which][j][i * DK:(i + 1) * DK].bitcast(F32),
                                         src.rearrange("p a b -> p (a b)").bitcast(F32)).then_inc(qk_in[j], 16)

                def max_rows(r, k):
                    j = k % HC
                    sp.wait_ge(max_split, r * (2 * HC) + 2 * (k + 1))
                    apart(sp, T["waited"])
                    for h in range(2):
                        sp.dma_start(q3[j][3 * DK + h:3 * DK + h + 1].bitcast(F32), mrow[k % 2][h][:].bitcast(F32)).then_inc(max_in[j], 16)

                for k in range(AHEAD + 1):
                    load(1, k)
                sp.dma_start(wraw[:], io["Wo"].rearrange("(c p) e -> p c e", p=P)).then_inc(wo_in, 16)
                for k in range(AHEAD):
                    max_rows(1, k)

                def body(r, last):
                    for k in range(HC):
                        if k + AHEAD + 1 < last:
                            load(r, k + AHEAD + 1)
                        if k + AHEAD < last:
                            max_rows(r, k + AHEAD)

                steps(sp, body)
                for c in range(STEPS):
                    for k in range(HC):
                        sp.wait_ge(l_read, (c + 1) * (B * HC) + (k + 1) * B)
                        at = c * HC * NT + k * NT
                        sp.dma_start(T["sums"][at:at + NT], sums_of[k * DK:k * DK + 1, c]).then_inc(sums_in, 16)
                sp.wait_ge(sums_in, 16 * NH)

            @block.gpsimd
            def _(pool):
                link = chained(pool, pool_step)
                pool.sem_inc(v_set, HC)
                pool.memset(vh[:, :, :, DK:DK + 1], 1.0).then_inc(const_set, 1)

                def value(r, k):
                    pool.wait_ge(pv_ready, r * (HC * NU) + (k - 1) * NU)
                    apart(pool, T["waited"])
                    at = r * P + (k * DK - P)
                    pool.tensor_copy(vh[:, k % 2, :, 0:DK], T["v"][:, :, bass.ds(at, DK)]).then_inc(v_set, 1)

                for k in range(AHEAD):
                    value(1, k)
                pool.wait_ge(v_set, HC + AHEAD)
                pool.wait_ge(wo_in, 16)
                link(pool.tensor_copy(T["Wohi"][:], wraw[:]))
                link(pool.tensor_tensor(T["Wolo"][:], wraw[:], T["Wohi"][:].bitcast(F32), ALU.subtract))
                link(pool.tensor_copy(same[:], ident[:, 0:HC * NT]))
                for c in range(1, STEPS):
                    link(pool.tensor_tensor(same[:], same[:], ident[:, c * HC * NT:(c + 1) * HC * NT], ALU.add))
                link(pool.tensor_copy(T["place"][:].rearrange("p t (k e) -> p t k e", e=DK),
                                      same[:].rearrange("p (k t) -> p t k", t=NT).unsqueeze(3).to_broadcast([P, NT, HC, DK])))

                def body(r, last):
                    for k in range(HC):
                        if k + AHEAD < last:
                            value(r, k + AHEAD)

                steps(pool, body)

            @block.tensor
            def _(pe):
                pe.sem_inc(row_ready, HC * NT)
                pe.sem_inc(max_turned, HC)
                pe.sem_inc(unit_ready, HC * NU)
                pe.sem_inc(pv_ready, HC * NU)
                
                def row(r, k, t):
                    j, b, q = k % HC, t // QT, t % QT
                    if t == 0:
                        pe.wait_ge(qk_in[j], r * LOADS + (k // HC) * LOADS)
                    pe.wait_ge(row_read, r * (HC * NT) + (k * NT + t - 1))
                    bank = ps[:, ROW + t % 2]
                    pe.matmul(bank[:, 0:(q + 1) * P], q3[j][0:3 * DK, t * P:(t + 1) * P],
                              k3[j][0:3 * DK, b * S:b * S + (q + 1) * P], start=True, stop=False)
                    pe.matmul(bank[:, q * P:(q + 1) * P], closed_r[:, 0], ident_r[:], start=False,
                              stop=True).then_inc(row_ready, 1)

                def turn_max(r, k):
                    pe.wait_ge(row_read, r * (HC * NT) + (k + 1) * NT)
                    pe.wait_ge(max_split, r * (2 * HC) + 2 * k)
                    pe.transpose(ps[0:NT, TURN, 0:P], rmax[:, k % 2], ident[:]).then_inc(max_turned, 1)

                def unit(r, k, v):
                    k, v = k + v // NU, v % NU
                    j, (b, g) = k % HC, UNITS[v]
                    if v == 0:
                        pe.wait_ge(max_in[j], r * 32 + (k // HC) * 32)
                    pe.wait_ge(p_ready, r * (HC * NU) + (k * NU + v - 2))
                    col = 0
                    for kt in TILES[g]:
                        n, k0 = S - kt * P, b * S + kt * P
                        pe.matmul(ps[:, UNIT + g, col:col + n], k3[j][:, k0:k0 + P], q3[j][:, k0:k0 + n], start=True, stop=False)
                        ins = pe.matmul(ps[:, UNIT + g, col:col + P], closed_r[:, 1], ident_r[:], start=False, stop=True)
                        col += n
                    ins.then_inc(unit_ready, 1)

                def value(r, k, v):
                    b, g = UNITS[v]
                    pe.wait_ge(p_ready, r * (HC * NU) + (k * NU + v + 1))
                    if g == 0:
                        if b == 0:
                            pe.wait_ge(v_set, r * HC + (k + 1))
                        pe.wait_ge(o_copied, r * (B * HC) + (k - 1) * B + b + 1)
                        pe.wait_ge(l_read, r * (B * HC) + (k - 1) * B + b + 1)
                    col = 0
                    for kt in TILES[g]:
                        n = S - kt * P
                        ins = pe.matmul(ps[0:DK + 1, PV + b, kt * P:S], vh[:, k % 2, b * QT + kt], pT[b][g][:, col:col + n],
                                        start=kt == 0, stop=kt == QT - 1)
                        col += n
                    ins.then_inc(pv_ready, 1)

                for k in range(AHEAD):
                    for t in range(NT):
                        row(1, k, t)
                    turn_max(1, k)
                pe.wait_ge(ones_set, HC)
                pe.wait_ge(const_set, 1)
                unit(1, 0, 0)
                unit(1, 0, 1)

                def body(r, last):
                    for k in range(HC):
                        for v in range(NU):
                            if k < HC - 1 or v + 2 < NU or last > HC:
                                unit(r, k, v + 2)
                            if k + AHEAD < last:
                                for t in ((0, 1), (2, 3), (4, 5), (6,), (7,), ())[v]:
                                    row(r, k + AHEAD, t)
                            value(r, k, v)
                        if k + AHEAD < last:
                            turn_max(r, k + AHEAD)

                steps(pe, body)

            @block.scalar
            def _(act):
                act.sem_inc(p_ready, HC * NU)
                act.sem_inc(o_copied, HC * B)

                def probs(r, k, v):
                    k, v = k + v // NU, v % NU
                    b, g = UNITS[v]
                    n = sum(S - kt * P for kt in TILES[g])
                    act.wait_ge(unit_ready, r * (HC * NU) + (k * NU + v + 1))
                    act.wait_ge(pv_ready, r * (HC * NU) + ((k - 1) * NU + v + 1))
                    act.activation(pT[b][g][:, 0:n], ps[:, UNIT + g, 0:n], ACT.Exp, scale=SC).then_inc(p_ready, 1)

                def output(r, k, b):
                    act.wait_ge(pv_ready, r * (HC * NU) + (k * NU + (b + 1) * 3))
                    rows = slice(k * DK, (k + 1) * DK)
                    act.copy(oT[rows, chunk(r, k), b * S:(b + 1) * S], ps[0:DK, PV + b].unsqueeze(1)).then_inc(o_copied, 1)

                for j in range(HC):
                    act.copy(k3[j][3 * DK:3 * DK + 2].rearrange("a (t p) -> a t p", p=P),
                             T["ones"][3 * DK:3 * DK + 2].unsqueeze(1).to_broadcast([2, NT, P])).then_inc(ones_set, 1)
                probs(1, 0, 0)
                probs(1, 0, 1)

                def body(r, last):
                    for k in range(HC):
                        for v in range(NU):
                            if k < HC - 1 or v + 2 < NU or last > HC:
                                probs(r, k, v + 2)
                            if v == 3:
                                output(r, k, 0)
                        output(r, k, 1)

                steps(act, body)

            @block.vector
            def _(dve):
                dve.sem_inc(row_read, HC * NT)
                dve.sem_inc(max_split, 2 * HC)
                dve.sem_inc(l_read, HC * B)

                def row_max(r, k, t):
                    n = (t % QT + 1) * P
                    dve.wait_ge(row_ready, r * (HC * NT) + (k * NT + t + 1))
                    dve.tensor_reduce(rmax[:, k % 2, t:t + 1], ps[:, ROW + t % 2, 0:n], AX.X, ALU.max).then_inc(row_read, 1)

                def split_max(r, k):
                    dve.wait_ge(max_turned, r * HC + (k + 1))
                    dve.tensor_scalar(mrow[k % 2][0][:], ps[0:NT, TURN, 0:P], -1.0, None, ALU.mult).then_inc(max_split, 1)
                    dve.wait_ge(max_split, r * (2 * HC) + 2 * k + 1)
                    dve.scalar_tensor_tensor(out=mrow[k % 2][1][:], in0=ps[0:NT, TURN, 0:P], scalar=-1.0,
                                             in1=mrow[k % 2][0][:].bitcast(F32), op0=ALU.mult, op1=ALU.subtract).then_inc(max_split, 1)

                def sums(r, k, b):
                    dve.wait_ge(pv_ready, r * (HC * NU) + (k * NU + (b + 1) * 3))
                    dve.tensor_copy(sums_of[k * DK:k * DK + 1, chunk(r, k), b * S:(b + 1) * S],
                                    ps[DK:DK + 1, PV + b].unsqueeze(1)).then_inc(l_read, 1)

                for k in range(AHEAD):
                    for t in range(NT):
                        row_max(1, k, t)
                    split_max(1, k)

                def body(r, last):
                    for k in range(HC):
                        for t in range(NT):
                            if k + AHEAD < last:
                                row_max(r, k + AHEAD, t)
                            if t == 5:
                                sums(r, k, 0)
                        sums(r, k, 1)
                        if k + AHEAD < last:
                            split_max(r, k + AHEAD)

                steps(dve, body)


def experts(nc, T, io):
    Q3 = 3 * H
    with ExitStack() as ctx:
        m = Mem(nc, ctx)
        ps, x, ident, w, y = T["ps"], T["x"], T["ident"], T["w"], T["y"]
        oT = T["acc"][:].rearrange("p t d -> p (t d)").rearrange("p (c r) -> p c r", c=DC)
        inv, chunked = m.sb("sums_inv", [P, P]), m.sb("sums_inv_chunked", [P, DC, P])
        chunkh = [m.sb(f"sums_inv_{h}", [P, DC, P], F32R) for h in ("hi", "lo")]
        RING = 3
        oThi, oTlo = m.sb("oT_hi", [P, RING, DC, P], F32R), m.sb("oT_lo", [P, RING, DC, P], F32R)
        stats, mv = m.sb("stats3", [P, NT, 6]), m.sb("mv3", [P, NT, 2])
        varp, std, rstd = (m.sb(n, [P, NT]) for n in ("varp3", "std3", "rstd3"))
        xn = m.sb("xn3", [P, 2, D])
        raw, oraw = m.sb("expert_raw", [P, 2, DC, 3, H]), m.sb("expert_out_raw", [P, 2, D])
        whi = [m.sb("expert_hi", [P, DC, Q3], F32R)[:], T["Wohi"][:, :, 0:Q3]]
        wlo = [m.sb("expert_lo", [P, DC, Q3], F32R)[:], T["Wolo"][:, :, 0:Q3]]
        square = chunked[:].rearrange("p c r -> p (c r)")
        sim, simsq = m.sb("sim", [P, DC, E]), m.sb("simsq", [P, DC, E])
        simh = m.sb("sim_halves", [P, DC, 2, E], F32R)
        gates, egate, sig, norm_e, inv_e = (m.sb(n, [P, E]) for n in ("gates", "egate", "sig", "norm_e", "inv_e"))
        rowsq, norm_n, inv_n = (m.sb(n, [P, NT]) for n in ("rowsq", "norm_n", "inv_n"))
        rev_i, rev = m.sb("rev_i", [P, E], I32), m.sb("rev", [P, E])
        L, L2, key, sel1, sel2, put, on, g, ex = (m.sb(n, [P, NT, E]) for n in (
            "logits", "logits2", "key", "sel1", "sel2", "put", "on", "gated", "gate_exp"))
        top, kmax, idle, gmax, gsum, ginv = (m.sb(n, [P, NT]) for n in ("top", "kmax", "idle", "gmax", "gsum", "ginv"))

        inv_ready, spread, o_scaled, o_hi, o_lo = (m.sem(n) for n in ("inv_ready", "inv_spread", "o_scaled", "o_hi", "o_lo"))
        out_ready, x_ready, var_ready, std_ready, xn_ready = (m.sem(n) for n in (
            "wo_ready", "x2_ready", "var3_ready", "std3_ready", "xn3_ready"))
        g_in, rev_set, dve_step = m.sem("gate_in"), m.sem("rev_set"), m.sem("e_dve_step")
        sq_ready, sim_split, y_zero = m.sem("sq_ready"), m.sem("sim_split"), m.sem("y_zero")
        turned, hi_ready, lo_ready = m.sem("xn3_turned"), m.sem("xn3_hi"), m.sem("xn3_lo")
        simsq_ready, colsq_ready, logits_ready = m.sem("simsq_ready"), m.sem("colsq_ready"), m.sem("logits_ready")
        norm_ready, logits_read, e_ready, x_asked, x_exp = (m.sem(n) for n in (
            "norm_ready", "logits_read", "egate_ready", "gexp_asked", "gexp_ready"))
        raw_in = [m.sem(f"expert_in{j}") for j in range(2)]
        split = [m.sem(f"expert_split{j}") for j in range(2)]
        y_ready, y_added = m.sem("y_ready"), m.sem("y_added")
        U = 2 * NT
        TURN, LOGITS, COLSQ, SPREAD, OUT = 0, 2, 3, 4, 6
        halves = ((0, 0), (1, 0), (0, 1))

        def tile(t):
            return slice(t * P, (t + 1) * P)

        def rows(a):
            return a[:].unsqueeze(2).to_broadcast([P, NT, E])

        def cols(a):
            return a[:].unsqueeze(1).to_broadcast([P, NT, E])

        with nc.Block() as block:

            @block.sync
            def _(sp):
                for j in range(2):
                    sp.sem_inc(split[j], 4)
                sp.dma_start(sim[:], io["sim"].rearrange("(c p) e -> p c e", p=P)).then_inc(g_in, 16)
                sp.dma_start(gates[:], io["gates"].rearrange("(a e) -> a e", a=1).to_broadcast([P, E])).then_inc(g_in, 16)
                qkv = [io[n].rearrange("e (c p) h -> e p c h", p=P) for n in ("qp", "kp", "vp")]
                with sp.Fori(1, E // 2 + 1) as r:
                    for j in range(2):
                        e = r * 2 + (j - 2)
                        sp.wait_ge(split[j], r * 4)
                        apart(sp, T["waited"])
                        for n in range(3):
                            sp.dma_start(raw[:, j, :, n], qkv[n][e]).then_inc(raw_in[j], 16)
                        sp.dma_start(oraw[:, j], io["op"][e]).then_inc(raw_in[j], 16)

            @block.gpsimd
            def _(pool):
                pool.iota(rev_i[:], pattern=[[-1, E]], base=E, channel_multiplier=0).then_inc(rev_set, 1)
                pool.wait_ge(rev_set, 1)
                pool.tensor_copy(rev[:], rev_i[:]).then_inc(rev_set, 1)
                pool.wait_ge(g_in, 32)
                pool.tensor_tensor(simsq[:], sim[:], sim[:], ALU.mult).then_inc(simsq_ready, 1)
                pool.tensor_copy(simh[:, :, 0], sim[:]).then_inc(sim_split, 1)
                pool.wait_ge(sim_split, 1)
                pool.tensor_tensor(simh[:, :, 1], sim[:], simh[:, :, 0].bitcast(F32), ALU.subtract).then_inc(sim_split, 1)
                with pool.Fori(1, E // 2 + 1) as r:
                    for j in range(2):
                        e = r * 2 + (j - 2)
                        if j == 1:
                            pool.wait_ge(out_ready, NT)
                        pool.wait_ge(raw_in[j], r * 64)
                        pool.wait_ge(y_ready, r * U + (j * NT - NT))
                        apart(pool, T["waited"])
                        raw_j = raw[:, j].rearrange("p c n h -> p c (n h)")
                        pool.tensor_copy(whi[j], raw_j).then_inc(split[j], 1)
                        pool.wait_ge(split[j], r * 4 + 1)
                        pool.tensor_tensor(wlo[j], raw_j, whi[j].bitcast(F32), ALU.subtract).then_inc(split[j], 1)
                        pool.tensor_copy(T["ohi"][:, bass.ds(e, 1)], oraw[:, j:j + 1]).then_inc(split[j], 1)
                        pool.wait_ge(split[j], r * 4 + 3)
                        pool.tensor_tensor(T["olo"][:, bass.ds(e, 1)], oraw[:, j:j + 1],
                                           T["ohi"][:, bass.ds(e, 1)].bitcast(F32), ALU.subtract).then_inc(split[j], 1)

            @block.scalar
            def _(act):
                def output_hi(t):
                    act.wait_ge(o_scaled, t + 1)
                    if t >= RING:
                        act.wait_ge(out_ready, t - RING + 1)
                    act.copy(oThi[:, t % RING], oT[:, :, tile(t)]).then_inc(o_hi, 1)

                def deviation(t):
                    act.wait_ge(var_ready, t + 1)
                    act.activation(std[:, t:t + 1], varp[:, t:t + 1], ACT.Sqrt).then_inc(std_ready, 1)

                def norm_hi(t):
                    act.wait_ge(xn_ready, t + 1)
                    if t >= 1:
                        act.wait_ge(sq_ready, t)
                    act.activation(square, xn[:, t % 2], ACT.Square, accum_out=rowsq[:, t:t + 1]).then_inc(sq_ready, 1)
                    act.wait_ge(turned, t + 1)
                    act.copy(T["xnhi"][:, :, tile(t)], ps[:, TURN + t % 2].rearrange("p (c r) -> p c r", c=DC)).then_inc(hi_ready, 1)

                output_hi(0)
                output_hi(1)
                for t in range(NT + 1):
                    if t + 2 < NT:
                        output_hi(t + 2)
                    if t < NT:
                        deviation(t)
                    if t >= 1:
                        norm_hi(t - 1)
                act.wait_ge(sq_ready, NT)
                act.activation(norm_n[:], rowsq[:], ACT.Sqrt).then_inc(norm_ready, 1)
                act.wait_ge(colsq_ready, 1)
                act.activation(norm_e[:], ps[:, COLSQ, 0:E], ACT.Sqrt).then_inc(norm_ready, 1)
                act.wait_ge(g_in, 32)
                act.activation(egate[:], gates[:], ACT.Exp, scale=-1.0).then_inc(e_ready, 1)
                act.wait_ge(x_asked, 1)
                act.activation(ex[:], key[:], ACT.Exp).then_inc(x_exp, 1)

            @block.vector
            def _(dve):
                link = chained(dve, dve_step)
                dve.sem_inc(y_added, U)
                dve.memset(chunked[:], 0.0).then_inc(inv_ready, 1)
                dve.reciprocal(inv[:], T["sums"][:]).then_inc(inv_ready, 1)
                dve.wait_ge(inv_ready, 2)
                HR = P // DC
                for c in range(DC):
                    dve.tensor_copy(chunked[c * HR:(c + 1) * HR, c], inv[c * HR:(c + 1) * HR]).then_inc(inv_ready, 1)
                dve.wait_ge(inv_ready, 2 + DC)
                dve.tensor_copy(chunkh[0][:], chunked[:]).then_inc(inv_ready, 1)
                dve.wait_ge(inv_ready, 3 + DC)
                dve.tensor_tensor(chunkh[1][:], chunked[:], chunkh[0][:].bitcast(F32), ALU.subtract).then_inc(inv_ready, 1)

                def scaled(t):
                    dve.wait_ge(spread, t + 1)
                    dve.tensor_tensor(oT[:, :, tile(t)], oT[:, :, tile(t)], ps[:, SPREAD + t % 2].rearrange("p (c r) -> p c r", c=DC),
                                      ALU.mult).then_inc(o_scaled, 1)

                def output_lo(t):
                    dve.wait_ge(o_hi, t + 1)
                    dve.tensor_tensor(oTlo[:, t % RING], oT[:, :, tile(t)], oThi[:, t % RING].bitcast(F32),
                                      ALU.subtract).then_inc(o_lo, 1)

                def add(t):
                    dve.wait_ge(out_ready, t + 1)
                    dve.tensor_tensor(x[:, t], ps[:, OUT + t % 2], x[:, t], ALU.add).then_inc(x_ready, 1)
                    dve.wait_ge(x_ready, t + 1)
                    link(dve.bn_stats(stats[:, t, :], x[:, t, :]))
                    link(dve.bn_aggr(mv[:, t, :], stats[:, t, :]))
                    dve.tensor_scalar(varp[:, t:t + 1], mv[:, t, 1:2], EPS, None, ALU.add).then_inc(var_ready, 1)

                def normed(t):
                    dve.wait_ge(std_ready, t + 1)
                    link(dve.reciprocal(rstd[:, t:t + 1], std[:, t:t + 1]))
                    if t >= 2:
                        dve.wait_ge(turned, t - 1)
                        dve.wait_ge(sq_ready, t - 1)
                    dve.tensor_scalar(xn[:, t % 2], x[:, t], mv[:, t, 0:1], rstd[:, t:t + 1], ALU.subtract,
                                      ALU.mult).then_inc(xn_ready, 1)

                def norm_lo(t):
                    dve.wait_ge(hi_ready, t + 1)
                    dve.tensor_tensor(T["xnlo"][:, :, tile(t)], ps[:, TURN + t % 2].rearrange("p (c r) -> p c r", c=DC),
                                      T["xnhi"][:, :, tile(t)].bitcast(F32), ALU.subtract).then_inc(lo_ready, 1)

                scaled(0)
                scaled(1)
                output_lo(0)
                scaled(2)
                output_lo(1)
                for t in range(NT + 2):
                    if t + 3 < NT:
                        scaled(t + 3)
                    if t + 2 < NT:
                        output_lo(t + 2)
                    if t < NT:
                        add(t)
                    if 1 <= t <= NT:
                        normed(t - 1)
                    if t >= 2:
                        norm_lo(t - 2)
                dve.memset(y, 0.0).then_inc(y_zero, 1)
                dve.wait_ge(norm_ready, 2)
                link(dve.tensor_scalar(norm_n[:], norm_n[:], 1e-12, None, ALU.max))
                link(dve.reciprocal(inv_n[:], norm_n[:]))
                link(dve.tensor_scalar(norm_e[:], norm_e[:], 1e-12, None, ALU.max))
                link(dve.reciprocal(inv_e[:], norm_e[:]))
                dve.wait_ge(e_ready, 1)
                link(dve.tensor_scalar(egate[:], egate[:], 1.0, None, ALU.add))
                link(dve.reciprocal(sig[:], egate[:]))
                dve.wait_ge(logits_ready, 1)
                sides = ps[:, LOGITS, 0:2 * NT * E].rearrange("p (t a e) -> p t a e", t=NT, a=2)
                link(dve.tensor_copy(L2[:], sides[:, :, 1]))
                link(dve.tensor_tensor(L[:], sides[:, :, 0], L2[:], ALU.add))
                dve.tensor_tensor(L[:], L[:], rows(inv_n), ALU.mult).then_inc(logits_read, 1)
                dve.wait_ge(logits_read, 1)
                link(dve.tensor_tensor(L[:], L[:], cols(inv_e), ALU.mult))
                link(dve.tensor_tensor(L[:], L[:], cols(sig), ALU.subtract))
                dve.wait_ge(rev_set, 2)
                for logits, sel in ((L, sel1), (L2, sel2)):
                    link(dve.tensor_reduce(top[:], logits[:], AX.X, ALU.max))
                    link(dve.tensor_tensor(key[:], logits[:], rows(top), ALU.is_equal))
                    link(dve.tensor_tensor(key[:], key[:], cols(rev), ALU.mult))
                    if sel is sel1:
                        link(dve.tensor_scalar(idle[:], top[:], 0.0, None, ALU.is_le))
                    link(dve.tensor_reduce(kmax[:], key[:], AX.X, ALU.max))
                    link(dve.tensor_tensor(sel[:], key[:], rows(kmax), ALU.is_equal))
                    if sel is sel1:
                        link(dve.scalar_tensor_tensor(out=L2[:], in0=sel1[:], scalar=-BIG, in1=L[:], op0=ALU.mult,
                                                      op1=ALU.add))
                link(dve.tensor_tensor(put[:], sel1[:], sel2[:], ALU.add))
                link(dve.tensor_tensor(put[:], put[:], rows(idle), ALU.mult))
                link(dve.tensor_scalar(on[:], L[:], 0.0, None, ALU.is_gt))
                link(dve.tensor_tensor(on[:], on[:], put[:], ALU.max))
                link(dve.tensor_scalar(g[:], L[:], 0.0, None, ALU.max))
                link(dve.tensor_scalar(on[:], on[:], BIG, -BIG, ALU.mult, ALU.add))
                link(dve.tensor_tensor(g[:], g[:], on[:], ALU.add))
                link(dve.tensor_reduce(gmax[:], g[:], AX.X, ALU.max))
                dve.tensor_tensor(key[:], g[:], rows(gmax), ALU.subtract).then_inc(x_asked, 1)
                dve.wait_ge(x_exp, 1)
                link(dve.tensor_reduce(gsum[:], ex[:], AX.X, ALU.add))
                link(dve.reciprocal(ginv[:], gsum[:]))
                link(dve.tensor_tensor(w[:], ex[:], rows(ginv), ALU.mult))
                dve.wait_ge(y_zero, 1)
                with dve.Fori(1, E // 2 + 1) as r:
                    for n in range(U):
                        j, t = divmod(n, NT)
                        dve.wait_ge(y_added, r * U + (n + 1 - NT))
                        dve.wait_ge(y_ready, r * U + (n + 1))
                        dve.scalar_tensor_tensor(out=y[:, t], in0=ps[:, (t + 4) % 8, 0:Q3], scalar=w[:, t, bass.ds(r * 2 + (j - 2), 1)],
                                                 in1=y[:, t], op0=ALU.mult, op1=ALU.add).then_inc(y_added, 1)

            @block.tensor
            def _(pe):
                pe.sem_inc(y_ready, U)

                def spread_inv(t):
                    if t >= 2:
                        pe.wait_ge(o_scaled, t - 1)
                    for h in range(2):
                        ins = pe.matmul(ps[:, SPREAD + t % 2], T["place"][:, t], chunkh[h][:].rearrange("p c r -> p (c r)"),
                                        start=h == 0, stop=h == 1)
                    ins.then_inc(spread, 1)

                def output(t):
                    pe.wait_ge(o_lo, t + 1)
                    if t >= 2:
                        pe.wait_ge(x_ready, t - 1)
                    o, wo, n = (oThi, oTlo), (T["Wohi"], T["Wolo"]), 0
                    for d in range(DC):
                        for a, b in halves:
                            ins = pe.matmul(ps[:, OUT + t % 2], o[a][:, t % RING, d], wo[b][:, d], start=n == 0,
                                            stop=n == 3 * DC - 1)
                            n += 1
                    ins.then_inc(out_ready, 1)

                def turn(t):
                    pe.wait_ge(xn_ready, t + 1)
                    if t >= 2:
                        pe.wait_ge(lo_ready, t - 1)
                    for d in range(DC):
                        ins = pe.transpose(ps[:, TURN + t % 2, d * P:(d + 1) * P], xn[:, t % 2, d * P:(d + 1) * P], ident[:])
                    ins.then_inc(turned, 1)

                def logits(t):
                    pe.wait_ge(lo_ready, t + 1)
                    for d in range(DC):
                        pe.matmul(ps[:, LOGITS, 2 * t * E:2 * (t + 1) * E], T["xnhi"][:, d, tile(t)],
                                  simh[:, d].rearrange("p a e -> p (a e)"), start=d == 0, stop=False)
                        ins = pe.matmul(ps[:, LOGITS, 2 * t * E:(2 * t + 1) * E], T["xnlo"][:, d, tile(t)], simh[:, d, 0],
                                        start=False, stop=d == DC - 1)
                    return ins

                pe.wait_ge(inv_ready, 4 + DC)
                spread_inv(0)
                spread_inv(1)
                pe.wait_ge(simsq_ready, 1)
                for d in range(DC):
                    ins = pe.matmul(ps[:, COLSQ, 0:E], T["ones"][:], simsq[:, d], start=d == 0, stop=d == DC - 1)
                ins.then_inc(colsq_ready, 1)
                pe.wait_ge(sim_split, 2)
                spread_inv(2)
                for t in range(NT + 3):
                    if t + 3 < NT:
                        spread_inv(t + 3)
                    if t < NT:
                        output(t)
                    if 2 <= t < NT + 2:
                        turn(t - 2)
                    if t >= 3:
                        ins = logits(t - 3)
                ins.then_inc(logits_ready, 1)
                pe.wait_ge(x_ready, NT)
                with pe.Fori(1, E // 2 + 1) as r:
                    for n in range(U):
                        j, t = divmod(n, NT)
                        if t == 0:
                            pe.wait_ge(split[j], r * 4 + 2)
                        if n == 4:
                            pe.wait_ge(norm_ready, 2)
                            pe.wait_ge(logits_read, 1)
                        pe.wait_ge(y_added, r * U + (n + 1 - NT))
                        i = 0
                        for d in range(DC):
                            for a, b in ((T["xnhi"], whi), (T["xnlo"], whi), (T["xnhi"], wlo)):
                                ins = pe.matmul(ps[:, (t + 4) % 8, 0:Q3], a[:, d, tile(t)], b[j][:, d], start=i == 0,
                                                stop=i == 3 * DC - 1)
                                i += 1
                        ins.then_inc(y_ready, 1)


def expert_attention(nc, T, io, out):
    SC = float(H) ** -0.5
    ASIDE = 4
    NA = E // ASIDE
    ROUNDS = NT + 3
    with ExitStack() as ctx:
        m = Mem(nc, ctx)
        ps, x, ident, w, y = T["ps"], T["x"], T["ident"], T["w"], T["y"]
        qkT = m.sb("qkT", [P, 2, B * S])
        p, pT = m.sb("y_probs", [P, 2, S]), m.sb("y_probsT", [P, 2, S])
        rmax, nb, rsum, rinv = (m.sb("y_" + n, [P, NT]) for n in ("max", "nb", "sum", "inv"))
        o = m.sb("y_out", [P, NT, H])
        ohi, olo = m.sb("y_outT_hi", [P, NT, P], F32R), m.sb("y_outT_lo", [P, NT, P], F32R)
        aside, aside_sum = m.sb("aside", [P, 2, NA, D]), m.sb("aside_sum", [P, 2, D])

        dve_step = m.sem("g_dve_step")
        qk_turned, qk_copied = m.sem("qk_turned"), m.sem("qk_copied")
        s_ready, r_ready, nb_ready, p_ready = m.sem("ys_ready"), m.sem("yr_ready"), m.sem("ynb_ready"), m.sem("yp_ready")
        pt_ready, pt_copied, pv_ready, o_ready = m.sem("ypt_ready"), m.sem("ypt_copied"), m.sem("ypv_ready"), m.sem("yo_ready")
        o_turned, o_hi, o_lo = m.sem("yo_turned"), m.sem("yo_hi"), m.sem("yo_lo")
        unit_ready, added, set_aside, aside_added = (m.sem(n) for n in ("unit_ready", "unit_added", "set_aside", "aside_added"))
        x_ready, stored = m.sem("x3_ready"), m.sem("stored")
        SCORE, TURN, PT, PV, UNIT = 0, 2, 3, 4, 5
        UNITS = [(2 * pair + i, e) for pair in range(NT // 2) for e in range(E) for i in range(2)]
        by_act = [e % ASIDE == 1 for t, e in UNITS]
        acts = [sum(by_act[:n + 1]) for n in range(len(UNITS))]
        dves = [n + 1 - a for n, a in enumerate(acts)]

        def schedule(round_, unit):
            parts = [(i, part) for i in range(ROUNDS) for part in range(4)]
            first, rest = parts[:5 * 4], parts[5 * 4:]
            for i, part in first:
                round_(i, part)
            for n in range(len(UNITS)):
                unit(n)
                if n % 4 == 2 and rest:
                    round_(*rest.pop(0))

        with nc.Block() as block:

            @block.sync
            def _(sp):
                rows = out.rearrange("b (t p) d -> (b t) p d", p=P)
                for t in range(NT):
                    sp.wait_ge(x_ready, t + 1)
                    sp.dma_start(rows[t], x[:, t]).then_inc(stored, 16)
                sp.wait_ge(stored, 16 * NT)

            @block.tensor
            def _(pe):
                def turn_qk(b):
                    for which in range(2):
                        if b == 1:
                            pe.wait_ge(qk_copied, which + 1)
                        for k in range(QT):
                            ins = pe.transpose(ps[:, UNIT + which, k * P:(k + 1) * P], y[:, b * QT + k, which * H:(which + 1) * H], ident[:])
                        ins.then_inc(qk_turned, 1)

                def round_(i, part):
                    if part == 0 and i < NT:
                        b = i // QT
                        if i in (0, 2):
                            turn_qk(i // 2)
                        if i % QT == 0:
                            pe.wait_ge(qk_copied, 2 * b + 2)
                        if i >= 2:
                            pe.wait_ge(p_ready, i - 1)
                        pe.matmul(ps[:, SCORE + i % 2], qkT[:, 0, i * P:(i + 1) * P], qkT[:, 1, b * S:(b + 1) * S],
                                  start=True, stop=True).then_inc(s_ready, 1)
                    if part == 1 and 1 <= i <= NT:
                        u = i - 1
                        pe.wait_ge(p_ready, u + 1)
                        if u >= 1:
                            pe.wait_ge(pt_copied, u)
                        for k in range(QT):
                            ins = pe.transpose(ps[:, PT, k * P:(k + 1) * P], p[:, u % 2, k * P:(k + 1) * P], ident[:])
                        ins.then_inc(pt_ready, 1)
                    if part == 2 and 2 <= i <= NT + 1:
                        u = i - 2
                        pe.wait_ge(pt_copied, u + 1)
                        if u >= 1:
                            pe.wait_ge(o_ready, u)
                        for k in range(QT):
                            ins = pe.matmul(ps[:, PV, 0:H], pT[:, u % 2, k * P:(k + 1) * P],
                                            y[:, (u // QT) * QT + k, 2 * H:3 * H], start=k == 0, stop=k == QT - 1)
                        ins.then_inc(pv_ready, 1)
                    if part == 3 and i >= 3:
                        u = i - 3
                        pe.wait_ge(o_ready, u + 1)
                        if u >= 1:
                            pe.wait_ge(o_lo, u)
                        pe.transpose(ps[:, TURN, 0:P], o[:, u], ident[:]).then_inc(o_turned, 1)

                def unit(n):
                    t, e = UNITS[n]
                    if e == 0:
                        pe.wait_ge(o_lo, t + 1)
                        pe.wait_ge(qk_copied, 2 * B)
                    if n >= 3:
                        if by_act[n - 3]:
                            pe.wait_ge(set_aside, acts[n - 3])
                        else:
                            pe.wait_ge(added, dves[n - 3])
                    for i, (a, b) in enumerate(((ohi, T["ohi"]), (olo, T["ohi"]), (ohi, T["olo"]))):
                        ins = pe.matmul(ps[:, UNIT + n % 3], a[:, t], b[:, e], start=i == 0, stop=i == 2)
                    ins.then_inc(unit_ready, 1)

                schedule(round_, unit)

            @block.scalar
            def _(act):
                def copy_qk(b):
                    for which in range(2):
                        act.wait_ge(qk_turned, 2 * b + which + 1)
                        act.copy(qkT[:, which, b * S:(b + 1) * S], ps[:, UNIT + which]).then_inc(qk_copied, 1)

                def round_(i, part):
                    if part == 0 and i < NT:
                        if i in (0, 2):
                            copy_qk(i // 2)
                        act.wait_ge(nb_ready, i + 1)
                        if i >= 2:
                            act.wait_ge(pt_ready, i - 1)
                        act.activation(p[:, i % 2], ps[:, SCORE + i % 2], ACT.Exp, bias=nb[:, i:i + 1], scale=SC,
                                       accum_out=rsum[:, i:i + 1]).then_inc(p_ready, 1)
                    if part == 1 and 1 <= i <= NT:
                        u = i - 1
                        act.wait_ge(pt_ready, u + 1)
                        if u >= 2:
                            act.wait_ge(pv_ready, u - 1)
                        act.copy(pT[:, u % 2], ps[:, PT]).then_inc(pt_copied, 1)
                    if part == 3 and i >= 3:
                        u = i - 3
                        act.wait_ge(o_turned, u + 1)
                        act.copy(ohi[:, u], ps[:, TURN, 0:P]).then_inc(o_hi, 1)

                def unit(n):
                    t, e = UNITS[n]
                    if by_act[n]:
                        act.wait_ge(unit_ready, n + 1)
                        if t >= 2 and e == 1:
                            act.wait_ge(aside_added, (t - 1) * (NA - 1))
                        act.activation(aside[:, t % 2, e // ASIDE], ps[:, UNIT + n % 3], ACT.Copy,
                                       scale=w[:, t, e:e + 1]).then_inc(set_aside, 1)

                schedule(round_, unit)

            @block.gpsimd
            def _(pool):
                def unit(n):
                    t, e = UNITS[n]
                    if by_act[n] and e >= ASIDE:
                        k, i = e // ASIDE, t % 2
                        pool.wait_ge(set_aside, acts[n])
                        if k == 1:
                            if t >= 2:
                                pool.wait_ge(x_ready, t - 1)
                            pool.tensor_tensor(aside_sum[:, i], aside[:, i, 0], aside[:, i, 1], ALU.add).then_inc(aside_added, 1)
                        else:
                            pool.wait_ge(aside_added, (t - i) * (NA - 1) + 2 * (k - 2) + i + 1)
                            pool.tensor_tensor(aside_sum[:, i], aside_sum[:, i], aside[:, i, k], ALU.add).then_inc(aside_added, 1)

                schedule(lambda i, part: None, unit)

            @block.vector
            def _(dve):
                last_add = {}

                def round_(i, part):
                    if part == 0 and i < NT:
                        dve.wait_ge(s_ready, i + 1)
                        dve.tensor_reduce(rmax[:, i:i + 1], ps[:, SCORE + i % 2], AX.X, ALU.max).then_inc(dve_step, 1)
                        dve.wait_ge(dve_step, i + 1)
                        dve.tensor_scalar(nb[:, i:i + 1], rmax[:, i:i + 1], -SC, None, ALU.mult).then_inc(nb_ready, 1)
                    if part == 2 and 2 <= i <= NT + 1:
                        u = i - 2
                        dve.wait_ge(p_ready, u + 1)
                        dve.reciprocal(rinv[:, u:u + 1], rsum[:, u:u + 1]).then_inc(r_ready, 1)
                        dve.wait_ge(r_ready, u + 1)
                        dve.wait_ge(pv_ready, u + 1)
                        dve.tensor_scalar(o[:, u], ps[:, PV, 0:H], rinv[:, u:u + 1], None, ALU.mult).then_inc(o_ready, 1)
                    if part == 3 and i >= 3:
                        u = i - 3
                        dve.wait_ge(o_hi, u + 1)
                        dve.tensor_tensor(olo[:, u], ps[:, TURN, 0:P], ohi[:, u].bitcast(F32), ALU.subtract).then_inc(o_lo, 1)

                def other_experts(t):
                    dve.wait_ge(added, last_add[t])
                    dve.wait_ge(aside_added, (t - t % 2) * (NA - 1) + 2 * (NA - 2) + t % 2 + 1)
                    dve.tensor_tensor(x[:, t], x[:, t], aside_sum[:, t % 2], ALU.add).then_inc(x_ready, 1)

                def unit(n):
                    t, e = UNITS[n]
                    if not by_act[n]:
                        dve.wait_ge(unit_ready, n + 1)
                        if e > 0:
                            dve.wait_ge(added, last_add[t])
                        dve.scalar_tensor_tensor(out=x[:, t], in0=ps[:, UNIT + n % 3], scalar=w[:, t, e:e + 1], in1=x[:, t],
                                                 op0=ALU.mult, op1=ALU.add).then_inc(added, 1)
                        last_add[t] = dves[n]
                    if e == 3 and t % 2 and t >= 3:
                        other_experts(t - 3)
                        other_experts(t - 2)

                schedule(round_, unit)
                other_experts(NT - 2)
                other_experts(NT - 1)




def program(nc, io, out):
    with ExitStack() as ctx:
        m = Mem(nc, ctx)
        T = {"ps": ctx.enter_context(nc.psum_tensor("ps", [P, 8, 512], F32))}
        T["x"] = m.sb("x", [P, NT, D])
        T["ident"] = m.sb("ident", [P, P])
        T["ones"] = m.sb("ones", [P, P])
        T["waited"] = m.sem("waited")
        T["weights_in"], T["weights_total"] = m.sem("weights_in"), 5 * 16

        T["acc"] = m.sb("acc", [P, NT, D])
        T["Wvhi"], T["Wvlo"] = m.sb("Wv_hi", [P, DC, D], F32R), m.sb("Wv_lo", [P, DC, D], F32R)
        T["Wohi"], T["Wolo"] = T["Wvhi"], T["Wvlo"]
        T["sums"], T["place"] = m.sb("head_sums", [P, P]), m.sb("place", [P, NT, P], F32R)

        with ExitStack() as early:
            m = Mem(nc, early)
            T["closed"], T["ident_r"] = m.sb("closed", [P, 2, P], F32R), m.sb("ident_r", [P, P], F32R)
            T["m_run"], T["l_run"] = m.sb("m_run", [P, NT]), m.sb("l_run", [P, NT])
            latent_weights = m.sb("latent_weights", [P, 5, D])
            T["dqkv"] = latent_weights[:, 0:2].rearrange("p i (c e) -> p i c e", e=DCQ)
            T["uq"], T["uk"], T["uv"] = (latent_weights[:, 2 + i] for i in range(3))
            with ExitStack() as front:
                m = Mem(nc, front)
                T["ghi"], T["glo"] = m.sb("g_hi", [P, DC, B * S], F32R), m.sb("g_lo", [P, DC, B * S], F32R)
                T["c"] = m.sb("c", [P, NT])
                T["live"] = m.sb("live", [P, NB + 2], I32)
                queries(nc, T, io)
                cross_attention(nc, T, io)
            m = Mem(nc, early)
            T["v"], T["o"] = m.sb("v", [P, NT, D]), m.sb("o", [P, NT, D])
            T["qkT"] = [[m.sb(f"{n}T_{h}", [P, DC, B * S], F32R) for h in ("hi", "lo")] for n in ("q", "k")]
            latents(nc, T, io)
            T["Wo"] = latent_weights[:, 0:DC]
            heads(nc, T, io)
        with ExitStack() as late:
            m = Mem(nc, late)
            T["xnhi"], T["xnlo"] = m.sb("xn3T_hi", [P, DC, B * S], F32R), m.sb("xn3T_lo", [P, DC, B * S], F32R)
            T["ohi"], T["olo"] = m.sb("O_hi", [P, E, D], F32R), m.sb("O_lo", [P, E, D], F32R)
            T["w"], T["y"] = m.sb("w", [P, NT, E]), T["acc"][:, :, 0:3 * H]
            experts(nc, T, io)
            expert_attention(nc, T, io, out)


_INS = {"x": "x", "ctx": "ctx_1024", "mask": "mask_SxS2_bk0", "Wq": "L0_xattn_Wq", "bq": "L0_xattn_bq",
        "Wk": "L0_xattn_Wk", "bk": "L0_xattn_bk", "Wv": "L0_xattn_Wv", "bv": "L0_xattn_bv", "dq": "L0_attn_W_dq",
        "uq": "L0_attn_W_uq", "dkv": "L0_attn_W_dkv", "uk": "L0_attn_W_uk", "uv": "L0_attn_W_uv", "Wo": "L0_attn_W_o",
        "sim": "L0_ffn_sim_matrix", "gates": "L0_ffn_gates", "qp": "L0_ffn_q_proj", "kp": "L0_ffn_k_proj",
        "vp": "L0_ffn_v_proj", "op": "L0_ffn_o_proj"}


def kernel(**inputs):
    import numpy as _np
    import concourse.bacc as _bacc
    from concourse import mybir as _mybir
    from concourse.bass_utils import run_bass_kernel_spmd as _run

    nc = _bacc.Bacc("TRN2", target_bir_lowering=False, num_devices=1)
    arrays, io = {}, {}
    for name, key in _INS.items():
        a = _np.ascontiguousarray(inputs[key])
        arrays[f"in_{name}_dram"] = a
        dt = U8 if a.dtype == _np.bool_ else _mybir.dt.from_np(a.dtype)
        io[name] = nc.dram_tensor(f"in_{name}_dram", a.shape, dt, kind="ExternalInput").ap()
    out = nc.dram_tensor("out_dram", (B, S, D), _mybir.dt.from_np(_np.dtype("float32")), kind="ExternalOutput").ap()
    program(nc, io, out)
    r = _run(nc, [arrays], core_ids=[0])
    return r.results[0]["out_dram"]
```
